# Optimizing a Trainium2 kernel written in Bass

```python
import numpy as np
import jax
import jax.numpy as jnp

def _softmax(x, axis=-1):
    return jax.nn.softmax(x, axis=axis)

def _gelu(x):
    return jax.nn.gelu(x, approximate=True)

def _silu(x):
    return jax.nn.silu(x)

def _sigmoid(x):
    return jax.nn.sigmoid(x)

def _layernorm(x, axis=-1, eps=1e-05):
    m = jnp.mean(x, axis=axis, keepdims=True)
    v = jnp.var(x, axis=axis, keepdims=True)
    return (x - m) / jnp.sqrt(v + eps)

def _scatter_add(tgt, idx, src, axis=0):
    return tgt.at[idx].add(src)

def _segment_sum(src, seg, n):
    return jax.ops.segment_sum(src, seg, n)
kernel_name = 'mk_decoder_preln_d2_seqx_r8_88aa73'

def setup_inputs(seed: int=0):
    np.random.seed(seed)
    _w = jnp.asarray

    def _rec_inputs():
        import jax
        import jax.numpy as jnp
        _rk = jax.random.key(seed)
        x = 0.002226 + 0.9996 * jax.random.normal(jax.random.fold_in(_rk, 1), (8, 128, 128), jnp.float32)
        _lenS = 128 - jax.random.randint(jax.random.fold_in(_rk, 7), (8,), 0, max(1, 128 // 4) + 1, jnp.int32)
        _lenS2 = 120 - jax.random.randint(jax.random.fold_in(_rk, 8), (8,), 0, max(1, 120 // 4) + 1, jnp.int32)
        _ctx_1024P = jax.random.normal(jax.random.fold_in(_rk, 11), (8, 16, 128), jnp.float32)
        _ctx_1024c = jax.random.dirichlet(jax.random.fold_in(_rk, 511), 0.3 * jnp.ones((16,), jnp.float32), (8, 120))
        _ctx_1024t = jnp.einsum('bsk,bkd->bsd', _ctx_1024c, _ctx_1024P)
        _ctx_1024t = _ctx_1024t * jax.lax.rsqrt(jnp.mean(jnp.square(_ctx_1024t)) + 1e-12) * 0.953939
        ctx_1024 = -0.000125008 + 0.999885 * (_ctx_1024t + 0.3 * jax.random.normal(jax.random.fold_in(_rk, 611), (8, 120, 128), jnp.float32))
        _validS = jnp.arange(128)[None, :] < _lenS[:, None]
        _validS2 = jnp.arange(120)[None, :] < _lenS2[:, None]
        _causal = jnp.tril(jnp.ones((128, 128), dtype=bool))
        mask_BxS2_bf1 = jnp.ones((8, 120), dtype=bool)
        return (x, ctx_1024, mask_BxS2_bf1)
    x, ctx_1024, mask_BxS2_bf1 = _rec_inputs()

    def _L0_attn_setup():
        import jax, jax.numpy as jnp
        import numpy as np
        DIM = 128
        NUM_HEADS = 16
        HEAD_DIM = DIM // NUM_HEADS
        BATCH, TIME = (4, 512)
        key = jax.random.key(seed)
        ks = jax.random.split(key, 9)
        s = 1.0 / np.sqrt(DIM)
        x = jax.random.normal(ks[0], (BATCH, TIME, DIM), dtype=jnp.float32)
        Wq = jax.random.uniform(ks[1], (DIM, DIM), jnp.float32, -s, s)
        bq = jax.random.uniform(ks[2], (DIM,), jnp.float32, -s, s)
        Wk = jax.random.uniform(ks[3], (DIM, DIM), jnp.float32, -s, s)
        bk = jax.random.uniform(ks[4], (DIM,), jnp.float32, -s, s)
        Wv = jax.random.uniform(ks[5], (DIM, DIM), jnp.float32, -s, s)
        bv = jax.random.uniform(ks[6], (DIM,), jnp.float32, -s, s)
        Wo = jax.random.uniform(ks[7], (DIM, DIM), jnp.float32, -s, s)
        bo = jax.random.uniform(ks[8], (DIM,), jnp.float32, -s, s)
        return {'x': x, 'Wq': Wq, 'bq': bq, 'Wk': Wk, 'bk': bk, 'Wv': Wv, 'bv': bv, 'Wo': Wo, 'bo': bo}
    _L0_attn_all = _L0_attn_setup()
    _L0_attn_in = {k: v for k, v in _L0_attn_all.items() if k in ('Wq', 'bq', 'Wk', 'bk', 'Wv', 'bv', 'Wo', 'bo')}
    del _L0_attn_all

    def _L0_xattn_setup():
        import jax, jax.numpy as jnp
        import numpy as np
        DIM = 128
        HEADS = 16
        DIM_HEAD = 64
        INNER = HEADS * DIM_HEAD
        EPS = 1e-05

        def layer_norm(x, gamma, beta):
            mu = jnp.mean(x, axis=-1, keepdims=True)
            var = jnp.var(x, axis=-1, keepdims=True)
            return (x - mu) * jax.lax.rsqrt(var + EPS) * gamma + beta
        key = jax.random.key(seed)
        ks = jax.random.split(key, 8)
        b, n, m = (8, 512, 64)
        x = jax.random.normal(ks[0], (b, n, DIM), dtype=jnp.float32)
        latents = jax.random.normal(ks[1], (b, m, DIM), dtype=jnp.float32)
        mask = jnp.ones((b, n), dtype=bool)
        s = 0.02
        Wq = jax.random.normal(ks[2], (DIM, INNER), dtype=jnp.float32) * s
        Wkv = jax.random.normal(ks[3], (DIM, 2 * INNER), dtype=jnp.float32) * s
        Wout = jax.random.normal(ks[4], (INNER, DIM), dtype=jnp.float32) * s
        g_x = jnp.ones((DIM,), jnp.float32)
        b_x = jnp.zeros((DIM,), jnp.float32)
        g_l = jnp.ones((DIM,), jnp.float32)
        b_l = jnp.zeros((DIM,), jnp.float32)
        g_o = jnp.ones((DIM,), jnp.float32)
        b_o = jnp.zeros((DIM,), jnp.float32)
        return {'x': x, 'latents': latents, 'mask': mask, 'g_x': g_x, 'b_x': b_x, 'g_l': g_l, 'b_l': b_l, 'Wq': Wq, 'Wkv': Wkv, 'Wout': Wout, 'g_o': g_o, 'b_o': b_o}
    _L0_xattn_all = _L0_xattn_setup()
    _L0_xattn_in = {k: v for k, v in _L0_xattn_all.items() if k in ('g_x', 'b_x', 'g_l', 'b_l', 'Wq', 'Wkv', 'Wout', 'g_o', 'b_o')}
    del _L0_xattn_all

    def _L0_ffn_setup():
        import jax, jax.numpy as jnp
        import numpy as np
        H, I, E, K = (128, 64, 32, 8)
        B, S = (4, 128)

        def silu(x):
            return x * jax.nn.sigmoid(x)
        key = jax.random.key(seed)
        ks = jax.random.split(key, 14)

        def w(k, shape, fan_in):
            return jax.random.normal(k, shape, jnp.float32) / np.float32(np.sqrt(fan_in))
        return {'hidden_states': jax.random.normal(ks[0], (B, S, H), jnp.float32), 'Wr': w(ks[1], (H, E), H), 'br': jnp.zeros((E,), jnp.float32), 'Wg_s': w(ks[2], (H, I), H), 'bg_s': jnp.zeros((I,), jnp.float32), 'Wu_s': w(ks[3], (H, I), H), 'bu_s': jnp.zeros((I,), jnp.float32), 'Wd_s': w(ks[4], (I, H), I), 'bd_s': jnp.zeros((H,), jnp.float32), 'Wg': w(ks[5], (E, H, I), H), 'bg': jnp.zeros((E, I), jnp.float32), 'Wu': w(ks[6], (E, H, I), H), 'bu': jnp.zeros((E, I), jnp.float32), 'Wd': w(ks[7], (E, I, H), I), 'bd': jnp.zeros((E, H), jnp.float32)}
    _L0_ffn_all = _L0_ffn_setup()
    _L0_ffn_in = {k: v for k, v in _L0_ffn_all.items() if k in ('Wr', 'br', 'Wg_s', 'bg_s', 'Wu_s', 'bu_s', 'Wd_s', 'bd_s', 'Wg', 'bg', 'Wu', 'bu', 'Wd', 'bd')}
    del _L0_ffn_all

    def _L1_attn_setup():
        import jax, jax.numpy as jnp
        import numpy as np
        H = 8
        ROPE_DIM = 64
        GAMMA = 0.96875
        GROUPS = 16
        EPS = 1e-05

        def _rope(x, offset=0):
            T = x.shape[-2]
            inv_freq = 1.0 / 10000.0 ** (np.arange(0, ROPE_DIM, 2, dtype=np.float32) / ROPE_DIM)
            t = jnp.arange(T, dtype=jnp.float32) + offset
            freqs = t[:, None] * inv_freq[None, :]
            freqs = jnp.repeat(freqs, 2, axis=-1)
            cos, sin = (jnp.cos(freqs), jnp.sin(freqs))
            xr, xp = (x[..., :ROPE_DIM], x[..., ROPE_DIM:])
            x1, x2 = (xr[..., 0::2], xr[..., 1::2])
            rot = jnp.stack([-x2, x1], axis=-1).reshape(xr.shape)
            return jnp.concatenate([xr * cos + rot * sin, xp], axis=-1)

        def _to_scores(X, W):
            B, T, C = X.shape
            return (X @ W).reshape(B, T, H, C).transpose(0, 2, 1, 3)
        key = jax.random.key(seed)
        ks = jax.random.split(key, 4)
        B, T, C = (1, 256, 128)
        return {'X_Q': jax.random.normal(ks[0], (B, T, C), jnp.float32), 'W_Q': jax.random.normal(ks[1], (C, C * H), jnp.float32) / C, 'W_K': jax.random.normal(ks[2], (C, C * H), jnp.float32) / C, 'W_V': jax.random.normal(ks[3], (C, C * H), jnp.float32) / C, 'gn_weight': jnp.ones((C,), jnp.float32), 'gn_bias': jnp.zeros((C,), jnp.float32)}
    _L1_attn_all = _L1_attn_setup()
    _L1_attn_in = {k: v for k, v in _L1_attn_all.items() if k in ('W_Q', 'W_K', 'W_V', 'gn_weight', 'gn_bias')}
    del _L1_attn_all

    def _L1_xattn_setup():
        import jax, jax.numpy as jnp
        import numpy as np
        DIM = 128
        HEAD_DIM = 64
        NUM_HEADS = 8
        INNER = HEAD_DIM * NUM_HEADS
        ROT_DIM = HEAD_DIM
        ROPE_BASE = 10000.0
        EPS = 1e-05

        def layer_norm(x, g, b):
            mu = jnp.mean(x, axis=-1, keepdims=True)
            var = jnp.var(x, axis=-1, keepdims=True)
            return (x - mu) * jax.lax.rsqrt(var + EPS) * g + b

        def rope_rotate_k(k):
            n = k.shape[1]
            half = ROT_DIM // 2
            inv_freq = 1.0 / ROPE_BASE ** (jnp.arange(0, ROT_DIM, 2, dtype=jnp.float32) / ROT_DIM)
            theta = jnp.arange(n, dtype=jnp.float32)[:, None] * inv_freq[None, :]
            angles = jnp.concatenate([theta, theta], axis=-1)
            cos = jnp.cos(angles)[None, :, None, :].astype(k.dtype)
            sin = jnp.sin(angles)[None, :, None, :].astype(k.dtype)
            k_rope, k_pass = (k[..., :ROT_DIM], k[..., ROT_DIM:])
            neg_half = jnp.concatenate([-k_rope[..., half:], k_rope[..., :half]], axis=-1)
            k_rope = k_rope * cos + neg_half * sin
            return jnp.concatenate([k_rope, k_pass], axis=-1)
        key = jax.random.key(seed)
        ks = jax.random.split(key, 5)
        b, n, m = (8, 1024, 64)
        s = 1.0 / np.sqrt(DIM)
        return {'x': jax.random.normal(ks[0], (b, n, DIM), jnp.float32), 'latents': jax.random.normal(ks[1], (b, m, DIM), jnp.float32), 'gamma_x': jnp.ones((DIM,), jnp.float32), 'beta_x': jnp.zeros((DIM,), jnp.float32), 'gamma_l': jnp.ones((DIM,), jnp.float32), 'beta_l': jnp.zeros((DIM,), jnp.float32), 'Wq': jax.random.normal(ks[2], (DIM, INNER), jnp.float32) * s, 'Wkv': jax.random.normal(ks[3], (DIM, 2 * INNER), jnp.float32) * s, 'Wo': jax.random.normal(ks[4], (INNER, DIM), jnp.float32) * (1.0 / np.sqrt(INNER))}
    _L1_xattn_all = _L1_xattn_setup()
    _L1_xattn_in = {k: v for k, v in _L1_xattn_all.items() if k in ('gamma_x', 'beta_x', 'gamma_l', 'beta_l', 'Wq', 'Wkv', 'Wo')}
    del _L1_xattn_all

    def _L1_ffn_setup():
        import jax, jax.numpy as jnp
        import numpy as np
        EPS = 1e-08

        def _ternary_linear(x, w):
            alpha = jnp.mean(jnp.abs(w))
            w_t = jnp.sign(w) * (jnp.abs(w) > 0.5 * alpha).astype(w.dtype)
            w_q = w + jax.lax.stop_gradient(w_t - w)
            d = x.shape[-1]
            rms = jnp.sqrt(jnp.sum(x * x, axis=-1, keepdims=True)) / jnp.sqrt(jnp.asarray(d, x.dtype))
            x_norm = x / (rms + EPS)
            return jnp.einsum('bsd,fd->bsf', x_norm, w_q)
        key = jax.random.key(seed)
        k1, k2, k3 = jax.random.split(key, 3)
        d_model, d_ff = (128, 512)
        B, S = (4, 512)
        x = jax.random.normal(k1, (B, S, d_model), dtype=jnp.float32)
        w_up = jax.random.normal(k2, (d_ff, d_model), dtype=jnp.float32) * 0.02
        w_down = jax.random.normal(k3, (d_model, d_ff), dtype=jnp.float32) * 0.02
        return {'x': x, 'w_up': w_up, 'w_down': w_down}
    _L1_ffn_all = _L1_ffn_setup()
    _L1_ffn_in = {k: v for k, v in _L1_ffn_all.items() if k in ('w_up', 'w_down')}
    del _L1_ffn_all
    return {'x': x, 'ctx_1024': ctx_1024, 'mask_BxS2_bf1': mask_BxS2_bf1, 'L0_attn_Wq': _L0_attn_in['Wq'], 'L0_attn_bq': _L0_attn_in['bq'], 'L0_attn_Wk': _L0_attn_in['Wk'], 'L0_attn_bk': _L0_attn_in['bk'], 'L0_attn_Wv': _L0_attn_in['Wv'], 'L0_attn_bv': _L0_attn_in['bv'], 'L0_attn_Wo': _L0_attn_in['Wo'], 'L0_attn_bo': _L0_attn_in['bo'], 'L0_xattn_g_x': _L0_xattn_in['g_x'], 'L0_xattn_b_x': _L0_xattn_in['b_x'], 'L0_xattn_g_l': _L0_xattn_in['g_l'], 'L0_xattn_b_l': _L0_xattn_in['b_l'], 'L0_xattn_Wq': _L0_xattn_in['Wq'], 'L0_xattn_Wkv': _L0_xattn_in['Wkv'], 'L0_xattn_Wout': _L0_xattn_in['Wout'], 'L0_xattn_g_o': _L0_xattn_in['g_o'], 'L0_xattn_b_o': _L0_xattn_in['b_o'], 'L0_ffn_Wr': _L0_ffn_in['Wr'], 'L0_ffn_br': _L0_ffn_in['br'], 'L0_ffn_Wg_s': _L0_ffn_in['Wg_s'], 'L0_ffn_bg_s': _L0_ffn_in['bg_s'], 'L0_ffn_Wu_s': _L0_ffn_in['Wu_s'], 'L0_ffn_bu_s': _L0_ffn_in['bu_s'], 'L0_ffn_Wd_s': _L0_ffn_in['Wd_s'], 'L0_ffn_bd_s': _L0_ffn_in['bd_s'], 'L0_ffn_Wg': _L0_ffn_in['Wg'], 'L0_ffn_bg': _L0_ffn_in['bg'], 'L0_ffn_Wu': _L0_ffn_in['Wu'], 'L0_ffn_bu': _L0_ffn_in['bu'], 'L0_ffn_Wd': _L0_ffn_in['Wd'], 'L0_ffn_bd': _L0_ffn_in['bd'], 'L1_attn_W_Q': _L1_attn_in['W_Q'], 'L1_attn_W_K': _L1_attn_in['W_K'], 'L1_attn_W_V': _L1_attn_in['W_V'], 'L1_attn_gn_weight': _L1_attn_in['gn_weight'], 'L1_attn_gn_bias': _L1_attn_in['gn_bias'], 'L1_xattn_gamma_x': _L1_xattn_in['gamma_x'], 'L1_xattn_beta_x': _L1_xattn_in['beta_x'], 'L1_xattn_gamma_l': _L1_xattn_in['gamma_l'], 'L1_xattn_beta_l': _L1_xattn_in['beta_l'], 'L1_xattn_Wq': _L1_xattn_in['Wq'], 'L1_xattn_Wkv': _L1_xattn_in['Wkv'], 'L1_xattn_Wo': _L1_xattn_in['Wo'], 'L1_ffn_w_up': _L1_ffn_in['w_up'], 'L1_ffn_w_down': _L1_ffn_in['w_down']}

def reference(x, ctx_1024, mask_BxS2_bf1, L0_attn_Wq, L0_attn_bq, L0_attn_Wk, L0_attn_bk, L0_attn_Wv, L0_attn_bv, L0_attn_Wo, L0_attn_bo, L0_xattn_g_x, L0_xattn_b_x, L0_xattn_g_l, L0_xattn_b_l, L0_xattn_Wq, L0_xattn_Wkv, L0_xattn_Wout, L0_xattn_g_o, L0_xattn_b_o, L0_ffn_Wr, L0_ffn_br, L0_ffn_Wg_s, L0_ffn_bg_s, L0_ffn_Wu_s, L0_ffn_bu_s, L0_ffn_Wd_s, L0_ffn_bd_s, L0_ffn_Wg, L0_ffn_bg, L0_ffn_Wu, L0_ffn_bu, L0_ffn_Wd, L0_ffn_bd, L1_attn_W_Q, L1_attn_W_K, L1_attn_W_V, L1_attn_gn_weight, L1_attn_gn_bias, L1_xattn_gamma_x, L1_xattn_beta_x, L1_xattn_gamma_l, L1_xattn_beta_l, L1_xattn_Wq, L1_xattn_Wkv, L1_xattn_Wo, L1_ffn_w_up, L1_ffn_w_down):
    import jax
    import jax.numpy as jnp

    def _L0_attn_ref(x, Wq, bq, Wk, bk, Wv, bv, Wo, bo):
        import jax, jax.numpy as jnp
        import numpy as np
        DIM = 128
        NUM_HEADS = 16
        HEAD_DIM = DIM // NUM_HEADS
        BATCH, TIME = (4, 512)
        b, t, _ = x.shape
        kernel = lambda z: jax.nn.elu(z) + 1.0
        Q = kernel((x @ Wq.T + bq).reshape(b, t, NUM_HEADS, HEAD_DIM))
        K = kernel((x @ Wk.T + bk).reshape(b, t, NUM_HEADS, HEAD_DIM))
        V = (x @ Wv.T + bv).reshape(b, t, NUM_HEADS, HEAD_DIM)
        KV = jnp.einsum('bthd,bthe->bhde', K, V)
        Ksum = K.sum(axis=1)
        Z = 1.0 / (jnp.einsum('bthd,bhd->bth', Q, Ksum) + 1e-06)
        out = jnp.einsum('bthd,bhde->bthe', Q, KV) * Z[..., None]
        out = out.reshape(b, t, DIM)
        return out @ Wo.T + bo

    def _L0_xattn_ref(x, latents, mask, g_x, b_x, g_l, b_l, Wq, Wkv, Wout, g_o, b_o):
        import jax, jax.numpy as jnp
        import numpy as np
        DIM = 128
        HEADS = 16
        DIM_HEAD = 64
        INNER = HEADS * DIM_HEAD
        EPS = 1e-05

        def layer_norm(x, gamma, beta):
            mu = jnp.mean(x, axis=-1, keepdims=True)
            var = jnp.var(x, axis=-1, keepdims=True)
            return (x - mu) * jax.lax.rsqrt(var + EPS) * gamma + beta
        scale = DIM_HEAD ** (-0.5)
        xn = layer_norm(x, g_x, b_x)
        ln = layer_norm(latents, g_l, b_l)
        b, m = (ln.shape[0], ln.shape[1])
        q = jnp.einsum('bnd,de->bne', ln, Wq)
        kv_in = jnp.concatenate([xn, ln], axis=1)
        kv = jnp.einsum('bnd,de->bne', kv_in, Wkv)
        k, v = jnp.split(kv, 2, axis=-1)

        def split_heads(t):
            return t.reshape(t.shape[0], t.shape[1], HEADS, DIM_HEAD).transpose(0, 2, 1, 3)
        q, k, v = (split_heads(q), split_heads(k), split_heads(v))
        q = q * scale
        sim = jnp.einsum('bhid,bhjd->bhij', q, k)
        full_mask = jnp.concatenate([mask, jnp.ones((b, m), dtype=bool)], axis=1)
        max_neg = -jnp.finfo(sim.dtype).max
        sim = jnp.where(full_mask[:, None, None, :], sim, max_neg)
        attn = jax.nn.softmax(sim, axis=-1)
        out = jnp.einsum('bhij,bhjd->bhid', attn, v)
        out = out.transpose(0, 2, 1, 3).reshape(b, m, INNER)
        out = jnp.einsum('bne,ed->bnd', out, Wout)
        return layer_norm(out, g_o, b_o)

    def _L0_ffn_ref(hidden_states, Wr, br, Wg_s, bg_s, Wu_s, bu_s, Wd_s, bd_s, Wg, bg, Wu, bu, Wd, bd):
        import jax, jax.numpy as jnp
        import numpy as np
        H, I, E, K = (128, 64, 32, 8)
        B, S = (4, 128)

        def silu(x):
            return x * jax.nn.sigmoid(x)
        b, s, h = hidden_states.shape
        T = b * s
        x = hidden_states.reshape(T, h)
        logits = jnp.dot(x.astype(jnp.float32), Wr) + br
        aff = jax.nn.sigmoid(logits)
        top_v, top_i = jax.lax.top_k(aff, K)
        top_w = top_v / (jnp.sum(top_v, axis=-1, keepdims=True) + 1e-09)
        top_w = top_w.astype(hidden_states.dtype)
        e_total = Wr.shape[1]
        w_full = jnp.zeros((T, e_total), hidden_states.dtype)
        w_full = w_full.at[jnp.arange(T)[:, None], top_i].set(top_w)
        shared = jnp.dot(silu(jnp.dot(x, Wg_s) + bg_s) * (jnp.dot(x, Wu_s) + bu_s), Wd_s) + bd_s
        gate = silu(jnp.einsum('th,ehi->eti', x, Wg) + bg[:, None, :])
        up = jnp.einsum('th,ehi->eti', x, Wu) + bu[:, None, :]
        down = jnp.einsum('eti,eih->eth', gate * up, Wd) + bd[:, None, :]
        routed = jnp.einsum('te,eth->th', w_full, down)
        return (shared + routed).reshape(b, s, h)

    def _L1_attn_ref(X_Q, W_Q, W_K, W_V, gn_weight, gn_bias):
        import jax, jax.numpy as jnp
        import numpy as np
        H = 8
        ROPE_DIM = 64
        GAMMA = 0.96875
        GROUPS = 16
        EPS = 1e-05

        def _rope(x, offset=0):
            T = x.shape[-2]
            inv_freq = 1.0 / 10000.0 ** (np.arange(0, ROPE_DIM, 2, dtype=np.float32) / ROPE_DIM)
            t = jnp.arange(T, dtype=jnp.float32) + offset
            freqs = t[:, None] * inv_freq[None, :]
            freqs = jnp.repeat(freqs, 2, axis=-1)
            cos, sin = (jnp.cos(freqs), jnp.sin(freqs))
            xr, xp = (x[..., :ROPE_DIM], x[..., ROPE_DIM:])
            x1, x2 = (xr[..., 0::2], xr[..., 1::2])
            rot = jnp.stack([-x2, x1], axis=-1).reshape(xr.shape)
            return jnp.concatenate([xr * cos + rot * sin, xp], axis=-1)

        def _to_scores(X, W):
            B, T, C = X.shape
            return (X @ W).reshape(B, T, H, C).transpose(0, 2, 1, 3)
        B, T, C = X_Q.shape
        Q = _rope(_to_scores(X_Q, W_Q))
        K = _rope(_to_scores(X_Q, W_K))
        V = _to_scores(X_Q, W_V)
        Q, K, V = (jax.nn.silu(Q), jax.nn.silu(K), jax.nn.silu(V))
        n = jnp.arange(T)
        diff = n[:, None] - n[None, :]
        D = jnp.where(diff >= 0, GAMMA ** jnp.maximum(diff, 0).astype(jnp.float32), 0.0)
        A = jnp.einsum('bhqc,bhkc->bhqk', Q, K)
        A = A * D
        A = jnp.swapaxes(A, -2, -1)
        out = A @ V
        out = out.sum(axis=1)
        x = out.reshape(B * T, GROUPS, C // GROUPS)
        mu = x.mean(-1, keepdims=True)
        var = x.var(-1, keepdims=True)
        xn = (x - mu) * jax.lax.rsqrt(var + EPS)
        out = xn.reshape(B * T, C) * gn_weight + gn_bias
        return out.reshape(B, T, C)

    def _L1_xattn_ref(x, latents, gamma_x, beta_x, gamma_l, beta_l, Wq, Wkv, Wo):
        import jax, jax.numpy as jnp
        import numpy as np
        DIM = 128
        HEAD_DIM = 64
        NUM_HEADS = 8
        INNER = HEAD_DIM * NUM_HEADS
        ROT_DIM = HEAD_DIM
        ROPE_BASE = 10000.0
        EPS = 1e-05

        def layer_norm(x, g, b):
            mu = jnp.mean(x, axis=-1, keepdims=True)
            var = jnp.var(x, axis=-1, keepdims=True)
            return (x - mu) * jax.lax.rsqrt(var + EPS) * g + b

        def rope_rotate_k(k):
            n = k.shape[1]
            half = ROT_DIM // 2
            inv_freq = 1.0 / ROPE_BASE ** (jnp.arange(0, ROT_DIM, 2, dtype=jnp.float32) / ROT_DIM)
            theta = jnp.arange(n, dtype=jnp.float32)[:, None] * inv_freq[None, :]
            angles = jnp.concatenate([theta, theta], axis=-1)
            cos = jnp.cos(angles)[None, :, None, :].astype(k.dtype)
            sin = jnp.sin(angles)[None, :, None, :].astype(k.dtype)
            k_rope, k_pass = (k[..., :ROT_DIM], k[..., ROT_DIM:])
            neg_half = jnp.concatenate([-k_rope[..., half:], k_rope[..., :half]], axis=-1)
            k_rope = k_rope * cos + neg_half * sin
            return jnp.concatenate([k_rope, k_pass], axis=-1)
        b, n, _ = x.shape
        m = latents.shape[1]
        h, d = (NUM_HEADS, HEAD_DIM)
        scale = d ** (-0.5)
        xn = layer_norm(x, gamma_x, beta_x)
        ln = layer_norm(latents, gamma_l, beta_l)
        q = (ln @ Wq).reshape(b, m, h, d)
        kv_x = xn @ Wkv
        k_x, v_x = (kv_x[..., :INNER], kv_x[..., INNER:])
        kv_l = ln @ Wkv
        k_l, v_l = (kv_l[..., :INNER], kv_l[..., INNER:])
        k_x = k_x.reshape(b, n, h, d)
        v_x = v_x.reshape(b, n, h, d)
        k_x = rope_rotate_k(k_x)
        q = jnp.transpose(q, (0, 2, 1, 3)) * scale
        k_x = jnp.transpose(k_x, (0, 2, 1, 3))
        v_x = jnp.transpose(v_x, (0, 2, 1, 3))
        k_l = jnp.transpose(k_l.reshape(b, m, h, d), (0, 2, 1, 3))
        v_l = jnp.transpose(v_l.reshape(b, m, h, d), (0, 2, 1, 3))
        k = jnp.concatenate([k_x, k_l], axis=2)
        v = jnp.concatenate([v_x, v_l], axis=2)
        sim = jnp.einsum('bhid,bhjd->bhij', q, k)
        attn = jax.nn.softmax(sim, axis=-1)
        out = jnp.einsum('bhij,bhjd->bhid', attn, v)
        out = jnp.transpose(out, (0, 2, 1, 3)).reshape(b, m, INNER)
        return out @ Wo

    def _L1_ffn_ref(x, w_up, w_down):
        import jax, jax.numpy as jnp
        import numpy as np
        EPS = 1e-08

        def _ternary_linear(x, w):
            alpha = jnp.mean(jnp.abs(w))
            w_t = jnp.sign(w) * (jnp.abs(w) > 0.5 * alpha).astype(w.dtype)
            w_q = w + jax.lax.stop_gradient(w_t - w)
            d = x.shape[-1]
            rms = jnp.sqrt(jnp.sum(x * x, axis=-1, keepdims=True)) / jnp.sqrt(jnp.asarray(d, x.dtype))
            x_norm = x / (rms + EPS)
            return jnp.einsum('bsd,fd->bsf', x_norm, w_q)
        h = jax.nn.gelu(_ternary_linear(x, w_up), approximate=False)
        return _ternary_linear(h, w_down)
    x = x + _L0_attn_ref(_layernorm(x, axis=-1), L0_attn_Wq, L0_attn_bq, L0_attn_Wk, L0_attn_bk, L0_attn_Wv, L0_attn_bv, L0_attn_Wo, L0_attn_bo)
    x = x + _L0_xattn_ref(ctx_1024, _layernorm(x, axis=-1), mask_BxS2_bf1, L0_xattn_g_x, L0_xattn_b_x, L0_xattn_g_l, L0_xattn_b_l, L0_xattn_Wq, L0_xattn_Wkv, L0_xattn_Wout, L0_xattn_g_o, L0_xattn_b_o)
    x = x + _L0_ffn_ref(_layernorm(x, axis=-1), L0_ffn_Wr, L0_ffn_br, L0_ffn_Wg_s, L0_ffn_bg_s, L0_ffn_Wu_s, L0_ffn_bu_s, L0_ffn_Wd_s, L0_ffn_bd_s, L0_ffn_Wg, L0_ffn_bg, L0_ffn_Wu, L0_ffn_bu, L0_ffn_Wd, L0_ffn_bd)
    x = x + _L1_attn_ref(_layernorm(x, axis=-1), L1_attn_W_Q, L1_attn_W_K, L1_attn_W_V, L1_attn_gn_weight, L1_attn_gn_bias)
    x = x + _L1_xattn_ref(ctx_1024, _layernorm(x, axis=-1), L1_xattn_gamma_x, L1_xattn_beta_x, L1_xattn_gamma_l, L1_xattn_beta_l, L1_xattn_Wq, L1_xattn_Wkv, L1_xattn_Wo)
    x = x + _L1_ffn_ref(_layernorm(x, axis=-1), L1_ffn_w_up, L1_ffn_w_down)
    return x

_drawn_inputs = setup_inputs


def setup_inputs(seed=0):
    import zlib

    import numpy as np

    out = dict(_drawn_inputs(seed))
    spreads = {'L0_xattn_g_x': (1.0, 0.2),
     'L0_xattn_b_x': (0.0, 0.1),
     'L0_xattn_g_l': (1.0, 0.2),
     'L0_xattn_b_l': (0.0, 0.1),
     'L0_xattn_g_o': (1.0, 0.2),
     'L0_xattn_b_o': (0.0, 0.1),
     'L0_ffn_br': (0.0, 0.1),
     'L0_ffn_bg_s': (0.0, 0.1),
     'L0_ffn_bu_s': (0.0, 0.1),
     'L0_ffn_bd_s': (0.0, 0.1),
     'L0_ffn_bg': (0.0, 0.501),
     'L0_ffn_bu': (0.0, 0.47),
     'L0_ffn_bd': (0.0, 0.1),
     'L1_attn_gn_weight': (1.0, 0.2),
     'L1_attn_gn_bias': (0.0, 0.1),
     'L1_xattn_gamma_x': (1.0, 0.2),
     'L1_xattn_beta_x': (0.0, 0.1),
     'L1_xattn_gamma_l': (1.0, 0.2),
     'L1_xattn_beta_l': (0.0, 0.274)}
    factors = {'L0_attn_Wq': 131.856, 'L0_attn_bq': 200.0, 'L0_attn_bk': 164.083, 'L0_attn_Wk': 2.721}
    for name, (base, spread) in spreads.items():
        noise = np.random.default_rng([zlib.crc32(name.encode()), seed]).standard_normal(out[name].shape)
        drawn = base * np.exp(spread * noise) if base else spread * noise
        out[name] = jnp.asarray(drawn.astype(out[name].dtype))
    for name, factor in factors.items():
        out[name] = (out[name] * factor).astype(out[name].dtype)
    return out
```

```python
from contextlib import ExitStack

import numpy as np

import concourse.bass as bass
from concourse import mybir
from concourse.alu_op_type import AluOpType as ALU

F32 = mybir.dt.float32
F32R = mybir.dt.float32r
BF16 = mybir.dt.bfloat16
U8 = mybir.dt.uint8
ACT = mybir.ActivationFunctionType
AX_X = mybir.AxisListType.X

B, S, D = 8, 128, 128
S2 = 120
NB = 4
G = B // NB
T = NB * S
KEYS = S2 + S
LH0, LH1 = 16, 8
HD = 64
E, EI, TOPK = 32, 64, 8
PAIRS = E // 2
RH = 8
ROT = 64
GAMMA = 0.96875
DFF = 512
EPS = 1e-5
MASKED = -3.0e38

VEC = {}
for _name, _n in (("bq", 1), ("bo", 1), ("g_x0", 1), ("b_x0", 1), ("g_l0", 1), ("b_l0", 1), ("g_o0", 1),
                  ("b_o0", 1), ("bd_s", 1), ("gnw", 1), ("gnb", 1), ("g_x1", 1), ("b_x1", 1), ("g_l1", 1),
                  ("b_l1", 1), ("bg", PAIRS), ("bu", PAIRS), ("bg_s", 1), ("bu_s", 1)):
    VEC[_name] = (sum(n for _, n in VEC.values()), _n)
NVEC = sum(n for _, n in VEC.values())

CON = {}
for _name, _n in (("ident", 128), ("mean", 128), ("block", 128), ("head", 16), ("decay", 128), ("cosA", 128), ("sinA", 128),
                  ("cosX", S2), ("sinX", S2), ("vec", NVEC), ("bkv", 2 * D), ("br", E)):
    CON[_name] = (sum(n for _, n in CON.values()), _n)
NCON = sum(n for _, n in CON.values())

SPL = {}
for _name, _n in (("wq", D), ("wkv", 2 * D), ("wr", E), ("wg", E * EI), ("wu", E * EI), ("wg_s", EI), ("wu_s", EI),
                  ("rq_rot", 512), ("rq_swp", 512), ("rq_pas", 512), ("rk_rot", 512), ("rk_swp", 512),
                  ("rk_pas", 512), ("rv", 1024)):
    SPL[_name] = (sum(n for _, n in SPL.values()), _n)
NSPL = sum(n for _, n in SPL.values())
CHUNK = NSPL // 4

RAW = {}
for _name, _n in (("woT", D), ("wd", PAIRS * D), ("wd_s", D), ("bd3", D), ("xq", 512), ("xk", 512), ("xks", 512),
                  ("up", DFF), ("down", DFF)):
    RAW[_name] = (sum(n for _, n in RAW.values()), _n)
NRAW = sum(n for _, n in RAW.values())

FOLD = {"qT": 0, "kT": 1024, "vT": 2048, "o": 3072, "vT1": 4096, "o1": 4608}
NFOLD = 5120

ARENA = 11776


def decoder_kernel(nc, x_d, ctx_d, mask_d, con_d, sel_d, spl_d, raw_d, fold_d, out_d):
    ctx = ExitStack()
    with ctx:
        def sb(name, shape, dt=F32):
            return ctx.enter_context(nc.sbuf_tensor(name, shape, dt))

        def sem(name):
            return ctx.enter_context(nc.semaphore(name))

        con = sb("con", [128, NCON])
        sel = sb("sel", [96, PAIRS * 128], BF16)
        w_hi, w_lo = sb("w_hi", [128, NSPL], F32R), sb("w_lo", [128, NSPL], F32R)
        raw = sb("raw", [128, NRAW])
        fa_hi, fa_lo = sb("fa_hi", [128, LH0 * D], F32R), sb("fa_lo", [128, LH0 * D], F32R)
        fb0, fb1 = sb("fb0", [128, LH0 * D]), sb("fb1", [128, LH1 * D])
        xT, xc, sq = sb("xT", [128, T]), sb("xc", [128, T]), sb("sq", [128, T])
        rstd, hf = sb("rstd", [128, T]), sb("hf", [128, T])
        h_hi, h_lo = sb("h_hi", [128, T], F32R), sb("h_lo", [128, T], F32R)
        xin, cin = sb("xin", [128, NB, D]), sb("cin", [S2, NB, D])
        m8 = sb("m8", [1, NB * S2], U8)
        mrow = sb("mrow", [1, NB, KEYS], BF16)
        ones = sb("ones", [1, 128], BF16)
        cT = sb("cT", [128, NB, S2])
        kvT = sb("kvT", [128, NB, KEYS])
        kvc, kvl = sb("kvc", [S2, NB, D]), sb("kvl", [128, NB, D])
        small = sb("small", [128, 512])
        arena = sb("arena", [128, ARENA])

        at = [0]

        def cut(*shape, parts=128):
            n = int(np.prod(shape))
            assert at[0] + n <= ARENA, (at[0], n)
            v = arena[0:parts, at[0]:at[0] + n]
            at[0] += n
            names = "abcd"[:len(shape)]
            if len(shape) > 1:
                v = v.rearrange(f"p ({' '.join(names)}) -> p {' '.join(names)}",
                                **{k: d for k, d in zip(names[1:], shape[1:])})
            return v

        at[0] = 0
        r_fold = cut(NFOLD)
        r_ch = [cut(CHUNK), cut(CHUNK), arena[:, 0:CHUNK], arena[:, CHUNK:2 * CHUNK]]
        at[0] = 0
        q_m, q_e, q_f = cut(T), cut(T), cut(T)
        k_z, k_m, k_e, k_f = cut(NB, D), cut(NB, D), cut(NB, D), cut(NB, D)
        v_1 = cut(NB, D + 1)
        kv_b = cut(NB, D + 16)
        o_t, o_n = cut(NB, D), cut(T)
        at[0] = 0
        P = [cut(4, KEYS) for _ in range(3)]
        ptc, ptl = [rstd[:], cut(T)], [xc[:], sq[:]]
        us = cut(4, NB, S)
        g_s = [cut(4, T) for _ in range(2)]
        at[0] -= 2 * 4 * T
        xq_s, xk_s = cut(4, T), cut(4, NB, KEYS)
        xt1, xt2 = us[:, 0], us[:, 1]
        at[0] = 0
        si, tu, av = [cut(T) for _ in range(2)], [cut(T) for _ in range(2)], [cut(T) for _ in range(3)]
        lg, aff, rep, wn = cut(NB, E), cut(NB, E), cut(NB, E), cut(NB, E)
        wcat = cut(NB, 3 * E)
        w3f = cut(T)
        at[0] = 0
        r_v = cut(NB, RH * D)
        r_t1, r_t2 = [cut(T) for _ in range(2)], [cut(T) for _ in range(2)]
        r_qk = [cut(4, T) for _ in range(2)]
        r_a = [cut(4, S) for _ in range(2)]
        at[0] = 0
        f_g, f_sq = cut(4, T), cut(4, T)
        x_out = cut(NB, D)

        w3b = sb("w3b", [96, T], BF16)
        wpart = sb("wpart", [128, NB, E], BF16)
        nm, sm, rs = small[:, 0:12], small[:, 12:24], small[:, 24:36]
        top, tsum = small[:, 36:68], small[:, 68:72]
        bnst, bnag, crs = small[0:S2, 72:96], small[0:S2, 96:104], small[0:S2, 104:108]
        ve, rs_t = small[:, 256:320], small[:, 320:384]
        half_n, half_p = small[:, 384:448], small[:, 448:456]
        head8 = small[:, 456:472]
        lden = small[:, 320:384]
        bq1, gk0, gk1 = small[:, 108:109], small[:, 109:110], small[:, 110:111]
        wabs, thr, thr_n = small[:, 112:114], small[:, 114:116], small[:, 116:118]
        tern = sq
        tern2 = xc

        ps = [ctx.enter_context(nc.psum_tensor(f"bank{i}", [128, 512], F32)) for i in range(8)]

        def four(t):
            return t.rearrange("p (b s) -> p b s", b=NB)

        def c_(name, i=0, n=None):
            lo, w = CON[name]
            return con[:, lo + i:lo + (w if n is None else i + n)]

        def v_(name, i=0):
            lo = CON["vec"][0] + VEC[name][0] + i
            return con[:, lo:lo + 1]

        def s_(name, i=0, n=None):
            lo, w = SPL[name]
            n = w if n is None else n
            return w_hi[:, lo + i:lo + i + n], w_lo[:, lo + i:lo + i + n]

        def r_(name, i=0, n=None):
            lo, w = RAW[name]
            n = w if n is None else n
            return raw[:, lo + i:lo + i + n]

        ident, meanm, block = c_("ident"), c_("mean"), c_("block")

        d_con, d_fold, d_raw, d_sel = sem("d_con"), sem("d_fold"), sem("d_raw"), sem("d_sel")
        d_spl = [sem(f"d_spl{i}") for i in range(4)]
        d_x, d_c, d_m, d_out = sem("d_x"), sem("d_c"), sem("d_m"), sem("d_out")
        v_link, a_link, p_link = sem("v_link"), sem("a_link"), sem("p_link")
        w_split, w_hid = sem("w_split"), sem("w_hid")
        fold_full, fold_out = sem("fold_full"), sem("fold_out")
        tern_sum, tern_all, tern_ok = sem("tern_sum"), sem("tern_all"), sem("tern_ok")
        ln_x, ln_mean, ln_xc, ln_sq, ln_var, ln_ve, ln_pow, ln_bc, gn_ex, h_ok = (
            sem(n) for n in ("ln_x", "ln_mean", "ln_xc", "ln_sq", "ln_var", "ln_ve", "ln_pow", "ln_bc", "gn_ex", "h_ok"))
        xt_full, ct_full, kc_full, kl_full = sem("xt_full"), sem("ct_full"), sem("kc_full"), sem("kl_full")
        cn_ok, ckv_ok, kc_ok, kl_ok, m_ok = sem("cn_ok"), sem("ckv_ok"), sem("kc_ok"), sem("kl_ok"), sem("m_ok")
        c_ve, c_pow, half_ok = sem("c_ve"), sem("c_pow"), sem("half_ok")
        la_q, la_kv, la_min, la_exp, la_qf, la_kf = (sem(n) for n in ("la_q", "la_kv", "la_min", "la_exp", "la_qf",
                                                                      "la_kf"))
        la_sum, la_mask, la_nd, la_o, la_y, la_ot = (sem(n) for n in ("la_sum", "la_mask", "la_nd", "la_o", "la_y", "la_ot"))
        s_full, s_free, m_done, r_done, n_done = (sem(n) for n in ("s_full", "s_free", "m_done", "r_done", "n_done"))
        t_full, pc_done, pl_done, u_full, ue_done, bo_full = (sem(n) for n in ("t_full", "pc_done", "pl_done", "u_full",
                                                                               "ue_done", "bo_full"))
        mo_log, mo_lg, mo_sig, mo_w, mo_wt, mo_w3 = (sem(n) for n in ("mo_log", "mo_lg", "mo_sig", "mo_w", "mo_wt",
                                                                      "mo_w3"))
        mo_gu, mo_si, mo_tu, mo_wb, mo_a, mo_dn = (sem(n) for n in ("mo_gu", "mo_si", "mo_tu", "mo_wb", "mo_a",
                                                                    "mo_dn"))
        re_v, re_vs, re_p, re_t, re_t3, re_s, re_pas = (sem(n) for n in ("re_v", "re_vs", "re_p", "re_t", "re_t3",
                                                                         "re_s", "re_pas"))
        re_a, re_as, re_o, re_y = sem("re_a"), sem("re_as"), sem("re_o"), sem("re_y")
        xa_full, xa_q, xa_kx, xa_kt, xa_kl = (sem(n) for n in ("xa_full", "xa_q", "xa_kx", "xa_kt", "xa_kl"))
        ff_up, ff_g, ff_sq, ff_ms, ff_dn, fx_ok, fx_t, fx_out = (sem(n) for n in ("ff_up", "ff_g", "ff_sq", "ff_ms",
                                                                                  "ff_dn", "fx_ok", "fx_t", "fx_out"))
        f_ve, f_pow, f_rs, f_y, f_bc = (sem(n) for n in ("f_ve", "f_pow", "f_rs", "f_y", "f_bc"))

        NLN = 8
        U0, U1 = 4 * LH0 // 4, 4 * LH1 // 4

        def ln_n(g, k):
            return g * NLN + k + 1

        slots = {}
        for g in range(G):
            for u in range(-4, U0):
                if u < 0:
                    slots[g, 0, "g", u + 4] = len(slots)
                    continue
                if u + 4 < U0:
                    slots[g, 0, "g", u + 4] = len(slots)
                slots[g, 0, u, 0] = len(slots)
                slots[g, 0, u, 1] = len(slots)
            for u in range(U1):
                slots[g, 1, u, 0] = len(slots)
                slots[g, 1, u, 1] = len(slots)

        def unit_no(g, a, u):
            return g * (U0 + U1) + a * U0 + u

        def quad_no(g, a, q):
            return g * (U0 + U1) // 4 + a * U0 // 4 + q

        block_mean = small[:, 128:256]

        def bc(t, n):
            return t.rearrange("p (o e) -> p o e", o=1).to_broadcast([t.shape[0], n, t.shape[1]])

        def bc2(t):
            return bc(t, 2)

        def before(g, a, u, k):
            n = unit_no(g, a, u) - k
            g0, r = divmod(n, U0 + U1)
            return (g0, 0, r, 1) if r < U0 else (g0, 1, r - U0, 1)

        def store(sp, g):
            sp.wait_ge(fx_out, g + 1)
            sp.dma_start(out_d[g * NB:(g + 1) * NB].rearrange("b s d -> s b d"), x_out).then_inc(d_out, 16)

        block_ = ctx.enter_context(nc.Block())

        @block_.sync
        def _(sp):
            sp.dma_start(con[:], con_d).then_inc(d_con, 16)
            for g in range(G):
                if g == 0:
                    sp.dma_start(xin[:], x_d[0:NB].rearrange("b s d -> s b d")).then_inc(d_x, 16)
                    sp.dma_start(cin[:], ctx_d[0:NB].rearrange("b s d -> s b d")).then_inc(d_c, 16)
                    sp.dma_start(m8[:], mask_d[0:1, 0:NB * S2]).then_inc(d_m, 16)
                    sp.dma_start(r_fold, fold_d).then_inc(d_fold, 16)
                    for i in range(4):
                        if i == 2:
                            sp.dma_start(raw[:], raw_d).then_inc(d_raw, 16)
                            sp.wait_ge(fold_full, (2 * LH0 + LH1) // 4)
                        sp.dma_start(r_ch[i], spl_d[:, i * CHUNK:(i + 1) * CHUNK]).then_inc(d_spl[i], 16)
                    continue
                sp.wait_ge(xt_full, g)
                sp.dma_start(xin[:], x_d[g * NB:(g + 1) * NB].rearrange("b s d -> s b d")).then_inc(d_x, 16)
                sp.wait_ge(cn_ok, g)
                sp.dma_start(cin[:], ctx_d[g * NB:(g + 1) * NB].rearrange("b s d -> s b d")).then_inc(d_c, 16)
                sp.wait_ge(m_ok, g)
                sp.dma_start(m8[:], mask_d[0:1, g * NB * S2:(g + 1) * NB * S2]).then_inc(d_m, 16)
                store(sp, g - 1)
            store(sp, G - 1)
            sp.wait_ge(d_out, 16 * G)

        @block_.tensor
        def _(pe):
            mm, tr = nc.tensor.matmul, nc.tensor.transpose

            def mm3(out, w, m, start=True, stop=True, **kw):
                mm(out, w[0], m[0], start=start, stop=False, **kw)
                mm(out, w[1], m[0], start=False, stop=False, **kw)
                return mm(out, w[0], m[1], start=False, stop=stop, **kw)

            def spread_tokens():
                for b in range(NB):
                    last = tr(ps[5][:, b * S:(b + 1) * S], rs_t[:, b:b + 1].to_broadcast([128, D]), ident)
                return last

            def norm(g, k, src, w=1):
                n = ln_n(g, k)
                pe.wait_ge(ln_x, n)
                mm(ps[4][:], meanm if w == 1 else block_mean, src, start=True, stop=True).then_inc(ln_mean, 1)
                pe.wait_ge(ln_sq, n)
                for b in range(NB):
                    last = mm(ps[5][:, b * w:(b + 1) * w], four(sq[:])[:, b, :], meanm[:, 0:1] if w == 1 else head8,
                              start=True, stop=True)
                last.then_inc(ln_var, 1)
                pe.wait_ge(ln_pow, n)
                if w == 1:
                    spread_tokens().then_inc(ln_bc, 1)
                else:
                    pe.wait_ge(gn_ex, g + 1)
                    for b in range(NB):
                        last = tr(ps[5][:, b * S:(b + 1) * S], four(sq[:])[:, b, :], ident)
                    last.then_inc(ln_bc, 1)

            def fold():
                pe.wait_ge(d_fold, 16)
                for n in range((2 * LH0 + LH1) // 4):
                    if n >= 4:
                        pe.wait_ge(fold_out, n - 3)
                    a, b, h0 = (("qT", "kT", 0), ("vT", "o", LH0), ("vT1", "o1", 2 * LH0))[
                        0 if n < 4 else 1 if n < 8 else 2]
                    for j in range(4):
                        h = 8 * (n // 2) + n % 2 + 2 * j - h0
                        rows = slice(HD * (h % 2), HD * (h % 2) + HD)
                        ca, cb = FOLD[a] + h // 2 * D, FOLD[b] + h // 2 * D
                        last = mm(ps[n % 4][:, j * D:(j + 1) * D], r_fold[rows, ca:ca + D], r_fold[rows, cb:cb + D],
                                  start=True, stop=True)
                    last.then_inc(fold_full, 1)

            def alpha():
                pe.wait_ge(tern_sum, 1)
                mm(ps[6][:, 0:2], meanm, wabs, start=True, stop=True).then_inc(tern_all, 1)

            def enter(g):
                pe.wait_ge(d_x, 16 * (g + 1))
                if g == 0:
                    pe.wait_ge(d_con, 16)
                for b in range(NB):
                    last = tr(ps[6][:, b * S:(b + 1) * S], xin[:, b, :], ident)
                last.then_inc(xt_full, 1)

            def context(g):
                pe.wait_ge(cn_ok, g + 1)
                for b in range(NB):
                    last = tr(ps[7][:, b * 128:b * 128 + S2], kvc[:, b, :], ident[0:S2, 0:S2])
                last.then_inc(ct_full, 1)

            def keys_out(count, bank, rows, a):
                for b in range(NB):
                    src = kvT[:, b, 0:S2] if rows == S2 else kvT[:, b, S2:KEYS]
                    last = tr(ps[bank][0:rows, b * D:(b + 1) * D], src, ident)
                last.then_inc(kc_full if rows == S2 else kl_full, 1)

            def linear(g):
                norm(g, 0, xT[:])
                context(g)
                pe.wait_ge(h_ok, 6 * g + 1)
                if g == 0:
                    pe.wait_ge(w_split, 1)
                hb = four(h_hi[:]), four(h_lo[:])
                mm3(ps[0][:], s_("wq"), (h_hi[:], h_lo[:])).then_inc(la_q, 1)
                for b in range(NB):
                    last = mm3(ps[1 + b // 2][:, 256 * (b % 2):256 * (b % 2) + 256], (hb[0][:, b], hb[1][:, b]), s_("wkv"))
                    if b % 2:
                        last.then_inc(la_kv, 1)
                pe.wait_ge(ckv_ok, 2 * g + 1)
                keys_out(g, 7, S2, 0)
                pe.wait_ge(la_kf, g + 1)
                for b in range(NB):
                    o = (3, 6)[b // 2]
                    last = mm(ps[o][:, (D + 1) * (b % 2):(D + 1) * (b % 2) + D + 1], k_f[:, b, :], v_1[:, b, :],
                              start=True, stop=True)
                last.then_inc(la_sum, 1)
                pe.wait_ge(la_mask, g + 1)
                pe.wait_ge(la_qf, g + 1)
                w = D + 16
                for b in range(NB):
                    last = mm(ps[1 + b // 2][:, w * (b % 2):w * (b % 2) + w], four(q_f)[:, b, :], kv_b[:, b, :],
                              start=True, stop=True)
                last.then_inc(la_nd, 1)
                pe.wait_ge(la_o, 2 * g + 1)
                for b in range(NB):
                    last = tr(ps[3][:, b * S:(b + 1) * S], o_t[:, b, :], ident)
                last.then_inc(la_ot, 1)
                pe.wait_ge(la_o, 2 * g + 2)
                if g == 0:
                    pe.wait_ge(d_raw, 16)
                mm(ps[0][:], r_("woT"), o_n, start=True, stop=True).then_inc(la_y, 1)

            def attention(g, a):
                units = (U0, U1)[a]
                quads = units // 4
                fb = (fb0, fb1)[a]

                def slot(key):
                    r = slots[key]
                    if r >= 4:
                        pe.wait_ge(s_free, r - 3)
                    return ps[r % 4]

                def q_fold(n):
                    w = fa_hi[:, n * D:(n + 1) * D], fa_lo[:, n * D:(n + 1) * D]
                    mm3(slot((g, 0, "g", n))[:], w, (h_hi[:], h_lo[:])).then_inc(s_full, 1)

                def scores(u):
                    q, b = u // 4, u % 4
                    if b == 0 and a == 0:
                        pe.wait_ge(s_free, slots[g, 0, "g", 4 * q + 3] + 1)
                    for s in range(2):
                        bank = slot((g, a, u, s))
                        for j in range(2):
                            h = 2 * s + j if a == 0 else s + 2 * j
                            out = bank[:, j * KEYS:(j + 1) * KEYS]
                            if a == 0:
                                mm(out, ones[:], mrow[0:1, b], start=True, stop=False)
                                last = mm(out, four(g_s[q % 2][:, h, :])[:, b, :], kvT[:, b, :], start=False,
                                          stop=True)
                            else:
                                rows, p = slice(HD * (h % 2), HD * (h % 2) + HD), (4 * q + h) // 2
                                last = mm(out, four(xq_s[:, p, :])[rows, b, :], xk_s[rows, p, b, :], start=True,
                                          stop=True)
                        last.then_inc(s_full, 1)

                def turn(u):
                    n = unit_no(g, a, u)
                    pe.wait_ge(n_done, n + 1)
                    if n:
                        pe.wait_ge(pc_done, n)
                        pe.wait_ge(pl_done, n)
                    for h in range(4):
                        tr(ps[4][0:S2, h * S:(h + 1) * S], P[n % 3][:, h, 0:S2], ident)
                        last = tr(ps[5][:, h * S:(h + 1) * S], P[n % 3][:, h, S2:KEYS], ident)
                    last.then_inc(t_full, 1)

                def weigh(u):
                    n, b = unit_no(g, a, u), u % 4
                    pe.wait_ge(pc_done, n + 1)
                    pe.wait_ge(pl_done, n + 1)
                    if n:
                        pe.wait_ge(ue_done, n)
                    mm(ps[6][:], kvc[:, b, :], ptc[n % 2][0:S2, :], start=True, stop=False)
                    mm(ps[6][:], kvl[:, b, :], ptl[n % 2], start=False, stop=True).then_inc(u_full, 1)

                def project(q):
                    pe.wait_ge(ue_done, unit_no(g, a, 4 * q + 3) + 1)
                    for j in range(4):
                        h = 4 * q + (j if a == 0 else (0, 2, 1, 3)[j])
                        last = mm(ps[7][:], fb[:, h * D:(h + 1) * D], us[:, j].rearrange("p b s -> p (b s)"),
                                  start=(q == 0 and j == 0), stop=(q == quads - 1 and j == 3))
                    last.then_inc(bo_full, 1)

                if a == 0:
                    if g == 0:
                        pe.wait_ge(fold_out, (2 * LH0 + LH1) // 4)
                    for n in range(4):
                        q_fold(n)
                for i in range(units + 4):
                    if a == 0 and i + 4 < units:
                        q_fold(i + 4)
                    if i < units:
                        scores(i)
                    if 2 <= i < units + 2:
                        turn(i - 2)
                    if 3 <= i < units + 3:
                        if i == 3:
                            pe.wait_ge(kc_ok, 2 * g + a + 1)
                            pe.wait_ge(kl_ok, 2 * g + a + 1)
                        weigh(i - 3)
                    if i >= 4 and (i - 4) % 4 == 3:
                        project((i - 4) // 4)

            def latent0(g):
                norm(g, 1, xT[:])
                pe.wait_ge(h_ok, 6 * g + 2)
                keys_out(g, 6, S, 0)
                if g == 0:
                    pe.wait_ge(m_ok, 1)
                else:
                    pe.wait_ge(m_ok, g + 1)
                attention(g, 0)
                norm(g, 2, hf[:])

            def experts(g):
                norm(g, 3, xT[:])
                pe.wait_ge(h_ok, 6 * g + 3)
                if g == 0:
                    pe.wait_ge(w_split, 4)
                    pe.wait_ge(d_sel, 16)
                hb = four(h_hi[:]), four(h_lo[:])
                for b in range(NB):
                    last = mm3(ps[6][:, b * E:(b + 1) * E], (hb[0][:, b], hb[1][:, b]), s_("wr"))
                last.then_inc(mo_log, 1)
                n0 = g * (PAIRS + 1)

                def hidden(i):
                    n = n0 + i
                    if n >= 2:
                        pe.wait_ge(mo_si, n - 1)
                        pe.wait_ge(mo_tu, n - 1)
                    m = 128 if i < PAIRS else EI
                    wg = s_("wg", i * 128, 128) if i < PAIRS else s_("wg_s")
                    wu = s_("wu", i * 128, 128) if i < PAIRS else s_("wu_s")
                    mm3(ps[n % 2][0:m, :], wg, (h_hi[:], h_lo[:]))
                    mm3(ps[2 + n % 2][0:m, :], wu, (h_hi[:], h_lo[:])).then_inc(mo_gu, 1)

                def spread(i):
                    n = g * PAIRS + i
                    if i == 0:
                        pe.wait_ge(mo_w3, g + 1)
                    if i >= 2:
                        pe.wait_ge(mo_a, n0 + i - 1)
                    mm(ps[4 + i % 2][:], sel[:, i * 128:(i + 1) * 128], w3b[:], start=True, stop=True).then_inc(mo_wb, 1)

                def down(i):
                    pe.wait_ge(mo_a, n0 + i + 1)
                    if i == 0:
                        mm(ps[7][:], r_("bd3")[0:96, :], w3f[0:96, :], start=True, stop=False)
                    m = 128 if i < PAIRS else EI
                    w = r_("wd", i * D, D) if i < PAIRS else r_("wd_s")[0:EI, :]
                    a = av[(n0 + i) % 3][0:m, :]
                    last = mm(ps[7][:], w, a, start=False, stop=(i == PAIRS))
                    last.then_inc(mo_dn, 1)

                hidden(0)
                hidden(1)
                pe.wait_ge(mo_w, g + 1)
                for b in range(NB):
                    last = tr(ps[6][0:3 * E, b * S:(b + 1) * S], wcat[:, b, :], ident)
                last.then_inc(mo_wt, 1)
                for i in range(PAIRS + 3):
                    if 2 <= i <= PAIRS:
                        hidden(i)
                    if i < PAIRS:
                        spread(i)
                    if i >= 2:
                        down(i - 2)

            def retention(g):
                norm(g, 4, xT[:])
                pe.wait_ge(h_ok, 6 * g + 4)
                hb = four(h_hi[:]), four(h_lo[:])
                for n in range(2 * NB):
                    b, half = n // 2, n % 2
                    if n >= 4:
                        pe.wait_ge(re_vs, g * 2 * NB + n - 3)
                    mm3(ps[n % 4][:], (hb[0][:, b], hb[1][:, b]), s_("rv", half * 512, 512)).then_inc(re_v, 1)

                def project(i):
                    n = g * RH + i
                    p, k = i // 2, "qk"[i % 2]
                    if i < 2:
                        pe.wait_ge(re_vs, (g + 1) * 2 * NB - (1 if i == 0 else 0))
                    else:
                        pe.wait_ge(re_t, 2 * (n - 1))
                    if i:
                        pe.wait_ge(re_pas, n)
                    mm3(ps[0 + i % 2][:], s_(f"r{k}_rot", p * 128, 128), (h_hi[:], h_lo[:]))
                    mm3(ps[2 + i % 2][:], s_(f"r{k}_swp", p * 128, 128), (h_hi[:], h_lo[:]))
                    mm3(ps[4][:], s_(f"r{k}_pas", p * 128, 128), (h_hi[:], h_lo[:])).then_inc(re_p, 1)

                def decay(p, h):
                    n = g * RH + 2 * p + h
                    if h == 0:
                        pe.wait_ge(re_s, g * RH + 2 * p + 2)
                        pe.wait_ge(re_pas, g * RH + 2 * p + 2)
                    if n >= 2:
                        pe.wait_ge(re_as, n - 1)
                    t, rows = r_qk[p % 2], slice(64 * h, 64 * h + 64)
                    for b in range(NB):
                        o = ps[5 + h][:, b * S:(b + 1) * S]
                        mm(o, four(t[:, 0])[rows, b], four(t[:, 2])[rows, b], start=True, stop=False)
                        last = mm(o, four(t[:, 1])[rows, b], four(t[:, 3])[rows, b], start=False, stop=True)
                    last.then_inc(re_a, 1)

                def mix(p, h):
                    n = g * RH + 2 * p + h
                    pe.wait_ge(re_as, n + 1)
                    for b in range(NB):
                        c = (2 * p + h) * D
                        last = mm(ps[7][:, b * S:(b + 1) * S], r_v[:, b, c:c + D], r_a[n % 2][:, b, :],
                                  start=(p == 0 and h == 0 and b == 0), stop=(p == RH // 2 - 1 and h == 1),
                                  skip_group_check=True)
                    last.then_inc(re_o, 1)

                project(0)
                project(1)
                for p in range(RH // 2):
                    if p + 1 < RH // 2:
                        project(2 * p + 2)
                        project(2 * p + 3)
                    decay(p, 0)
                    decay(p, 1)
                    mix(p, 0)
                    mix(p, 1)
                norm(g, 5, hf[:], w=16)

            def latent1(g):
                norm(g, 6, xT[:])
                pe.wait_ge(h_ok, 6 * g + 5)
                pe.wait_ge(ckv_ok, 2 * g + 2)
                keys_out(g, 7, S2, 1)
                keys_out(g, 6, S, 1)
                for r in range(16):
                    if 4 <= r < 8:
                        pe.wait_ge(xa_q, 4 * g + r - 3)
                    elif 8 <= r:
                        pe.wait_ge(xa_kx, 8 * g + r - 7)
                    bank = ps[r % 4]
                    if r < 4:
                        last = mm(bank[:], r_("xq", r * 128, 128), kvT[:, :, S2:KEYS], start=True, stop=True)
                    elif r < 12:
                        p, name = (r - 4) // 2, ("xk", "xks")[r % 2]
                        last = mm(bank[:, 0:NB * S2], r_(name, p * 128, 128), kvT[:, :, 0:S2], start=True, stop=True)
                    else:
                        last = mm(bank[:], r_("xk", (r - 12) * 128, 128), kvT[:, :, S2:KEYS], start=True, stop=True)
                    last.then_inc(xa_full, 1)
                pe.wait_ge(xa_kl, 4 * (g + 1))
                pe.wait_ge(xa_kt, 4 * (g + 1))
                attention(g, 1)

            def ternary(g):
                norm(g, 7, xT[:])
                pe.wait_ge(h_ok, 6 * g + 6)
                if g == 0:
                    pe.wait_ge(tern_ok, 2)
                for j in range(4):
                    mm(ps[j][:], r_("up", j * 128, 128), hf[:], start=True, stop=True).then_inc(ff_up, 1)
                for j in range(4):
                    pe.wait_ge(ff_g, 4 * g + j + 1)
                    last = mm(ps[7][:], r_("down", j * 128, 128), f_g[:, j, :], start=(j == 0), stop=(j == 3))
                last.then_inc(ff_dn, 1)
                pe.wait_ge(ff_sq, 4 * g + 4)
                for b in range(NB):
                    for j in range(4):
                        last = mm(ps[6][:, b:b + 1], four(f_sq[:, j, :])[:, b, :], meanm[:, 0:1], start=(j == 0),
                                  stop=(j == 3))
                last.then_inc(ff_ms, 1)
                pe.wait_ge(f_rs, g + 1)
                spread_tokens().then_inc(f_bc, 1)
                pe.wait_ge(fx_ok, g + 1)
                for b in range(NB):
                    last = tr(ps[5][:, b * D:(b + 1) * D], four(xT[:])[:, b, :], ident)
                last.then_inc(fx_t, 1)

            enter(0)
            fold()
            alpha()
            for g in range(G):
                if g:
                    enter(g)
                linear(g)
                latent0(g)
                experts(g)
                retention(g)
                latent1(g)
                ternary(g)

        @block_.vector
        def _(dve):
            V = nc.vector
            count = [0]

            def link(ins):
                count[0] += 1
                ins.then_inc(v_link, 1)
                dve.wait_ge(v_link, count[0])

            def centre(g, k, src, eps=EPS, w=1):
                n = ln_n(g, k)
                dve.wait_ge(ln_mean, n)
                V.tensor_tensor(xc[:], src, ps[4][:], ALU.subtract).then_inc(ln_xc, 1)
                dve.wait_ge(ln_var, n)
                V.tensor_scalar(ve[:, 0:NB * w], ps[5][:, 0:NB * w], eps, None, ALU.add).then_inc(ln_ve, 1)
                if w > 1:
                    dve.wait_ge(ln_pow, n)
                    V.tensor_copy(sq[:].rearrange("p (k e) -> p k e", e=D // w),
                                  rs_t[:, 0:NB * w].rearrange("p (k o) -> p k o", o=1).to_broadcast(
                                      [128, NB * w, D // w])).then_inc(gn_ex, 1)
                dve.wait_ge(ln_bc, n)

            def parts(src, ok):
                link(V.tensor_copy(h_hi[:], src))
                V.tensor_tensor(h_lo[:], src, h_hi[:].bitcast(F32), ALU.subtract).then_inc(h_ok, 1)

            def plain_norm(g, k):
                centre(g, k, xT[:])
                link(V.tensor_tensor(hf[:], xc[:], ps[5][:], ALU.mult))
                parts(hf[:], None)

            def twice_norm(g, k, gk, shift):
                centre(g, k, xT[:], eps=EPS * EPS / (1 + EPS))
                link(V.scalar_tensor_tensor(out=hf[:], in0=xc[:], scalar=gk, in1=ps[5][:], op0=ALU.mult, op1=ALU.mult))
                link(V.tensor_scalar(hf[:], hf[:], shift, None, ALU.add))
                link(V.tensor_copy(kvT[:, :, S2:KEYS], four(hf[:])))
                parts(hf[:], None)

            def context(g):
                dve.wait_ge(d_c, 16 * (g + 1))
                if g:
                    dve.wait_ge(u_full, unit_no(g, 0, 0))
                for b in range(NB):
                    last = V.bn_stats(bnst[:, 6 * b:6 * b + 6], cin[:, b, :])
                link(last)
                for b in range(NB):
                    last = V.bn_aggr(bnag[:, 2 * b:2 * b + 2], bnst[:, 6 * b:6 * b + 6])
                link(last)
                V.tensor_scalar(crs[:, 0:NB], bnag.rearrange("p (b k) -> p k b", k=2)[:, 1, :], EPS, None,
                                ALU.add).then_inc(c_ve, 1)
                dve.wait_ge(c_pow, g + 1)
                for b in range(NB):
                    last = V.tensor_scalar(kvc[:, b, :], cin[:, b, :], bnag[:, 2 * b:2 * b + 1], crs[:, b:b + 1],
                                           ALU.subtract, ALU.mult)
                last.then_inc(cn_ok, 1)
                dve.wait_ge(d_m, 16 * (g + 1))
                mv = m8[:].rearrange("p (b k) -> p b k", b=NB)
                V.tensor_scalar(mrow[:, :, 0:S2], mv, -MASKED, MASKED, ALU.mult, ALU.add).then_inc(m_ok, 1)

            def context_keys(g, a):
                V.tensor_scalar(kvT[:, :, 0:S2], cT[:], v_(f"g_x{a}"), v_(f"b_x{a}"), ALU.mult, ALU.add)\
                    .then_inc(ckv_ok, 1)

            def prepare():
                dve.wait_ge(d_con, 16)
                V.tensor_scalar(bq1, v_("bq"), 1.0, None, ALU.add)
                V.tensor_scalar(gk0, v_("g_l0"), (1 + EPS) ** -0.5, None, ALU.mult)
                V.tensor_scalar(gk1, v_("g_l1"), (1 + EPS) ** -0.5, None, ALU.mult)
                V.tensor_scalar(block_mean, block, 0.125, None, ALU.mult)
                V.tensor_scalar(head8, c_("head"), 0.125, None, ALU.mult)
                V.memset(half_n, -0.5)
                V.memset(half_p, 0.5).then_inc(half_ok, 1)
                V.memset(mrow[:], 0.0)
                link(V.memset(ones[:], 1.0))
                dve.wait_ge(xt_full, 1)
                V.tensor_copy(xT[:], ps[6][:]).then_inc(ln_x, 1)
                context(0)
                for n in range((2 * LH0 + LH1) // 4):
                    dve.wait_ge(fold_full, n + 1)
                    def heads(t):
                        c = n // 2 % 2 * 1024
                        return t[:, c:c + 1024].rearrange("p (j two d) -> p two j d", two=2, d=D)[:, n % 2]
                    bank = ps[n % 4][:].rearrange("p (j d) -> p j d", d=D)
                    if n < 4:
                        V.tensor_scalar(heads(fa_hi), bank, HD ** -0.5, None, ALU.mult).then_inc(v_link, 1)
                        count[0] += 1
                        dve.wait_ge(v_link, count[0])
                        V.scalar_tensor_tensor(out=heads(fa_lo), in0=bank, scalar=HD ** -0.5,
                                               in1=heads(fa_hi).bitcast(F32), op0=ALU.mult, op1=ALU.subtract)\
                            .then_inc(fold_out, 1)
                    else:
                        V.tensor_copy(heads(fb0 if n < 8 else fb1), bank).then_inc(fold_out, 1)
                for i in range(4):
                    c = slice(i * CHUNK, (i + 1) * CHUNK)
                    dve.wait_ge(w_hid, i + 1)
                    V.tensor_tensor(w_lo[:, c], r_ch[i], w_hi[:, c].bitcast(F32), ALU.subtract)\
                        .then_inc(w_split, 1)
                dve.wait_ge(d_raw, 16)
                V.tensor_reduce(wabs[:, 0:1], r_("up"), AX_X, ALU.add, apply_absolute_value=True)
                V.tensor_reduce(wabs[:, 1:2], r_("down"), AX_X, ALU.add, apply_absolute_value=True).then_inc(tern_sum, 1)
                dve.wait_ge(tern_all, 1)
                V.tensor_scalar(thr, ps[6][:, 0:2], 0.5 / DFF, None, ALU.mult)
                link(V.tensor_scalar(thr_n, ps[6][:, 0:2], -0.5 / DFF, None, ALU.mult))

            def ternary_weights():
                for k, name in enumerate(("up", "down")):
                    w = r_(name)
                    V.tensor_scalar(tern[:], w, thr[:, k:k + 1], None, ALU.is_gt)
                    link(V.tensor_scalar(tern2[:], w, thr_n[:, k:k + 1], None, ALU.is_lt))
                    link(V.tensor_tensor(tern[:], tern[:], tern2[:], ALU.subtract))
                    link(V.tensor_tensor(tern[:], tern[:], w, ALU.subtract))
                    link(V.tensor_tensor(w, tern[:], w, ALU.add))
                count[0] += 0
                V.tensor_copy(thr, thr).then_inc(tern_ok, 2)

            def linear(g):
                plain_norm(g, 0)
                dve.wait_ge(ct_full, g + 1)
                link(V.tensor_copy(cT[:], ps[7][:].rearrange("p (b k) -> p b k", b=NB)[:, :, 0:S2]))
                context_keys(g, 0)
                dve.wait_ge(la_q, g + 1)
                V.tensor_scalar(q_m, ps[0][:], v_("bq"), 0.0, ALU.add, ALU.min).then_inc(la_min, 1)
                bkv = c_("bkv")
                dve.wait_ge(la_kv, 2 * g + 2)
                for i in range(2):
                    pv = ps[1 + i][:].rearrange("p (b k e) -> p k b e", b=2, k=2)
                    V.tensor_tensor(k_z[:, 2 * i:2 * i + 2, :], pv[:, 0], bc2(bkv[:, 0:D]), ALU.add)
                    last = V.tensor_tensor(v_1[:, 2 * i:2 * i + 2, 0:D], pv[:, 1], bc2(bkv[:, D:2 * D]), ALU.add)
                V.memset(v_1[:, :, D:D + 1], 1.0)
                link(last)
                V.tensor_scalar(k_m, k_z, 0.0, None, ALU.min).then_inc(la_min, 1)
                dve.wait_ge(la_exp, 2 * g + 1)
                link(V.tensor_scalar(q_e, q_e, -1.0, 1.0, ALU.add, ALU.add))
                V.scalar_tensor_tensor(out=q_f, in0=ps[0][:], scalar=bq1, in1=q_e, op0=ALU.add, op1=ALU.max)\
                    .then_inc(la_qf, 1)
                dve.wait_ge(la_exp, 2 * g + 2)
                link(V.tensor_scalar(k_e, k_e, -1.0, 1.0, ALU.add, ALU.add))
                V.scalar_tensor_tensor(out=k_f, in0=k_z, scalar=1.0, in1=k_e, op0=ALU.add, op1=ALU.max)\
                    .then_inc(la_kf, 1)
                dve.wait_ge(la_sum, g + 1)
                for i, o in enumerate((3, 6)):
                    pv = ps[o][:, 0:2 * (D + 1)].rearrange("p (b e) -> p b e", b=2)
                    V.tensor_tensor(kv_b[:, 2 * i:2 * i + 2, 0:D], pv[:, :, 0:D], bc2(block), ALU.mult)
                    for j in range(2):
                        last = V.tensor_scalar(kv_b[:, 2 * i + j, D:D + 16], c_("head"), pv[:, j, D:D + 1], None, ALU.mult)
                last.then_inc(la_mask, 1)
                dve.wait_ge(la_nd, g + 1)
                nd = [ps[1 + i][:, 0:2 * (D + 16)].rearrange("p (b e) -> p b e", b=2) for i in range(2)]
                ld = lden.rearrange("p (b h) -> p b h", b=NB)
                for i in range(2):
                    last = V.tensor_scalar(ld[:, 2 * i:2 * i + 2, :], nd[i][:, :, D:D + 16], 1e-6, None, ALU.add)
                link(last)
                link(V.reciprocal(lden, lden))
                for b in range(NB):
                    last = V.tensor_tensor(
                        o_t[:, b, :].rearrange("p (h e) -> p h e", h=16),
                        nd[b // 2][:, b % 2, 0:D].rearrange("p (h e) -> p h e", h=16),
                        ld[:, b, :].rearrange("p (h o) -> p h o", o=1).to_broadcast([128, 16, 8]), ALU.mult)
                last.then_inc(la_o, 1)
                dve.wait_ge(la_ot, g + 1)
                V.tensor_copy(o_n, ps[3][:]).then_inc(la_o, 1)
                dve.wait_ge(la_y, g + 1)
                V.scalar_tensor_tensor(out=xT[:], in0=ps[0][:], scalar=v_("bo"), in1=xT[:], op0=ALU.add, op1=ALU.add)\
                    .then_inc(ln_x, 1)

            def attention(g, a):
                units = (U0, U1)[a]

                def top_(u):
                    for s in range(2):
                        r = slots[g, a, u, s]
                        n = unit_no(g, a, u)
                        dve.wait_ge(s_full, r + 1)
                        if n >= 3 and s == 0:
                            dve.wait_ge(s_free, slots[before(g, a, u, 3)] + 1)
                        o = 4 * (n % 3) + 2 * s
                        V.tensor_reduce(nm[:, o:o + 2], ps[r % 4][:, 0:2 * KEYS].rearrange("p (h k) -> p h k", h=2), AX_X,
                                        ALU.max, negate=True).then_inc(m_done, 1)

                def recip(u):
                    n = unit_no(g, a, u)
                    o = 4 * (n % 3)
                    dve.wait_ge(s_free, slots[g, a, u, 1] + 1)
                    if n >= 3:
                        dve.wait_ge(n_done, n - 2)
                    V.reciprocal(rs[:, o:o + 4], sm[:, o:o + 4]).then_inc(r_done, 1)

                def turned(u):
                    n = unit_no(g, a, u)
                    dve.wait_ge(t_full, n + 1)
                    if n >= 2:
                        dve.wait_ge(u_full, n - 1)
                    V.tensor_copy(ptl[n % 2], ps[5][:]).then_inc(pl_done, 1)

                def weighed(u):
                    n = unit_no(g, a, u)
                    q, b = u // 4, u % 4
                    dve.wait_ge(u_full, n + 1)
                    if b == 0 and quad_no(g, a, q) >= 1:
                        dve.wait_ge(bo_full, quad_no(g, a, q))
                    V.tensor_copy(us[:, :, b, :], four(ps[6][:])).then_inc(ue_done, 1)

                for i in range(units + 3):
                    if i < units:
                        top_(i)
                    if 1 <= i <= units:
                        recip(i - 1)
                    if 2 <= i < units + 2:
                        turned(i - 2)
                    if i >= 3:
                        weighed(i - 3)
                dve.wait_ge(bo_full, quad_no(g, a, units // 4 - 1) + 1)

            def latent0(g):
                twice_norm(g, 1, gk0, v_("b_l0"))
                attention(g, 0)
                V.tensor_copy(hf[:], ps[7][:]).then_inc(ln_x, 1)
                centre(g, 2, hf[:])
                link(V.scalar_tensor_tensor(out=hf[:], in0=xc[:], scalar=v_("g_o0"), in1=ps[5][:], op0=ALU.mult,
                                            op1=ALU.mult))
                V.scalar_tensor_tensor(out=xT[:], in0=hf[:], scalar=v_("b_o0"), in1=xT[:], op0=ALU.add, op1=ALU.add)\
                    .then_inc(ln_x, 1)

            def experts(g):
                plain_norm(g, 3)
                n0 = g * (PAIRS + 1)
                br = c_("br")
                dve.wait_ge(mo_log, g + 1)
                V.tensor_tensor(lg, ps[6][:, 0:NB * E].rearrange("p (b e) -> p b e", b=NB), bc(br, NB), ALU.add)\
                    .then_inc(mo_lg, 1)
                dve.wait_ge(mo_sig, g + 1)
                for b in range(NB):
                    last = V.max(top[:, 8 * b:8 * b + 8], aff[:, b, :])
                link(last)
                for b in range(NB):
                    V.match_replace(rep[:, b, :], top[:, 8 * b:8 * b + 8], aff[:, b, :], 0.0)
                link(V.tensor_reduce(tsum, top.rearrange("p (b k) -> p b k", b=NB), AX_X, ALU.add))
                link(V.tensor_scalar(tsum, tsum, 1e-9, None, ALU.add))
                V.tensor_tensor(wn, aff, rep, ALU.subtract)
                link(V.reciprocal(tsum, tsum))
                link(V.tensor_tensor(wn, wn, tsum.rearrange("p (b o) -> p b o", o=1).to_broadcast([128, NB, E]), ALU.mult))
                for k in range(3):
                    link(V.tensor_copy(wpart[:], wn))
                    V.tensor_copy(wcat[:, :, k * E:(k + 1) * E], wpart[:])
                    link(V.tensor_tensor(wn, wn, wpart[:], ALU.subtract))
                V.tensor_copy(tsum, tsum).then_inc(mo_w, 1)
                dve.wait_ge(mo_wt, g + 1)
                link(V.tensor_copy(w3f[0:96, :], ps[6][0:96, :]))
                V.tensor_copy(w3b[:], w3f[0:96, :]).then_inc(mo_w3, 1)
                for i in range(PAIRS + 1):
                    n = n0 + i
                    m = 128 if i < PAIRS else EI
                    bu = v_("bu", i) if i < PAIRS else v_("bu_s")
                    dve.wait_ge(mo_si, n + 1)
                    dst = tu[n % 2] if i < PAIRS else av[n % 3]
                    if i == PAIRS:
                        dve.wait_ge(mo_dn, n - 2)
                    ins = V.scalar_tensor_tensor(out=dst[0:m, :], in0=ps[2 + n % 2][0:m, :], scalar=bu[0:m, :],
                                                 in1=si[n % 2][0:m, :], op0=ALU.add, op1=ALU.mult)
                    ins.then_inc(mo_tu, 1)
                    dve.wait_ge(mo_tu, n + 1)
                    if i < PAIRS:
                        dve.wait_ge(mo_wb, g * PAIRS + i + 1)
                        if i >= 3:
                            dve.wait_ge(mo_dn, n - 2)
                        V.tensor_tensor(av[n % 3], tu[n % 2], ps[4 + i % 2][:], ALU.mult).then_inc(mo_a, 1)
                    else:
                        V.tensor_copy(tsum, tsum).then_inc(mo_a, 1)
                dve.wait_ge(mo_dn, n0 + PAIRS + 1)
                V.scalar_tensor_tensor(out=xT[:], in0=ps[7][:], scalar=v_("bd_s"), in1=xT[:], op0=ALU.add, op1=ALU.add)\
                    .then_inc(ln_x, 1)

            def retention(g):
                plain_norm(g, 4)
                cos, sin = c_("cosA"), c_("sinA")

                def rotate(i):
                    n = g * RH + i
                    dve.wait_ge(re_p, n + 1)
                    if n >= 2:
                        dve.wait_ge(re_s, n - 1)
                    V.tensor_tensor(four(r_t1[n % 2]), four(ps[0 + i % 2][:]), bc(cos, NB), ALU.mult).then_inc(re_t, 1)
                    V.tensor_tensor(four(r_t2[n % 2]), four(ps[2 + i % 2][:]), bc(sin, NB), ALU.mult).then_inc(re_t, 1)

                def decayed(p, h):
                    n = g * RH + 2 * p + h
                    dve.wait_ge(re_a, n + 1)
                    if n >= 2:
                        dve.wait_ge(re_o, n - 1)
                    V.tensor_tensor(r_a[n % 2], four(ps[5 + h][:]), bc(c_("decay"), 4), ALU.mult).then_inc(re_as, 1)

                rotate(0)
                rotate(1)
                for p in range(RH // 2):
                    if p + 1 < RH // 2:
                        rotate(2 * p + 2)
                        rotate(2 * p + 3)
                    decayed(p, 0)
                    decayed(p, 1)
                dve.wait_ge(re_o, g * RH + RH)
                V.tensor_copy(hf[:], ps[7][:]).then_inc(ln_x, 1)
                centre(g, 5, hf[:], w=16)
                link(V.scalar_tensor_tensor(out=hf[:], in0=xc[:], scalar=v_("gnw"), in1=ps[5][:], op0=ALU.mult,
                                            op1=ALU.mult))
                V.scalar_tensor_tensor(out=xT[:], in0=hf[:], scalar=v_("gnb"), in1=xT[:], op0=ALU.add, op1=ALU.add)\
                    .then_inc(ln_x, 1)

            def latent1(g):
                context_keys(g, 1)
                twice_norm(g, 6, gk1, v_("b_l1"))
                cos, sin = c_("cosX"), c_("sinX")
                for p in range(4):
                    for k, (o, f) in enumerate(((xt1, cos), (xt2, sin))):
                        r = 4 + 2 * p + k
                        dve.wait_ge(xa_full, 16 * g + r + 1)
                        if p:
                            dve.wait_ge(xa_kt, 4 * g + p)
                        V.tensor_tensor(o[:, :, 0:S2], ps[r % 4][:, 0:NB * S2].rearrange("p (b k) -> p b k", b=NB),
                                        bc(f, NB), ALU.mult).then_inc(xa_kx, 1)
                attention(g, 1)
                V.tensor_tensor(xT[:], ps[7][:], xT[:], ALU.add).then_inc(ln_x, 1)

            def ternary(g):
                n = ln_n(g, 7)
                dve.wait_ge(ln_mean, n)
                V.tensor_tensor(xc[:], xT[:], ps[4][:], ALU.subtract).then_inc(ln_xc, 1)
                dve.wait_ge(ln_var, n)
                V.tensor_copy(ve[:, 0:NB], ps[5][:, 0:NB])
                V.tensor_scalar(ve[:, NB:2 * NB], ps[5][:, 0:NB], EPS, None, ALU.add).then_inc(ln_ve, 1)
                dve.wait_ge(f_pow, 2 * g + 1)
                link(V.scalar_tensor_tensor(out=rs_t[:, 0:NB], in0=rs_t[:, NB:2 * NB], scalar=1e-8, in1=rs_t[:, 0:NB],
                                            op0=ALU.mult, op1=ALU.add))
                V.reciprocal(rs_t[:, 0:NB], rs_t[:, 0:NB]).then_inc(ln_pow, 1)
                dve.wait_ge(ln_bc, n)
                V.tensor_tensor(hf[:], xc[:], ps[5][:], ALU.mult).then_inc(h_ok, 1)
                dve.wait_ge(ff_ms, g + 1)
                V.tensor_scalar(ve[:, 0:NB], ps[6][:, 0:NB], 128.0 / DFF, None, ALU.mult).then_inc(f_ve, 1)
                dve.wait_ge(f_pow, 2 * g + 2)
                link(V.tensor_scalar(rs_t[:, 0:NB], rs_t[:, 0:NB], 1e-8, None, ALU.add))
                V.reciprocal(rs_t[:, 0:NB], rs_t[:, 0:NB]).then_inc(f_rs, 1)
                dve.wait_ge(ff_dn, g + 1)
                V.tensor_copy(hf[:], ps[7][:]).then_inc(f_y, 1)
                dve.wait_ge(f_y, g + 1)
                dve.wait_ge(f_bc, g + 1)
                link(V.tensor_tensor(hf[:], hf[:], ps[5][:], ALU.mult))
                V.tensor_tensor(xT[:], xT[:], hf[:], ALU.add).then_inc(fx_ok, 1)
                dve.wait_ge(fx_t, g + 1)
                if g:
                    dve.wait_ge(d_out, 16 * g)
                V.tensor_copy(x_out, four(ps[5][:])).then_inc(fx_out, 1)

            prepare()
            ternary_weights()
            for g in range(G):
                if g:
                    dve.wait_ge(xt_full, g + 1)
                    V.tensor_copy(xT[:], ps[6][:]).then_inc(ln_x, 1)
                    dve.wait_ge(d_out, 16 * g)
                    context(g)
                linear(g)
                latent0(g)
                experts(g)
                retention(g)
                latent1(g)
                ternary(g)

        @block_.scalar
        def _(act):
            A = nc.scalar.activation

            def squares(g, k):
                act.wait_ge(ln_xc, ln_n(g, k))
                A(sq[:], xc[:], ACT.Square).then_inc(ln_sq, 1)

            def prepare():
                act.dma_start(sel[:], sel_d).then_inc(d_sel, 16)
                for i in range(4):
                    c = slice(i * CHUNK, (i + 1) * CHUNK)
                    act.wait_ge(d_spl[i], 16)
                    A(w_hi[:, c], r_ch[i], ACT.Copy).then_inc(w_hid, 1)

            def linear(g):
                squares(g, 0)
                act.wait_ge(la_min, 2 * g + 1)
                A(q_e, q_m, ACT.Exp).then_inc(la_exp, 1)
                act.wait_ge(la_min, 2 * g + 2)
                A(k_e, k_m, ACT.Exp).then_inc(la_exp, 1)
                act.wait_ge(kc_full, 2 * g + 1)
                A(kvc[:], ps[7][0:S2, :].rearrange("p (b d) -> p b d", b=NB), ACT.Copy).then_inc(kc_ok, 1)

            def attention(g, a):
                units = (U0, U1)[a]

                def query(n):
                    r = slots[g, 0, "g", n]
                    act.wait_ge(s_full, r + 1)
                    A(g_s[n // 4 % 2][:, n % 4, :], ps[r % 4][:], ACT.Copy).then_inc(s_free, 1)

                def exps(u):
                    n = unit_no(g, a, u)
                    for s in range(2):
                        r = slots[g, a, u, s]
                        act.wait_ge(m_done, 2 * n + s + 1)
                        if s == 0 and n >= 3:
                            act.wait_ge(t_full, n - 2)
                            act.wait_ge(r_done, n - 2)
                        for j in range(2):
                            o = 4 * (n % 3) + 2 * s + j
                            last = A(P[n % 3][:, 2 * s + j, :], ps[r % 4][:, j * KEYS:(j + 1) * KEYS], ACT.Exp,
                                     bias=nm[:, o:o + 1], accum_out=sm[:, o:o + 1])
                        last.then_inc(s_free, 1)

                def turned(u):
                    n = unit_no(g, a, u)
                    act.wait_ge(t_full, n + 1)
                    if n >= 2:
                        act.wait_ge(u_full, n - 1)
                    A(ptc[n % 2][0:S2, :], ps[4][0:S2, :], ACT.Copy).then_inc(pc_done, 1)

                if a == 0:
                    for n in range(4):
                        query(n)
                for i in range(units + 2):
                    if a == 0 and i + 4 < units:
                        query(i + 4)
                    if i < units:
                        exps(i)
                    if i >= 2:
                        turned(i - 2)

            def latent0(g):
                squares(g, 1)
                act.wait_ge(kl_full, 2 * g + 1)
                A(kvl[:], four(ps[6][:]), ACT.Copy).then_inc(kl_ok, 1)
                attention(g, 0)
                squares(g, 2)

            def experts(g):
                squares(g, 3)
                n0 = g * (PAIRS + 1)
                act.wait_ge(mo_lg, g + 1)
                A(aff, lg, ACT.Sigmoid).then_inc(mo_sig, 1)
                for i in range(PAIRS + 1):
                    n = n0 + i
                    m = 128 if i < PAIRS else EI
                    bg = v_("bg", i) if i < PAIRS else v_("bg_s")
                    act.wait_ge(mo_gu, n + 1)
                    if n >= 2:
                        act.wait_ge(mo_tu, n - 1)
                    A(si[n % 2][0:m, :], ps[n % 2][0:m, :], ACT.Silu, bias=bg[0:m, :]).then_inc(mo_si, 1)

            def retention(g):
                squares(g, 4)
                for n in range(2 * NB):
                    act.wait_ge(re_v, g * 2 * NB + n + 1)
                    A(r_v[:, n // 2, n % 2 * 512:n % 2 * 512 + 512], ps[n % 4][:], ACT.Silu).then_inc(re_vs, 1)
                for i in range(RH):
                    n = g * RH + i
                    t = r_qk[i // 2 % 2]
                    act.wait_ge(re_p, n + 1)
                    if i % 2 == 0 and i >= 4:
                        act.wait_ge(re_a, g * RH + i - 2)
                    A(t[:, 2 * (i % 2) + 1, :], ps[4][:], ACT.Silu).then_inc(re_pas, 1)
                    act.wait_ge(re_t3, n + 1)
                    A(t[:, 2 * (i % 2), :], r_t1[n % 2], ACT.Silu).then_inc(re_s, 1)
                squares(g, 5)

            def latent1(g):
                squares(g, 6)
                act.wait_ge(kc_full, 2 * g + 2)
                A(kvc[:], ps[7][0:S2, :].rearrange("p (b d) -> p b d", b=NB), ACT.Copy).then_inc(kc_ok, 1)
                act.wait_ge(kl_full, 2 * g + 2)
                A(kvl[:], four(ps[6][:]), ACT.Copy).then_inc(kl_ok, 1)
                for p in range(4):
                    act.wait_ge(xa_full, 16 * g + p + 1)
                    A(xq_s[:, p, :], ps[p][:], ACT.Copy, scale=HD ** -0.5).then_inc(xa_q, 1)
                for p in range(4):
                    act.wait_ge(xa_full, 16 * g + 12 + p + 1)
                    A(xk_s[:, p, :, S2:KEYS], four(ps[p][:]), ACT.Copy).then_inc(xa_kl, 1)
                attention(g, 1)

            def ternary(g):
                squares(g, 7)
                for j in range(4):
                    act.wait_ge(ff_up, 4 * g + j + 1)
                    A(f_g[:, j, :], ps[j][:], ACT.Gelu).then_inc(ff_g, 1)

            prepare()
            for g in range(G):
                linear(g)
                latent0(g)
                experts(g)
                retention(g)
                latent1(g)
                ternary(g)

        @block_.gpsimd
        def _(pool):
            def attention(g, a):
                for u in range((U0, U1)[a]):
                    n = unit_no(g, a, u)
                    o = 4 * (n % 3)
                    pool.wait_ge(r_done, n + 1)
                    r = rs[:, o:o + 4].rearrange("p (h o) -> p h o", o=1).to_broadcast([128, 4, KEYS])
                    nc.gpsimd.tensor_tensor(P[n % 3], P[n % 3], r, ALU.mult).then_inc(n_done, 1)

            def factor(g, k, w=1):
                pool.wait_ge(ln_ve, ln_n(g, k))
                nc.gpsimd.tensor_tensor(rs_t[:, 0:NB * w], ve[:, 0:NB * w], half_n[:, 0:NB * w], ALU.pow)\
                    .then_inc(ln_pow, 1)

            def root(g, n, w):
                nc.gpsimd.tensor_tensor(rs_t[:, 0:w], ve[:, 0:w], half_p[:, 0:w], ALU.pow).then_inc(f_pow, 1)

            pool.wait_ge(half_ok, 1)
            for g in range(G):
                pool.wait_ge(c_ve, g + 1)
                nc.gpsimd.tensor_tensor(crs[:, 0:NB], crs[:, 0:NB], half_n[0:S2, 0:NB], ALU.pow).then_inc(c_pow, 1)
                factor(g, 0)
                factor(g, 1)
                attention(g, 0)
                factor(g, 2)
                factor(g, 3)
                factor(g, 4)
                for i in range(RH):
                    n = g * RH + i
                    pool.wait_ge(re_t, 2 * n + 2)
                    nc.gpsimd.tensor_tensor(r_t1[n % 2], r_t1[n % 2], r_t2[n % 2], ALU.add).then_inc(re_t3, 1)
                factor(g, 5, w=16)
                factor(g, 6)
                for p in range(4):
                    pool.wait_ge(xa_kx, 8 * g + 2 * p + 2)
                    nc.gpsimd.tensor_tensor(xk_s[:, p, :, 0:S2], xt1[:, :, 0:S2], xt2[:, :, 0:S2], ALU.add)\
                        .then_inc(xa_kt, 1)
                attention(g, 1)
                pool.wait_ge(ln_ve, ln_n(g, 7))
                root(g, 0, 2 * NB)
                for j in range(4):
                    pool.wait_ge(ff_g, 4 * g + j + 1)
                    nc.gpsimd.tensor_tensor(f_sq[:, j, :], f_g[:, j, :], f_g[:, j, :], ALU.mult).then_inc(ff_sq, 1)
                pool.wait_ge(f_ve, g + 1)
                root(g, 1, NB)


def _constants():
    f = np.float32
    con = np.zeros((128, NCON), f)

    def put(name, a):
        lo, n = CON[name]
        con[:, lo:lo + n] = a
    i = np.arange(128)
    put("ident", np.eye(128))
    put("mean", np.full((128, 128), 1 / 128))
    put("block", (i[:, None] // 8 == i[None, :] // 8))
    put("head", (i[:, None] // 8 == np.arange(16)[None, :]))
    diff = i[:, None] - i[None, :]
    put("decay", np.where(diff >= 0, f(GAMMA) ** np.maximum(diff, 0).astype(f), 0))
    inv = (1.0 / 10000.0 ** (np.arange(0, ROT, 2, dtype=f) / f(ROT))).astype(f)
    ang = (np.arange(S, dtype=f)[None, :] * np.tile(np.repeat(inv, 2), 2)[:, None]).astype(f)
    put("cosA", np.cos(ang))
    put("sinA", np.sin(ang) * np.where(i % 2 == 0, -1, 1)[:, None])
    ang = (np.arange(S2, dtype=f)[None, :] * np.tile(inv, 4)[:, None]).astype(f)
    put("cosX", np.cos(ang))
    put("sinX", np.sin(ang) * np.where(i % HD < HD // 2, -1, 1)[:, None])
    sel = np.zeros((96, PAIRS * 128), f)
    for p in range(PAIRS):
        for m in range(128):
            for k in range(3):
                sel[k * E + 2 * p + m // EI, p * 128 + m] = 1
    return con, sel


def _layout(a):
    con, sel = _constants()
    f = np.float32

    def vec(name, v):
        lo = CON["vec"][0] + VEC[name][0]
        v = np.asarray(v)
        v = v.reshape(VEC[name][1], -1).T
        con[0:v.shape[0], lo:lo + v.shape[1]] = v
    for name, key in (("bq", "L0_attn_bq"), ("bo", "L0_attn_bo"), ("g_x0", "L0_xattn_g_x"), ("b_x0", "L0_xattn_b_x"),
                      ("g_l0", "L0_xattn_g_l"), ("b_l0", "L0_xattn_b_l"), ("g_o0", "L0_xattn_g_o"),
                      ("b_o0", "L0_xattn_b_o"), ("bd_s", "L0_ffn_bd_s"), ("gnw", "L1_attn_gn_weight"),
                      ("gnb", "L1_attn_gn_bias"), ("g_x1", "L1_xattn_gamma_x"), ("b_x1", "L1_xattn_beta_x"),
                      ("g_l1", "L1_xattn_gamma_l"), ("b_l1", "L1_xattn_beta_l"), ("bg", "L0_ffn_bg"),
                      ("bu", "L0_ffn_bu"), ("bg_s", "L0_ffn_bg_s"), ("bu_s", "L0_ffn_bu_s")):
        vec(name, a[key])
    lo, n = CON["bkv"]
    con[:, lo:lo + D] = a["L0_attn_bk"][None, :]
    con[:, lo + D:lo + n] = a["L0_attn_bv"][None, :]
    lo, n = CON["br"]
    con[:, lo:lo + n] = a["L0_ffn_br"][None, :]

    spl = np.zeros((128, NSPL), f)

    def put(pack, table, name, w):
        lo, n = table[name]
        w = np.asarray(w).reshape(-1, n)
        pack[0:w.shape[0], lo:lo + n] = w
    put(spl, SPL, "wq", a["L0_attn_Wq"].T)
    put(spl, SPL, "wkv", np.concatenate([a["L0_attn_Wk"].T, a["L0_attn_Wv"].T], axis=1))
    put(spl, SPL, "wr", a["L0_ffn_Wr"])
    put(spl, SPL, "wg", a["L0_ffn_Wg"].transpose(1, 0, 2).reshape(D, -1))
    put(spl, SPL, "wu", a["L0_ffn_Wu"].transpose(1, 0, 2).reshape(D, -1))
    put(spl, SPL, "wg_s", a["L0_ffn_Wg_s"])
    put(spl, SPL, "wu_s", a["L0_ffn_Wu_s"])
    for k in "QK":
        w = a[f"L1_attn_W_{k}"].reshape(D, RH, D)
        rot, pas = w[:, :, 0:ROT], w[:, :, ROT:]
        put(spl, SPL, f"r{k.lower()}_rot", rot.reshape(D, -1))
        put(spl, SPL, f"r{k.lower()}_swp", rot[:, :, np.arange(ROT) ^ 1].reshape(D, -1))
        put(spl, SPL, f"r{k.lower()}_pas", pas.reshape(D, -1))
    put(spl, SPL, "rv", a["L1_attn_W_V"])

    raw = np.zeros((128, NRAW), f)
    put(raw, RAW, "woT", a["L0_attn_Wo"].T)
    put(raw, RAW, "wd", a["L0_ffn_Wd"].reshape(PAIRS, 128, D).transpose(1, 0, 2).reshape(128, -1))
    put(raw, RAW, "wd_s", a["L0_ffn_Wd_s"])
    put(raw, RAW, "bd3", np.concatenate([a["L0_ffn_bd"]] * 3, axis=0))
    inner = LH1 * HD
    wk = a["L1_xattn_Wkv"][:, 0:inner]
    put(raw, RAW, "xq", a["L1_xattn_Wq"])
    put(raw, RAW, "xk", wk)
    put(raw, RAW, "xks", wk.reshape(D, LH1, 2, HD // 2)[:, :, ::-1, :].reshape(D, -1))
    put(raw, RAW, "up", a["L1_ffn_w_up"].T)
    put(raw, RAW, "down", a["L1_ffn_w_down"].T.reshape(4, 128, D).transpose(1, 0, 2).reshape(128, -1))

    def pairs(w):
        return w.reshape(-1, 128, w.shape[1]).transpose(1, 0, 2).reshape(128, -1)
    inner0 = LH0 * HD
    kv = a["L0_xattn_Wkv"]
    fold = np.concatenate([pairs(a["L0_xattn_Wq"].T), pairs(kv[:, 0:inner0].T), pairs(kv[:, inner0:].T),
                           pairs(a["L0_xattn_Wout"]), pairs(a["L1_xattn_Wkv"][:, inner:].T),
                           pairs(a["L1_xattn_Wo"])], axis=1)
    return con, sel, spl, raw, fold


def kernel(**inputs):
    import ml_dtypes
    import concourse.bacc as _bacc
    from concourse.bass_utils import run_bass_kernel_spmd as _run

    a = {k: np.asarray(v) for k, v in inputs.items()}
    con, sel, spl, raw, fold = _layout(a)
    arrays = {
        "x": np.ascontiguousarray(a["x"]), "ctx": np.ascontiguousarray(a["ctx_1024"]),
        "mask": np.ascontiguousarray(a["mask_BxS2_bf1"]).view(np.uint8).reshape(1, B * S2),
        "con": con, "sel": sel.astype(ml_dtypes.bfloat16), "spl": spl, "raw": raw, "fold": np.ascontiguousarray(fold),
    }
    nc = _bacc.Bacc("TRN2", target_bir_lowering=False, num_devices=1)
    args = [nc.dram_tensor(f"in_{k}", v.shape, mybir.dt.from_np(v.dtype), kind="ExternalInput").ap()
            for k, v in arrays.items()]
    args.append(nc.dram_tensor("out_0", (B, S, D), F32, kind="ExternalOutput").ap())
    decoder_kernel(nc, *args)
    r = _run(nc, [{f"in_{k}": v for k, v in arrays.items()}], core_ids=[0])
    return r.results[0]["out_0"]
```

```python
from contextlib import ExitStack

import numpy as np

import concourse.bass as bass
from concourse import mybir
from concourse.alu_op_type import AluOpType as ALU

F32 = mybir.dt.float32
F32R = mybir.dt.float32r
BF16 = mybir.dt.bfloat16
U8 = mybir.dt.uint8
ACT = mybir.ActivationFunctionType
AX_X = mybir.AxisListType.X

B, S, D = 8, 128, 128
S2 = 120
NB = 4
G = B // NB
T = NB * S
KEYS = S2 + S
LH0, LH1 = 16, 8
HD = 64
E, EI, TOPK = 32, 64, 8
PAIRS = E // 2
RH = 8
ROT = 64
GAMMA = 0.96875
DFF = 512
EPS = 1e-5
MASKED = -3.0e38

VEC = {}
for _name, _n in (("bq", 1), ("bo", 1), ("g_x0", 1), ("b_x0", 1), ("g_l0", 1), ("b_l0", 1), ("g_o0", 1),
                  ("b_o0", 1), ("bd_s", 1), ("gnw", 1), ("gnb", 1), ("g_x1", 1), ("b_x1", 1), ("g_l1", 1),
                  ("b_l1", 1), ("bg", PAIRS), ("bu", PAIRS), ("bg_s", 1), ("bu_s", 1)):
    VEC[_name] = (sum(n for _, n in VEC.values()), _n)
NVEC = sum(n for _, n in VEC.values())

CON = {}
for _name, _n in (("ident", 128), ("mean", 128), ("block", 128), ("head", 16), ("decay", 128), ("cosA", 128), ("sinA", 128),
                  ("cosX", S2), ("sinX", S2), ("vec", NVEC), ("bkv", 2 * D), ("br", E)):
    CON[_name] = (sum(n for _, n in CON.values()), _n)
NCON = sum(n for _, n in CON.values())

def columns(*names):
    table = {}
    for name, n in names:
        table[name] = (sum(m for _, m in table.values()), n)
    return table, sum(m for _, m in table.values())


LIN, NLIN = columns(("wq", D), ("wkv", 2 * D))
MOE, NMOE = columns(("wr", E), ("wg", E * EI), ("wu", E * EI), ("wg_s", EI), ("wu_s", EI))
RET, NRET = columns(("rv", 1024), ("rq_rot", 512), ("rq_swp", 512), ("rq_pas", 512), ("rk_rot", 512), ("rk_swp", 512),
                    ("rk_pas", 512))
CH = 8
RING = 5
RAW, NRAW = columns(("woT", D), ("wd", PAIRS * D), ("wd_s", D), ("bd3", D))
XAT, NXAT = columns(("xq", 512), ("xk", 512), ("xks", 512))
FFN, NFFN = columns(("up", DFF), ("down", DFF))
FOLD = {"qT": 0, "kT": 1024, "vT": 2048, "o": 3072, "vT1": 4096, "o1": 4608}
NFOLD = 5120
QF = LH0 * D
STAGE = max(RING * (NMOE // CH), 4 * T + NFFN)
ARENA = 11264


def weave(main, side, every=1):
    n = 0
    for _ in main:
        n += 1
        if n % every == 0:
            next(side, None)
    for _ in side:
        pass


def decoder_kernel(nc, x_d, ctx_d, mask_d, con_d, sel_d, lin_d, moe_d, ret_d, raw_d, xat_d, ffn_d, fold_d, out_d):
    ctx = ExitStack()
    with ctx:
        def sb(name, shape, dt=F32):
            return ctx.enter_context(nc.sbuf_tensor(name, shape, dt))

        def sem(name):
            return ctx.enter_context(nc.semaphore(name))

        def sems(name):
            return [sem(f"{name}_{g}") for g in range(G)]

        con = sb("con", [128, NCON])
        sel = sb("sel", [96, PAIRS * 128], BF16)
        wa = sb("wa", [128, 2 * NRET], F32R)
        wb = sb("wb", [128, 2 * NMOE], F32R)
        stage = sb("stage", [128, STAGE])
        raw = sb("raw", [128, NRAW])
        fb0, fb1 = sb("fb0", [128, LH0 * D]), sb("fb1", [128, LH1 * D])
        mrow = sb("mrow", [128, B, S2], BF16)
        ones = sb("ones", [128, 128], BF16)
        small = sb("small", [128, 272])
        wpart = sb("wpart", [128, NB, E], BF16)
        m8 = sb("m8", [1, B * S2], U8)
        xT = [sb(f"xT{g}", [128, T]) for g in range(G)]
        xc = [sb(f"xc{g}", [128, T]) for g in range(G)]
        sq = [sb(f"sq{g}", [128, T]) for g in range(G)]
        hf = [sb(f"hf{g}", [128, T]) for g in range(G)]
        h_hi = [sb(f"h_hi{g}", [128, T], F32R) for g in range(G)]
        h_lo = [sb(f"h_lo{g}", [128, T], F32R) for g in range(G)]
        cT = [sb(f"cT{g}", [128, NB, S2]) for g in range(G)]
        kvT = [sb(f"kvT{g}", [128, NB, KEYS]) for g in range(G)]
        kvc = [sb(f"kvc{g}", [S2, NB, D]) for g in range(G)]
        kvl = [sb(f"kvl{g}", [128, NB, D]) for g in range(G)]
        tiny = [sb(f"tiny{g}", [128, 240]) for g in range(G)]
        arena = sb("arena", [128, ARENA])

        def shaped(v, *shape):
            names = "abcd"[:len(shape)]
            if len(shape) == 1:
                return v
            return v.rearrange(f"p ({' '.join(names)}) -> p {' '.join(names)}",
                               **{k: d for k, d in zip(names[1:], shape[1:])})

        at = [0]

        def cut(*shape):
            n = int(np.prod(shape))
            assert at[0] + n <= ARENA, (at[0], n)
            at[0] += n
            return shaped(arena[:, at[0] - n:at[0]], *shape)

        r_fold = cut(NFOLD)
        q_m, q_f = cut(T), cut(T)
        q_e = q_m
        k_z, k_m, k_f = cut(NB, D), cut(NB, D), cut(NB, D)
        k_e = k_m
        v_1 = cut(NB, D + 1)
        kv_b = cut(NB, D + 16)
        o_t, o_n = cut(NB, D), cut(T)
        at[0] = 0
        P = [cut(4, KEYS) for _ in range(3)]
        ptc, ptl = [cut(T) for _ in range(2)], [cut(T) for _ in range(2)]
        us = cut(4, NB, S)
        g_s = [cut(4, T) for _ in range(2)]
        at[0] -= 2 * 4 * T
        xk_s = cut(4, NB, KEYS)
        xq_s = shaped(stage[:, 0:4 * T], 4, T)
        xt1, xt2 = us[:, 0], us[:, 1]
        at[0] = 0
        si, tu, av = [cut(T) for _ in range(2)], [cut(T) for _ in range(2)], [cut(T) for _ in range(3)]
        at[0] = 0
        r_v = cut(NB, RH * D)
        r_t1, r_t2 = [cut(T) for _ in range(2)], [cut(T) for _ in range(2)]
        r_qk = [cut(4, T) for _ in range(2)]
        r_a = [cut(4, S) for _ in range(2)]
        at[0] = 0
        f_g, f_sq = cut(4, T), cut(4, T)
        x_out = [cut(NB, D) for _ in range(G)]

        lg, aff, rep, wn = ([shaped(hf[g][:, i * NB * E:(i + 1) * NB * E], NB, E) for g in range(G)] for i in range(4))
        wcat = [shaped(xc[g][:, 0:NB * 3 * E], NB, 3 * E) for g in range(G)]
        w3f = [sq[g][0:96, :] for g in range(G)]
        w3b = [xc[g][0:96, 0:T // 2].bitcast(BF16) for g in range(G)]
        nm, sm, rs = small[:, 0:12], small[:, 12:24], small[:, 24:36]
        bq1, gk0, gk1 = small[:, 36:37], small[:, 37:38], small[:, 38:39]
        wabs, thr, thr_n = small[:, 40:42], small[:, 42:44], small[:, 44:46]
        half_n, half_p, head8 = small[:, 48:112], small[:, 112:120], small[:, 120:136]
        block_mean = small[:, 136:264]
        ve, rs_t = [t[:, 0:64] for t in tiny], [t[:, 64:128] for t in tiny]
        lden = rs_t
        top, tsum = [t[:, 128:160] for t in tiny], [t[:, 160:164] for t in tiny]
        bnst, bnag, crs = ([t[0:S2, a:b] for t in tiny] for a, b in ((168, 192), (192, 200), (200, 204)))

        ps = [ctx.enter_context(nc.psum_tensor(f"bank{i}", [128, 512], F32)) for i in range(8)]
        OUT, CHAIN = ps[6], ps[7]

        def four(t):
            return t.rearrange("p (b s) -> p b s", b=NB)

        def c_(name):
            lo, w = CON[name]
            return con[:, lo:lo + w]

        def v_(name, i=0):
            lo = CON["vec"][0] + VEC[name][0] + i
            return con[:, lo:lo + 1]

        def split(t, base, size, table, name, i=0, n=None):
            lo, w = table[name]
            lo, n = base + lo + i, w if n is None else n
            return t[:, lo:lo + n], t[:, size + lo:size + lo + n]

        def lin(name):
            return split(wa, 2 * QF, NLIN, LIN, name)

        def moe(name, *a):
            return split(wb, 0, NMOE, MOE, name, *a)

        def ret(name, *a):
            return split(wa, 0, NRET, RET, name, *a)

        def whole(t, base, table, name, i=0, n=None):
            lo, w = table[name]
            return t[:, base + lo + i:base + lo + i + (w if n is None else n)]

        def r_(name, *a):
            return whole(raw, 0, RAW, name, *a)

        def x_(name, *a):
            return whole(fb0, 0, XAT, name, *a)

        def f_(name, *a):
            return whole(stage, 4 * T, FFN, name, *a)

        fa_hi, fa_lo = wa[:, 0:QF], wa[:, QF:2 * QF]
        ident, meanm, block = c_("ident"), c_("mean"), c_("block")

        d_con, d_fold, d_raw, d_sel, d_lin, d_xat, d_ffn, d_m = (sem(n) for n in (
            "d_con", "d_fold", "d_raw", "d_sel", "d_lin", "d_xat", "d_ffn", "d_m"))
        d_ring = [sem(f"d_ring{i}") for i in range(RING)]
        d_x, d_c, d_out = sems("d_x"), sems("d_c"), sem("d_out")
        v_link = sem("v_link")
        l_split, w_hid, w_split = sem("l_split"), sem("w_hid"), sem("w_split")
        fold_full, fold_out = sem("fold_full"), sem("fold_out")
        tern_sum, tern_all, tern_ok, half_ok = sem("tern_sum"), sem("tern_all"), sem("tern_ok"), sem("half_ok")
        ln_x, ln_mean, ln_xc, ln_sq, ln_var, ln_ve, ln_pow, ln_bc, gn_ex, h_ok = (sems(n) for n in (
            "ln_x", "ln_mean", "ln_xc", "ln_sq", "ln_var", "ln_ve", "ln_pow", "ln_bc", "gn_ex", "h_ok"))
        xt_full, ct_full, kc_full, kl_full, cn_ok, ckv_ok, kc_ok, kl_ok, c_ve, c_pow = (sems(n) for n in (
            "xt_full", "ct_full", "kc_full", "kl_full", "cn_ok", "ckv_ok", "kc_ok", "kl_ok", "c_ve", "c_pow"))
        m_ok = sem("m_ok")
        mo_log, mo_lg, mo_sig, mo_w, mo_wt, mo_w3 = (sems(n) for n in (
            "mo_log", "mo_lg", "mo_sig", "mo_w", "mo_wt", "mo_w3"))
        la_q, la_kv, la_min, la_exp, la_qf, la_kf, la_sum, la_mask, la_nd, la_o, la_y, la_ot = (sem(n) for n in (
            "la_q", "la_kv", "la_min", "la_exp", "la_qf", "la_kf", "la_sum", "la_mask", "la_nd", "la_o", "la_y",
            "la_ot"))
        s_full, s_free, m_done, r_done, n_done = (sem(n) for n in ("s_full", "s_free", "m_done", "r_done", "n_done"))
        t_full, pc_done, pl_done, u_full, ue_done, bo_full = (sem(n) for n in (
            "t_full", "pc_done", "pl_done", "u_full", "ue_done", "bo_full"))
        mo_gu, mo_si, mo_tu, mo_wb, mo_a, mo_dn = (sem(n) for n in ("mo_gu", "mo_si", "mo_tu", "mo_wb", "mo_a",
                                                                    "mo_dn"))
        re_v, re_vs, re_p, re_t, re_t3, re_s, re_pas, re_a, re_as, re_o = (sem(n) for n in (
            "re_v", "re_vs", "re_p", "re_t", "re_t3", "re_s", "re_pas", "re_a", "re_as", "re_o"))
        xa_full, xa_q, xa_kx, xa_kt, xa_kl = (sem(n) for n in ("xa_full", "xa_q", "xa_kx", "xa_kt", "xa_kl"))
        ff_up, ff_g, ff_sq, ff_ms, ff_dn, fx_ok, fx_t, fx_out, f_ve, f_pow, f_rs, f_y, f_bc, f_root = (
            sem(n) for n in ("ff_up", "ff_g", "ff_sq", "ff_ms", "ff_dn", "fx_ok", "fx_t", "fx_out", "f_ve", "f_pow",
                             "f_rs", "f_y", "f_bc", "f_root"))

        UNITS = (4 * LH0 // 4, 4 * LH1 // 4)
        NS = 3

        def unit_no(g, a, u):
            return a * G * UNITS[0] + g * UNITS[a] + u

        def quad_no(g, a, q):
            return unit_no(g, a, 4 * q) // 4

        slots = {}
        for a in range(2):
            for g in range(G):
                for u in range(-4, UNITS[a]):
                    if a == 0 and u + 4 < UNITS[0]:
                        slots[g, a, "g", u + 4] = len(slots)
                    if u >= 0:
                        slots[g, a, u, 0] = len(slots)
                        slots[g, a, u, 1] = len(slots)
        unit_key = {unit_no(g, a, u): (g, a, u) for a in range(2) for g in range(G) for u in range(UNITS[a])}

        def exp_of(n):
            return slots[(*unit_key[n], 1)] + 1

        def bc(t, n):
            return t.rearrange("p (o e) -> p o e", o=1).to_broadcast([t.shape[0], n, t.shape[1]])

        def idle(n):
            for _ in range(n):
                yield

        def run(prepare, main, chain):
            weave(prepare(), chain[1](0))
            weave(main[1](0), chain[1](1))
            weave(main[1](1), chain[2](0))
            weave(main[2](0), chain[2](1), 2)
            weave(main[2](1), chain[3](0), 2)
            weave(main[3](0), chain[3](1))
            weave(main[3](1), chain[4](0), 2)
            weave(main[4](0), chain[4](1), 2)
            weave(main[4](1), chain[5](0))
            weave(main[5](0), chain[5](1), 2)
            weave(main[5](1), chain[6](0), 2)
            weave(main[6](0), chain[6](1))
            weave(main[6](1), idle(0))

        block_ = ctx.enter_context(nc.Block())

        @block_.sync
        def _(sp):
            def rows(t, g):
                return t[g * NB:(g + 1) * NB].rearrange("b s d -> s b d")

            sp.dma_start(hf[0][:].rearrange("p (b d) -> p b d", b=NB), rows(x_d, 0)).then_inc(d_x[0], 16)
            sp.dma_start(con[:], con_d).then_inc(d_con, 16)
            sp.dma_start(kvc[0][:], rows(ctx_d, 0)).then_inc(d_c[0], 16)
            sp.dma_start(shaped(stage[:, 0:NLIN], NLIN), lin_d).then_inc(d_lin, 16)
            sp.dma_start(r_fold, fold_d).then_inc(d_fold, 16)
            sp.dma_start(hf[1][:].rearrange("p (b d) -> p b d", b=NB), rows(x_d, 1)).then_inc(d_x[1], 16)
            sp.dma_start(kvc[1][:], rows(ctx_d, 1)).then_inc(d_c[1], 16)
            sp.dma_start(m8[:], mask_d).then_inc(d_m, 16)
            sp.dma_start(raw[:], raw_d).then_inc(d_raw, 16)
            for k in range(2 * CH):
                if k == 0:
                    sp.wait_ge(l_split, 1)
                if k == CH:
                    sp.wait_ge(bo_full, quad_no(1, 0, 3) + 1)
                    sp.dma_start(fb0[:, 0:NXAT], xat_d).then_inc(d_xat, 16)
                if k >= RING:
                    sp.wait_ge(w_split, k - RING + 1)
                src, n = (moe_d, NMOE // CH) if k < CH else (ret_d, NRET // CH)
                sp.dma_start(stage[:, k % RING * (NMOE // CH):k % RING * (NMOE // CH) + n],
                             src[:, k % CH * n:k % CH * n + n]).then_inc(d_ring[k % RING], 16)
            sp.wait_ge(w_split, 2 * CH)
            sp.dma_start(stage[:, 4 * T:4 * T + NFFN], ffn_d).then_inc(d_ffn, 16)
            for g in range(G):
                sp.wait_ge(fx_out, g + 1)
                sp.dma_start(rows(out_d, g), x_out[g]).then_inc(d_out, 16)
            sp.wait_ge(d_out, 16 * G)

        @block_.tensor
        def _(pe):
            mm, tr = nc.tensor.matmul, nc.tensor.transpose

            def mm3(out, w, m, start=True, stop=True):
                mm(out, w[0], m[0], start=start, stop=False)
                mm(out, w[1], m[0], start=False, stop=False)
                return mm(out, w[0], m[1], start=False, stop=stop)

            def spread_tokens(g, bank):
                for b in range(NB):
                    last = tr(bank[:, b * S:(b + 1) * S], rs_t[g][:, b:b + 1].to_broadcast([128, D]), ident)
                return last

            def norm(g, k, src, w=1):
                pe.wait_ge(ln_x[g], k + 1)
                mm(CHAIN[:], meanm if w == 1 else block_mean, src, start=True, stop=True).then_inc(ln_mean[g], 1)
                yield from idle(3)
                pe.wait_ge(ln_sq[g], k + 1)
                for b in range(NB):
                    last = mm(CHAIN[:, b * w:(b + 1) * w], four(sq[g][:])[:, b, :], meanm[:, 0:1] if w == 1 else head8,
                              start=True, stop=True)
                last.then_inc(ln_var[g], 1)
                yield from idle(4)
                if w == 1:
                    pe.wait_ge(ln_pow[g], k + 1)
                    spread_tokens(g, CHAIN).then_inc(ln_bc[g], 1)
                else:
                    pe.wait_ge(gn_ex[g], 1)
                    for b in range(NB):
                        last = tr(CHAIN[:, b * S:(b + 1) * S], four(sq[g][:])[:, b, :], ident)
                    last.then_inc(ln_bc[g], 1)
                yield

            def keys_out(g, n):
                for b in range(NB):
                    src = kvT[g][:, b, 0:S2] if n == S2 else kvT[g][:, b, S2:KEYS]
                    last = tr(CHAIN[0:n, b * D:(b + 1) * D], src, ident)
                last.then_inc(kc_full[g] if n == S2 else kl_full[g], 1)

            def chain1(g):
                pe.wait_ge(d_x[g], 16)
                if g == 0:
                    pe.wait_ge(d_con, 16)
                else:
                    pe.wait_ge(kc_ok[0], 1)
                for b in range(NB):
                    last = tr(CHAIN[:, b * S:(b + 1) * S], hf[g][:, b * D:(b + 1) * D], ident)
                last.then_inc(xt_full[g], 1)
                yield
                yield
                yield from norm(g, 0, xT[g][:])
                yield
                yield
                pe.wait_ge(cn_ok[g], 1)
                for b in range(NB):
                    last = tr(CHAIN[:, b * 128:b * 128 + S2], kvc[g][:, b, :], ident[0:S2, 0:S2])
                last.then_inc(ct_full[g], 1)
                yield
                yield
                pe.wait_ge(ckv_ok[g], 1)
                keys_out(g, S2)
                yield
                yield

            def chain2(g):
                yield
                if g == 0:
                    pe.wait_ge(kc_ok[1], 1)
                else:
                    pe.wait_ge(kl_ok[0], 1)
                yield from norm(g, 1, xT[g][:])
                yield
                pe.wait_ge(h_ok[g], 2)
                keys_out(g, S)
                yield
                yield

            def chain3(g):
                yield
                if g == 0:
                    pe.wait_ge(kl_ok[1], 1)
                yield from norm(g, 2, hf[g][:])
                yield
                yield from norm(g, 3, xT[g][:])
                yield
                pe.wait_ge(h_ok[g], 3)
                pe.wait_ge(w_split, CH)
                hb = four(h_hi[g][:]), four(h_lo[g][:])
                for b in range(NB):
                    last = mm3(CHAIN[:, b * E:(b + 1) * E], (hb[0][:, b], hb[1][:, b]), moe("wr"))
                last.then_inc(mo_log[g], 1)
                yield
                yield
                yield
                yield
                pe.wait_ge(mo_w[g], 1)
                for b in range(NB):
                    last = tr(CHAIN[0:3 * E, b * S:(b + 1) * S], wcat[g][:, b, :], ident)
                last.then_inc(mo_wt[g], 1)
                yield
                yield

            def chain4(g):
                yield
                yield from norm(g, 4, xT[g][:])
                yield

            def chain5(g):
                yield
                if g == 1:
                    pe.wait_ge(kl_ok[0], 2)
                yield from norm(g, 5, hf[g][:], w=16)
                yield
                yield from norm(g, 6, xT[g][:])
                yield
                pe.wait_ge(h_ok[g], 5)
                keys_out(g, S2)
                yield
                yield
                pe.wait_ge(kc_ok[g], 2)
                keys_out(g, S)
                yield
                yield

            def chain6(g):
                yield
                if g == 0:
                    pe.wait_ge(kl_ok[1], 2)
                yield from norm(g, 7, xT[g][:])
                yield

            def prepare():
                pe.wait_ge(d_fold, 16)
                for n in range((2 * LH0 + LH1) // 4):
                    if n >= 4:
                        pe.wait_ge(fold_out, n - 3)
                    a, b, h0 = (("qT", "kT", 0), ("vT", "o", LH0), ("vT1", "o1", 2 * LH0))[
                        0 if n < 4 else 1 if n < 8 else 2]
                    for j in range(4):
                        h = 8 * (n // 2) + n % 2 + 2 * j - h0
                        rows = slice(HD * (h % 2), HD * (h % 2) + HD)
                        ca, cb = FOLD[a] + h // 2 * D, FOLD[b] + h // 2 * D
                        last = mm(ps[n % 4][:, j * D:(j + 1) * D], r_fold[rows, ca:ca + D], r_fold[rows, cb:cb + D],
                                  start=True, stop=True)
                    last.then_inc(fold_full, 1)
                    yield

            def main1(g):
                pe.wait_ge(h_ok[g], 1)
                if g == 0:
                    pe.wait_ge(l_split, 1)
                    pe.wait_ge(fold_out, (2 * LH0 + LH1) // 4)
                hh = h_hi[g][:], h_lo[g][:]
                hb = four(hh[0]), four(hh[1])
                mm3(ps[0][:], lin("wq"), hh).then_inc(la_q, 1)
                yield
                for b in range(NB):
                    last = mm3(ps[1 + b // 2][:, 256 * (b % 2):256 * (b % 2) + 256], (hb[0][:, b], hb[1][:, b]),
                               lin("wkv"))
                    if b % 2:
                        last.then_inc(la_kv, 1)
                        yield
                yield
                yield
                pe.wait_ge(la_kf, g + 1)
                for b in range(NB):
                    last = mm(ps[3 + b // 2][:, (D + 1) * (b % 2):(D + 1) * (b % 2) + D + 1], k_f[:, b, :],
                              v_1[:, b, :], start=True, stop=True)
                last.then_inc(la_sum, 1)
                yield
                yield
                pe.wait_ge(la_mask, g + 1)
                pe.wait_ge(la_qf, g + 1)
                w = D + 16
                for b in range(NB):
                    last = mm(ps[1 + b // 2][:, w * (b % 2):w * (b % 2) + w], four(q_f)[:, b, :], kv_b[:, b, :],
                              start=True, stop=True)
                last.then_inc(la_nd, 1)
                yield
                yield
                pe.wait_ge(la_o, 2 * g + 1)
                for b in range(NB):
                    last = tr(ps[3][:, b * S:(b + 1) * S], o_t[:, b, :], ident)
                last.then_inc(la_ot, 1)
                yield
                yield
                pe.wait_ge(la_o, 2 * g + 2)
                if g == 0:
                    pe.wait_ge(d_raw, 16)
                else:
                    pe.wait_ge(ln_x[0], 2)
                mm(OUT[:], r_("woT"), o_n, start=True, stop=True).then_inc(la_y, 1)
                yield

            def attention(g, a):
                units, fb = UNITS[a], (fb0, fb1)[a]

                def slot(key):
                    r = slots[key]
                    if r >= NS:
                        pe.wait_ge(s_free, r - NS + 1)
                    return ps[r % NS]

                def q_fold(n):
                    w = fa_hi[:, n * D:(n + 1) * D], fa_lo[:, n * D:(n + 1) * D]
                    mm3(slot((g, 0, "g", n))[:], w, (h_hi[g][:], h_lo[g][:])).then_inc(s_full, 1)

                def scores(u):
                    q, b = u // 4, u % 4
                    if b == 0 and a == 0:
                        pe.wait_ge(s_free, slots[g, 0, "g", 4 * q + 3] + 1)
                    for s in range(2):
                        bank = slot((g, a, u, s))
                        for j in range(2):
                            out = bank[:, j * KEYS:(j + 1) * KEYS]
                            if a == 0:
                                mm(out[:, 0:S2], ones[:], mrow[:, g * NB + b, :], start=True, stop=False,
                                   skip_group_check=True)
                                last = mm(out, four(g_s[q % 2][:, 2 * s + j, :])[:, b, :], kvT[g][:, b, :], start=False,
                                          stop=True, skip_group_check=True)
                            else:
                                rows, p = slice(HD * s, HD * s + HD), (4 * q + s + 2 * j) // 2
                                last = mm(out, four(xq_s[:, p, :])[rows, b, :], xk_s[rows, p, b, :], start=True,
                                          stop=True)
                        last.then_inc(s_full, 1)

                def turn(u):
                    n = unit_no(g, a, u)
                    pe.wait_ge(n_done, n + 1)
                    if n:
                        pe.wait_ge(pc_done, n)
                        pe.wait_ge(pl_done, n)
                    for h in range(4):
                        tr(ps[3][0:S2, h * S:(h + 1) * S], P[n % 3][:, h, 0:S2], ident)
                        last = tr(ps[4][:, h * S:(h + 1) * S], P[n % 3][:, h, S2:KEYS], ident)
                    last.then_inc(t_full, 1)

                def weigh(u):
                    n, b = unit_no(g, a, u), u % 4
                    pe.wait_ge(pc_done, n + 1)
                    pe.wait_ge(pl_done, n + 1)
                    if n:
                        pe.wait_ge(ue_done, n)
                    mm(ps[5][:], kvc[g][:, b, :], ptc[n % 2][0:S2, :], start=True, stop=False)
                    mm(ps[5][:], kvl[g][:, b, :], ptl[n % 2], start=False, stop=True).then_inc(u_full, 1)

                def project(q):
                    pe.wait_ge(ue_done, unit_no(g, a, 4 * q + 3) + 1)
                    if q == 0 and g == 1:
                        pe.wait_ge(ln_x[0], (3, 8)[a])
                    for j in range(4):
                        h = 4 * q + (j if a == 0 else (0, 2, 1, 3)[j])
                        last = mm(OUT[:], fb[:, h * D:(h + 1) * D], us[:, j].rearrange("p b s -> p (b s)"),
                                  start=(q == 0 and j == 0), stop=(q == units // 4 - 1 and j == 3))
                    last.then_inc(bo_full, 1)

                if a == 0:
                    for n in range(4):
                        q_fold(n)
                        yield
                for i in range(units + 4):
                    if a == 0 and i + 4 < units:
                        q_fold(i + 4)
                    if i < units:
                        scores(i)
                    yield
                    if 2 <= i < units + 2:
                        turn(i - 2)
                    yield
                    if 3 <= i < units + 3:
                        if i == 3:
                            pe.wait_ge(kc_ok[g], a + 1)
                            pe.wait_ge(kl_ok[g], a + 1)
                        weigh(i - 3)
                    if i >= 4 and (i - 4) % 4 == 3:
                        project((i - 4) // 4)
                    yield

            def main2(g):
                pe.wait_ge(h_ok[g], 2)
                if g == 0:
                    pe.wait_ge(m_ok, 1)
                yield from attention(g, 0)

            def main3(g):
                hh = h_hi[g][:], h_lo[g][:]
                n0 = g * (PAIRS + 1)

                def hidden(i):
                    n = n0 + i
                    if n >= 2:
                        pe.wait_ge(mo_si, n - 1)
                        pe.wait_ge(mo_tu, n - 1)
                    m = 128 if i < PAIRS else EI
                    wg = moe("wg", i * 128, 128) if i < PAIRS else moe("wg_s")
                    wu = moe("wu", i * 128, 128) if i < PAIRS else moe("wu_s")
                    mm3(ps[n % 2][0:m, :], wg, hh)
                    mm3(ps[2 + n % 2][0:m, :], wu, hh).then_inc(mo_gu, 1)

                def spread(i):
                    n = g * PAIRS + i
                    if i == 0:
                        pe.wait_ge(mo_w3[g], 1)
                        if g == 0:
                            pe.wait_ge(d_sel, 16)
                    if n >= 2:
                        pe.wait_ge(mo_a, n - 1)
                    mm(ps[4 + i % 2][:], sel[:, i * 128:(i + 1) * 128], w3b[g], start=True, stop=True)\
                        .then_inc(mo_wb, 1)

                def down(i):
                    if i < PAIRS:
                        pe.wait_ge(mo_a, g * PAIRS + i + 1)
                    else:
                        pe.wait_ge(mo_tu, n0 + i + 1)
                    if i == 0:
                        if g == 1:
                            pe.wait_ge(ln_x[0], 5)
                        mm(OUT[:], r_("bd3")[0:96, :], w3f[g], start=True, stop=False)
                    m = 128 if i < PAIRS else EI
                    w = r_("wd", i * D, D) if i < PAIRS else r_("wd_s")[0:EI, :]
                    mm(OUT[:], w, av[(n0 + i) % 3][0:m, :], start=False, stop=(i == PAIRS)).then_inc(mo_dn, 1)

                pe.wait_ge(h_ok[g], 3)
                if g == 0:
                    pe.wait_ge(u_full, unit_no(1, 0, UNITS[0] - 1) + 1)
                hidden(0)
                hidden(1)
                for i in range(PAIRS + 3):
                    if 2 <= i <= PAIRS:
                        hidden(i)
                    yield
                    if i < PAIRS:
                        spread(i)
                    if i >= 2:
                        down(i - 2)
                    yield

            def main4(g):
                pe.wait_ge(h_ok[g], 4)
                pe.wait_ge(w_split, 2 * CH)
                if g == 0:
                    pe.wait_ge(tern_sum, 1)
                    mm(ps[5][:, 0:2], meanm, wabs, start=True, stop=True).then_inc(tern_all, 1)
                hh = h_hi[g][:], h_lo[g][:]
                hb = four(hh[0]), four(hh[1])
                for n in range(2 * NB):
                    b, half = n // 2, n % 2
                    if n >= 4:
                        pe.wait_ge(re_vs, g * 2 * NB + n - 3)
                    mm3(ps[n % 4][:], (hb[0][:, b], hb[1][:, b]), ret("rv", half * 512, 512)).then_inc(re_v, 1)
                    yield

                def project(i):
                    n = g * RH + i
                    p, k = i // 2, "qk"[i % 2]
                    if i == 0:
                        pe.wait_ge(re_vs, (g + 1) * 2 * NB)
                    else:
                        pe.wait_ge(re_t, 2 * n)
                        pe.wait_ge(re_pas, n)
                    mm3(ps[i % 2][:], ret(f"r{k}_rot", p * 128, 128), hh)
                    mm3(ps[2][:], ret(f"r{k}_swp", p * 128, 128), hh)
                    mm3(ps[3][:], ret(f"r{k}_pas", p * 128, 128), hh).then_inc(re_p, 1)

                def decay(p, h):
                    n = g * RH + 2 * p + h
                    if h == 0:
                        pe.wait_ge(re_s, g * RH + 2 * p + 2)
                        pe.wait_ge(re_pas, g * RH + 2 * p + 2)
                    if n >= 2:
                        pe.wait_ge(re_as, n - 1)
                    if n < 2:
                        pe.wait_ge(tern_ok, 1)
                    t, rows = r_qk[p % 2], slice(64 * h, 64 * h + 64)
                    for b in range(NB):
                        o = ps[4 + h][:, b * S:(b + 1) * S]
                        mm(o, four(t[:, 0])[rows, b], four(t[:, 2])[rows, b], start=True, stop=False)
                        last = mm(o, four(t[:, 1])[rows, b], four(t[:, 3])[rows, b], start=False, stop=True)
                    last.then_inc(re_a, 1)

                def mix(p, h):
                    n = g * RH + 2 * p + h
                    pe.wait_ge(re_as, n + 1)
                    if n == RH:
                        pe.wait_ge(ln_x[0], 6)
                    for b in range(NB):
                        c = (2 * p + h) * D
                        last = mm(OUT[:, b * S:(b + 1) * S], r_v[:, b, c:c + D], r_a[n % 2][:, b, :],
                                  start=(p == 0 and h == 0 and b == 0), stop=(p == RH // 2 - 1 and h == 1),
                                  skip_group_check=True)
                    last.then_inc(re_o, 1)

                for i in range(2):
                    project(i)
                    yield
                for p in range(RH // 2):
                    for i in range(2):
                        if p + 1 < RH // 2:
                            project(2 * p + 2 + i)
                        yield
                    for h in range(2):
                        decay(p, h)
                        yield
                    for h in range(2):
                        mix(p, h)
                        yield

            def main5(g):
                pe.wait_ge(h_ok[g], 5)
                if g == 0:
                    pe.wait_ge(d_xat, 16)
                else:
                    pe.wait_ge(s_free, exp_of(unit_no(1, 1, 0) - 1))
                for r in range(16):
                    if 3 <= r < 7:
                        pe.wait_ge(xa_q, 4 * g + r - 2)
                    elif 7 <= r < 15:
                        pe.wait_ge(xa_kx, 8 * g + r - 6)
                    elif r == 15:
                        pe.wait_ge(xa_kl, 4 * g + 1)
                    bank = ps[r % 3]
                    if r < 4:
                        last = mm(bank[:], x_("xq", r * 128, 128), kvT[g][:, :, S2:KEYS], start=True, stop=True)
                    elif r < 12:
                        p, name = (r - 4) // 2, ("xk", "xks")[r % 2]
                        last = mm(bank[:, 0:NB * S2], x_(name, p * 128, 128), kvT[g][:, :, 0:S2], start=True, stop=True)
                    else:
                        last = mm(bank[:], x_("xk", (r - 12) * 128, 128), kvT[g][:, :, S2:KEYS], start=True, stop=True)
                    last.then_inc(xa_full, 1)
                    yield
                pe.wait_ge(xa_kl, 4 * (g + 1))
                pe.wait_ge(xa_kt, 4 * (g + 1))
                yield from attention(g, 1)

            def main6(g):
                pe.wait_ge(h_ok[g], 6)
                for j in range(4):
                    if g:
                        pe.wait_ge(ff_g, j + 1)
                    mm(ps[j][:], f_("up", j * 128, 128), hf[g][:], start=True, stop=True).then_inc(ff_up, 1)
                    yield
                for j in range(4):
                    pe.wait_ge(ff_g, 4 * g + j + 1)
                    if g and j == 0:
                        pe.wait_ge(f_y, 1)
                    last = mm(OUT[:], f_("down", j * 128, 128), f_g[:, j, :], start=(j == 0), stop=(j == 3))
                    yield
                last.then_inc(ff_dn, 1)
                pe.wait_ge(ff_sq, 4 * g + 4)
                if g:
                    pe.wait_ge(fx_out, 1)
                for b in range(NB):
                    for j in range(4):
                        last = mm(ps[4][:, b:b + 1], four(f_sq[:, j, :])[:, b, :], meanm[:, 0:1], start=(j == 0),
                                  stop=(j == 3))
                last.then_inc(ff_ms, 1)
                yield
                pe.wait_ge(f_rs, g + 1)
                spread_tokens(g, ps[5]).then_inc(f_bc, 1)
                yield
                pe.wait_ge(fx_ok, g + 1)
                for b in range(NB):
                    last = tr(ps[4][:, b * D:(b + 1) * D], four(xT[g][:])[:, b, :], ident)
                last.then_inc(fx_t, 1)
                yield

            run(prepare, [None, main1, main2, main3, main4, main5, main6],
                [None, chain1, chain2, chain3, chain4, chain5, chain6])

        @block_.vector
        def _(dve):
            V = nc.vector
            count = [0]

            def link(ins):
                count[0] += 1
                ins.then_inc(v_link, 1)
                dve.wait_ge(v_link, count[0])

            def centre(g, k, src, eps=EPS, w=1):
                yield
                dve.wait_ge(ln_mean[g], k + 1)
                V.tensor_tensor(xc[g][:], src, CHAIN[:], ALU.subtract).then_inc(ln_xc[g], 1)
                yield from idle(3)
                dve.wait_ge(ln_var[g], k + 1)
                V.tensor_scalar(ve[g][:, 0:NB * w], CHAIN[:, 0:NB * w], eps, None, ALU.add).then_inc(ln_ve[g], 1)
                yield from idle(2)
                if w > 1:
                    dve.wait_ge(ln_pow[g], k + 1)
                    V.tensor_copy(sq[g][:].rearrange("p (k e) -> p k e", e=D // w),
                                  rs_t[g][:, 0:NB * w].rearrange("p (k o) -> p k o", o=1).to_broadcast(
                                      [128, NB * w, D // w])).then_inc(gn_ex[g], 1)
                yield from idle(2)
                dve.wait_ge(ln_bc[g], k + 1)

            def parts(g):
                link(V.tensor_copy(h_hi[g][:], hf[g][:]))
                V.tensor_tensor(h_lo[g][:], hf[g][:], h_hi[g][:].bitcast(F32), ALU.subtract).then_inc(h_ok[g], 1)

            def plain_norm(g, k):
                yield from centre(g, k, xT[g][:])
                link(V.tensor_tensor(hf[g][:], xc[g][:], CHAIN[:], ALU.mult))
                parts(g)
                yield

            def twice_norm(g, k, gk, shift):
                yield from centre(g, k, xT[g][:], eps=EPS * EPS / (1 + EPS))
                link(V.scalar_tensor_tensor(out=hf[g][:], in0=xc[g][:], scalar=gk, in1=CHAIN[:], op0=ALU.mult,
                                            op1=ALU.mult))
                link(V.tensor_scalar(hf[g][:], hf[g][:], shift, None, ALU.add))
                V.tensor_copy(kvT[g][:, :, S2:KEYS], four(hf[g][:]))
                parts(g)
                yield

            def scaled_residual(g, scale, shift):
                link(V.scalar_tensor_tensor(out=hf[g][:], in0=xc[g][:], scalar=scale, in1=CHAIN[:], op0=ALU.mult,
                                            op1=ALU.mult))
                V.scalar_tensor_tensor(out=xT[g][:], in0=hf[g][:], scalar=shift, in1=xT[g][:], op0=ALU.add,
                                       op1=ALU.add).then_inc(ln_x[g], 1)

            def context_keys(g, a):
                V.tensor_scalar(kvT[g][:, :, 0:S2], cT[g][:], v_(f"g_x{a}"), v_(f"b_x{a}"), ALU.mult, ALU.add)\
                    .then_inc(ckv_ok[g], 1)

            def chain1(g):
                yield
                dve.wait_ge(xt_full[g], 1)
                V.tensor_copy(xT[g][:], CHAIN[:]).then_inc(ln_x[g], 1)
                yield
                dve.wait_ge(d_c[g], 16)
                for b in range(NB):
                    last = V.bn_stats(bnst[g][:, 6 * b:6 * b + 6], kvc[g][:, b, :])
                link(last)
                for b in range(NB):
                    last = V.bn_aggr(bnag[g][:, 2 * b:2 * b + 2], bnst[g][:, 6 * b:6 * b + 6])
                link(last)
                V.tensor_scalar(crs[g], bnag[g].rearrange("p (b k) -> p k b", k=2)[:, 1, :], EPS, None,
                                ALU.add).then_inc(c_ve[g], 1)
                yield from plain_norm(g, 0)
                dve.wait_ge(c_pow[g], 1)
                for b in range(NB):
                    last = V.tensor_scalar(kvc[g][:, b, :], kvc[g][:, b, :], bnag[g][:, 2 * b:2 * b + 1],
                                           crs[g][:, b:b + 1], ALU.subtract, ALU.mult)
                last.then_inc(cn_ok[g], 1)
                yield
                yield
                dve.wait_ge(ct_full[g], 1)
                link(V.tensor_copy(cT[g][:], CHAIN[:].rearrange("p (b k) -> p b k", b=NB)[:, :, 0:S2]))
                context_keys(g, 0)
                yield
                yield
                yield

            def chain2(g):
                dve.wait_ge(la_y, g + 1)
                V.scalar_tensor_tensor(out=xT[g][:], in0=OUT[:], scalar=v_("bo"), in1=xT[g][:], op0=ALU.add,
                                       op1=ALU.add).then_inc(ln_x[g], 1)
                yield
                yield from twice_norm(g, 1, gk0, v_("b_l0"))
                yield
                yield

            def chain3(g):
                dve.wait_ge(bo_full, quad_no(g, 0, LH0 // 4 - 1) + 1)
                V.tensor_copy(hf[g][:], OUT[:]).then_inc(ln_x[g], 1)
                yield
                yield from centre(g, 2, hf[g][:])
                scaled_residual(g, v_("g_o0"), v_("b_o0"))
                yield
                yield from plain_norm(g, 3)
                yield
                dve.wait_ge(mo_log[g], 1)
                V.tensor_tensor(lg[g], CHAIN[:, 0:NB * E].rearrange("p (b e) -> p b e", b=NB), bc(c_("br"), NB),
                                ALU.add).then_inc(mo_lg[g], 1)
                yield
                yield
                dve.wait_ge(mo_sig[g], 1)
                for b in range(NB):
                    last = V.max(top[g][:, 8 * b:8 * b + 8], aff[g][:, b, :])
                link(last)
                for b in range(NB):
                    V.match_replace(rep[g][:, b, :], top[g][:, 8 * b:8 * b + 8], aff[g][:, b, :], 0.0)
                link(V.tensor_reduce(tsum[g], top[g].rearrange("p (b k) -> p b k", b=NB), AX_X, ALU.add))
                link(V.tensor_scalar(tsum[g], tsum[g], 1e-9, None, ALU.add))
                V.tensor_tensor(wn[g], aff[g], rep[g], ALU.subtract)
                link(V.reciprocal(tsum[g], tsum[g]))
                link(V.tensor_tensor(wn[g], wn[g], tsum[g].rearrange("p (b o) -> p b o", o=1).to_broadcast([128, NB, E]),
                                     ALU.mult))
                for k in range(3):
                    link(V.tensor_copy(wpart[:], wn[g]))
                    last = V.tensor_copy(wcat[g][:, :, k * E:(k + 1) * E], wpart[:])
                    if k < 2:
                        link(V.tensor_tensor(wn[g], wn[g], wpart[:], ALU.subtract))
                last.then_inc(mo_w[g], 1)
                yield
                yield
                dve.wait_ge(mo_wt[g], 1)
                link(V.tensor_copy(w3f[g], CHAIN[0:96, :]))
                V.tensor_copy(w3b[g], w3f[g]).then_inc(mo_w3[g], 1)
                yield

            def chain4(g):
                dve.wait_ge(mo_dn, (g + 1) * (PAIRS + 1))
                V.scalar_tensor_tensor(out=xT[g][:], in0=OUT[:], scalar=v_("bd_s"), in1=xT[g][:], op0=ALU.add,
                                       op1=ALU.add).then_inc(ln_x[g], 1)
                yield
                yield from plain_norm(g, 4)

            def chain5(g):
                dve.wait_ge(re_o, (g + 1) * RH)
                V.tensor_copy(hf[g][:], OUT[:]).then_inc(ln_x[g], 1)
                context_keys(g, 1)
                yield
                yield from centre(g, 5, hf[g][:], w=16)
                scaled_residual(g, v_("gnw"), v_("gnb"))
                yield
                yield from twice_norm(g, 6, gk1, v_("b_l1"))
                yield
                yield
                yield

            def chain6(g):
                dve.wait_ge(bo_full, quad_no(g, 1, LH1 // 4 - 1) + 1)
                V.tensor_tensor(xT[g][:], OUT[:], xT[g][:], ALU.add).then_inc(ln_x[g], 1)
                yield
                yield
                dve.wait_ge(ln_mean[g], 8)
                V.tensor_tensor(xc[g][:], xT[g][:], CHAIN[:], ALU.subtract).then_inc(ln_xc[g], 1)
                yield from idle(3)
                dve.wait_ge(ln_var[g], 8)
                V.tensor_copy(ve[g][:, 0:NB], CHAIN[:, 0:NB])
                V.tensor_scalar(ve[g][:, NB:2 * NB], CHAIN[:, 0:NB], EPS, None, ALU.add).then_inc(ln_ve[g], 1)
                yield from idle(2)
                dve.wait_ge(f_root, g + 1)
                link(V.scalar_tensor_tensor(out=rs_t[g][:, 0:NB], in0=rs_t[g][:, NB:2 * NB], scalar=1e-8,
                                            in1=rs_t[g][:, 0:NB], op0=ALU.mult, op1=ALU.add))
                V.reciprocal(rs_t[g][:, 0:NB], rs_t[g][:, 0:NB]).then_inc(ln_pow[g], 1)
                yield from idle(2)
                dve.wait_ge(ln_bc[g], 8)
                V.tensor_tensor(hf[g][:], xc[g][:], CHAIN[:], ALU.mult).then_inc(h_ok[g], 1)
                yield

            def prepare():
                V.memset(half_n, -0.5)
                V.memset(half_p, 0.5).then_inc(half_ok, 1)
                V.memset(ones[:], 1.0)
                link(V.memset(mrow[:], 0.0))
                dve.wait_ge(d_con, 16)
                V.tensor_scalar(bq1, v_("bq"), 1.0, None, ALU.add)
                V.tensor_scalar(gk0, v_("g_l0"), (1 + EPS) ** -0.5, None, ALU.mult)
                V.tensor_scalar(gk1, v_("g_l1"), (1 + EPS) ** -0.5, None, ALU.mult)
                V.tensor_scalar(block_mean, block, 0.125, None, ALU.mult)
                link(V.tensor_scalar(head8, c_("head"), 0.125, None, ALU.mult))
                yield
                dve.wait_ge(d_lin, 16)
                hi, lo = wa[:, 2 * QF:2 * QF + NLIN], wa[:, 2 * QF + NLIN:2 * QF + 2 * NLIN]
                link(V.tensor_copy(hi, stage[:, 0:NLIN]))
                V.tensor_tensor(lo, stage[:, 0:NLIN], hi.bitcast(F32), ALU.subtract).then_inc(l_split, 1)
                for n in range((2 * LH0 + LH1) // 4):
                    def heads(t):
                        c = n // 2 % 2 * 1024
                        return t[:, c:c + 1024].rearrange("p (j two d) -> p two j d", two=2, d=D)[:, n % 2]
                    bank = ps[n % 4][:].rearrange("p (j d) -> p j d", d=D)
                    dve.wait_ge(fold_full, n + 1)
                    if n < 4:
                        link(V.tensor_scalar(heads(fa_hi), bank, HD ** -0.5, None, ALU.mult))
                        V.scalar_tensor_tensor(out=heads(fa_lo), in0=bank, scalar=HD ** -0.5,
                                               in1=heads(fa_hi).bitcast(F32), op0=ALU.mult, op1=ALU.subtract)\
                            .then_inc(fold_out, 1)
                    else:
                        V.tensor_copy(heads(fb0 if n < 8 else fb1), bank).then_inc(fold_out, 1)
                    if n < 9:
                        yield
                dve.wait_ge(d_m, 16)
                V.tensor_scalar(mrow[0:1], shaped(m8[:], B, S2), -MASKED, MASKED, ALU.mult, ALU.add).then_inc(m_ok, 1)

            def main1(g):
                if g:
                    dve.wait_ge(la_y, 1)
                if g == 0:
                    V.memset(v_1[:, :, D:D + 1], 1.0)
                dve.wait_ge(la_q, g + 1)
                V.tensor_scalar(q_m, ps[0][:], v_("bq"), 0.0, ALU.add, ALU.min).then_inc(la_min, 1)
                yield
                bkv = c_("bkv")
                for i in range(2):
                    dve.wait_ge(la_kv, 2 * g + i + 1)
                    pv = ps[1 + i][:].rearrange("p (b k e) -> p k b e", b=2, k=2)
                    V.tensor_tensor(k_z[:, 2 * i:2 * i + 2, :], pv[:, 0], bc(bkv[:, 0:D], 2), ALU.add)
                    last = V.tensor_tensor(v_1[:, 2 * i:2 * i + 2, 0:D], pv[:, 1], bc(bkv[:, D:2 * D], 2), ALU.add)
                    if i:
                        link(last)
                    yield
                V.tensor_scalar(k_m, k_z, 0.0, None, ALU.min).then_inc(la_min, 1)
                dve.wait_ge(la_exp, 2 * g + 1)
                link(V.tensor_scalar(q_e, q_e, -1.0, 1.0, ALU.add, ALU.add))
                V.scalar_tensor_tensor(out=q_f, in0=ps[0][:], scalar=bq1, in1=q_e, op0=ALU.add, op1=ALU.max)\
                    .then_inc(la_qf, 1)
                yield
                dve.wait_ge(la_exp, 2 * g + 2)
                link(V.tensor_scalar(k_e, k_e, -1.0, 1.0, ALU.add, ALU.add))
                V.scalar_tensor_tensor(out=k_f, in0=k_z, scalar=1.0, in1=k_e, op0=ALU.add, op1=ALU.max)\
                    .then_inc(la_kf, 1)
                yield
                yield
                dve.wait_ge(la_sum, g + 1)
                for i in range(2):
                    pv = ps[3 + i][:, 0:2 * (D + 1)].rearrange("p (b e) -> p b e", b=2)
                    V.tensor_tensor(kv_b[:, 2 * i:2 * i + 2, 0:D], pv[:, :, 0:D], bc(block, 2), ALU.mult)
                    for j in range(2):
                        last = V.tensor_scalar(kv_b[:, 2 * i + j, D:D + 16], c_("head"), pv[:, j, D:D + 1], None,
                                               ALU.mult)
                last.then_inc(la_mask, 1)
                yield
                yield
                dve.wait_ge(la_nd, g + 1)
                nd = [ps[1 + i][:, 0:2 * (D + 16)].rearrange("p (b e) -> p b e", b=2) for i in range(2)]
                ld = lden[g].rearrange("p (b h) -> p b h", b=NB)
                for i in range(2):
                    last = V.tensor_scalar(ld[:, 2 * i:2 * i + 2, :], nd[i][:, :, D:D + 16], 1e-6, None, ALU.add)
                link(last)
                link(V.reciprocal(lden[g], lden[g]))
                for b in range(NB):
                    last = V.tensor_tensor(
                        o_t[:, b, :].rearrange("p (h e) -> p h e", h=16),
                        nd[b // 2][:, b % 2, 0:D].rearrange("p (h e) -> p h e", h=16),
                        ld[:, b, :].rearrange("p (h o) -> p h o", o=1).to_broadcast([128, 16, 8]), ALU.mult)
                last.then_inc(la_o, 1)
                yield
                yield
                dve.wait_ge(la_ot, g + 1)
                V.tensor_copy(o_n, ps[3][:]).then_inc(la_o, 1)
                yield
                yield

            def attention(g, a):
                units = UNITS[a]

                def top_(u):
                    n = unit_no(g, a, u)
                    for s in range(2):
                        r = slots[g, a, u, s]
                        dve.wait_ge(s_full, r + 1)
                        if n >= 3 and s == 0:
                            dve.wait_ge(s_free, exp_of(n - 3))
                        o = 4 * (n % 3) + 2 * s
                        V.tensor_reduce(nm[:, o:o + 2], ps[r % NS][:, 0:2 * KEYS].rearrange("p (h k) -> p h k", h=2),
                                        AX_X, ALU.max, negate=True).then_inc(m_done, 1)

                def recip(u):
                    n = unit_no(g, a, u)
                    o = 4 * (n % 3)
                    dve.wait_ge(s_free, exp_of(n))
                    if n >= 3:
                        dve.wait_ge(n_done, n - 2)
                    V.reciprocal(rs[:, o:o + 4], sm[:, o:o + 4]).then_inc(r_done, 1)

                def turned(u):
                    n = unit_no(g, a, u)
                    dve.wait_ge(t_full, n + 1)
                    if n >= 2:
                        dve.wait_ge(u_full, n - 1)
                    V.tensor_copy(ptl[n % 2], ps[4][:]).then_inc(pl_done, 1)

                def weighed(u):
                    n = unit_no(g, a, u)
                    q, b = u // 4, u % 4
                    dve.wait_ge(u_full, n + 1)
                    if b == 0 and quad_no(g, a, q) >= 1:
                        dve.wait_ge(bo_full, quad_no(g, a, q))
                    V.tensor_copy(us[:, :, b, :], four(ps[5][:])).then_inc(ue_done, 1)

                if a == 0:
                    yield from idle(4)
                for i in range(units + 4):
                    if i < units:
                        top_(i)
                    if 1 <= i <= units:
                        recip(i - 1)
                    yield
                    if 2 <= i < units + 2:
                        turned(i - 2)
                    yield
                    if 3 <= i < units + 3:
                        weighed(i - 3)
                    yield

            def main2(g):
                yield from attention(g, 0)

            def main3(g):
                n0 = g * (PAIRS + 1)
                for i in range(PAIRS + 3):
                    if i > PAIRS:
                        yield
                        yield
                        continue
                    n = n0 + i
                    m = 128 if i < PAIRS else EI
                    bu = v_("bu", i) if i < PAIRS else v_("bu_s")
                    dve.wait_ge(mo_si, n + 1)
                    dst = tu[n % 2] if i < PAIRS else av[n % 3]
                    if i == PAIRS:
                        dve.wait_ge(mo_dn, n - 2)
                    ins = V.scalar_tensor_tensor(out=dst[0:m, :], in0=ps[2 + n % 2][0:m, :], scalar=bu[0:m, :],
                                                 in1=si[n % 2][0:m, :], op0=ALU.add, op1=ALU.mult)
                    ins.then_inc(mo_tu, 1)
                    yield
                    if i < PAIRS:
                        dve.wait_ge(mo_tu, n + 1)
                        dve.wait_ge(mo_wb, g * PAIRS + i + 1)
                        if n >= 3:
                            dve.wait_ge(mo_dn, n - 2)
                        V.tensor_tensor(av[n % 3], tu[n % 2], ps[4 + i % 2][:], ALU.mult).then_inc(mo_a, 1)
                    yield

            def main4(g):
                cos, sin = c_("cosA"), c_("sinA")

                def rotate(i):
                    n = g * RH + i
                    dve.wait_ge(re_p, n + 1)
                    if n >= 2:
                        dve.wait_ge(re_s, n - 1)
                    V.tensor_tensor(four(r_t1[n % 2]), four(ps[i % 2][:]), bc(cos, NB), ALU.mult).then_inc(re_t, 1)
                    V.tensor_tensor(four(r_t2[n % 2]), four(ps[2][:]), bc(sin, NB), ALU.mult).then_inc(re_t, 1)

                def decayed(p, h):
                    n = g * RH + 2 * p + h
                    dve.wait_ge(re_a, n + 1)
                    if n >= 2:
                        dve.wait_ge(re_o, n - 1)
                    V.tensor_tensor(r_a[n % 2], four(ps[4 + h][:]), bc(c_("decay"), 4), ALU.mult).then_inc(re_as, 1)

                if g == 0:
                    dve.wait_ge(d_ffn, 16)
                    V.tensor_reduce(wabs[:, 0:1], f_("up"), AX_X, ALU.add, apply_absolute_value=True)
                    V.tensor_reduce(wabs[:, 1:2], f_("down"), AX_X, ALU.add, apply_absolute_value=True)\
                        .then_inc(tern_sum, 1)
                    dve.wait_ge(tern_all, 1)
                    V.tensor_scalar(thr, ps[5][:, 0:2], 0.5 / DFF, None, ALU.mult)
                    link(V.tensor_scalar(thr_n, ps[5][:, 0:2], -0.5 / DFF, None, ALU.mult))
                    t1, t2 = stage[:, 0:DFF], stage[:, DFF:2 * DFF]
                    for k, name in enumerate(("up", "down")):
                        w = f_(name)
                        V.tensor_scalar(t1, w, thr[:, k:k + 1], None, ALU.is_gt)
                        link(V.tensor_scalar(t2, w, thr_n[:, k:k + 1], None, ALU.is_lt))
                        link(V.tensor_tensor(t1, t1, t2, ALU.subtract))
                        link(V.tensor_tensor(t1, t1, w, ALU.subtract))
                        last = V.tensor_tensor(w, t1, w, ALU.add)
                        if k == 0:
                            link(last)
                    last.then_inc(tern_ok, 1)
                yield from idle(2 * NB)
                for i in range(2):
                    rotate(i)
                    yield
                for p in range(RH // 2):
                    for i in range(2):
                        if p + 1 < RH // 2:
                            rotate(2 * p + 2 + i)
                        yield
                    for h in range(2):
                        decayed(p, h)
                        yield
                    yield
                    yield

            def main5(g):
                cos, sin = c_("cosX"), c_("sinX")
                yield from idle(4)
                for p in range(4):
                    for k, (o, f) in enumerate(((xt1, cos), (xt2, sin))):
                        r = 4 + 2 * p + k
                        dve.wait_ge(xa_full, 16 * g + r + 1)
                        if p:
                            dve.wait_ge(xa_kt, 4 * g + p)
                        V.tensor_tensor(o[:, :, 0:S2], ps[r % 3][:, 0:NB * S2].rearrange("p (b k) -> p b k", b=NB),
                                        bc(f, NB), ALU.mult).then_inc(xa_kx, 1)
                        yield
                yield from idle(4)
                yield from attention(g, 1)

            def main6(g):
                yield from idle(8)
                dve.wait_ge(ff_ms, g + 1)
                V.tensor_scalar(ve[g][:, 0:NB], ps[4][:, 0:NB], 128.0 / DFF, None, ALU.mult).then_inc(f_ve, 1)
                dve.wait_ge(f_pow, g + 1)
                link(V.tensor_scalar(rs_t[g][:, 0:NB], rs_t[g][:, 0:NB], 1e-8, None, ALU.add))
                V.reciprocal(rs_t[g][:, 0:NB], rs_t[g][:, 0:NB]).then_inc(f_rs, 1)
                dve.wait_ge(ff_dn, g + 1)
                V.tensor_copy(hf[g][:], OUT[:]).then_inc(f_y, 1)
                yield
                dve.wait_ge(f_y, g + 1)
                dve.wait_ge(f_bc, g + 1)
                link(V.tensor_tensor(hf[g][:], hf[g][:], ps[5][:], ALU.mult))
                V.tensor_tensor(xT[g][:], xT[g][:], hf[g][:], ALU.add).then_inc(fx_ok, 1)
                yield
                dve.wait_ge(fx_t, g + 1)
                V.tensor_copy(x_out[g], four(ps[4][:])).then_inc(fx_out, 1)
                yield

            run(prepare, [None, main1, main2, main3, main4, main5, main6],
                [None, chain1, chain2, chain3, chain4, chain5, chain6])

        @block_.scalar
        def _(act):
            A = nc.scalar.activation

            def squares(g, k):
                yield
                yield
                act.wait_ge(ln_xc[g], k + 1)
                A(sq[g][:], xc[g][:], ACT.Square).then_inc(ln_sq[g], 1)
                yield from idle(6)

            def keys(g, k, n):
                if n == S2:
                    act.wait_ge(kc_full[g], k)
                    A(kvc[g][:], CHAIN[0:S2, :].rearrange("p (b d) -> p b d", b=NB), ACT.Copy).then_inc(kc_ok[g], 1)
                else:
                    act.wait_ge(kl_full[g], k)
                    A(kvl[g][:], four(CHAIN[:]), ACT.Copy).then_inc(kl_ok[g], 1)

            def chain1(g):
                yield
                yield
                yield from squares(g, 0)
                yield from idle(5)
                keys(g, 1, S2)
                yield

            def chain2(g):
                yield
                yield from squares(g, 1)
                yield
                yield
                keys(g, 1, S)
                yield

            def chain3(g):
                yield
                yield from squares(g, 2)
                yield
                yield from squares(g, 3)
                yield from idle(3)
                act.wait_ge(mo_lg[g], 1)
                A(aff[g], lg[g], ACT.Sigmoid).then_inc(mo_sig[g], 1)
                yield from idle(4)

            def chain4(g):
                yield
                yield from squares(g, 4)
                yield

            def chain5(g):
                yield
                yield from squares(g, 5)
                yield
                yield from squares(g, 6)
                yield
                yield
                keys(g, 2, S2)
                yield
                yield
                keys(g, 2, S)
                yield

            def chain6(g):
                yield
                yield from squares(g, 7)
                yield

            def high(k):
                n, w = (NMOE // CH, wb) if k < CH else (NRET // CH, wa)
                act.wait_ge(d_ring[k % RING], 16 * (k // RING + 1))
                o = k % RING * (NMOE // CH)
                A(w[:, k % CH * n:k % CH * n + n], stage[:, o:o + n], ACT.Copy).then_inc(w_hid, 1)

            def prepare():
                act.dma_start(sel[:], sel_d).then_inc(d_sel, 16)
                yield from idle(10)

            def main1(g):
                yield
                act.wait_ge(la_min, 2 * g + 1)
                A(q_e, q_m, ACT.Exp).then_inc(la_exp, 1)
                yield
                yield
                yield
                act.wait_ge(la_min, 2 * g + 2)
                A(k_e, k_m, ACT.Exp).then_inc(la_exp, 1)
                yield from idle(9)

            def attention(g, a):
                units = UNITS[a]

                def query(n):
                    r = slots[g, 0, "g", n]
                    act.wait_ge(s_full, r + 1)
                    A(g_s[n // 4 % 2][:, n % 4, :], ps[r % NS][:], ACT.Copy).then_inc(s_free, 1)

                def exps(u):
                    n = unit_no(g, a, u)
                    for s in range(2):
                        r = slots[g, a, u, s]
                        act.wait_ge(m_done, 2 * n + s + 1)
                        if s == 0 and n >= 3:
                            act.wait_ge(t_full, n - 2)
                            act.wait_ge(r_done, n - 2)
                        for j in range(2):
                            o = 4 * (n % 3) + 2 * s + j
                            last = A(P[n % 3][:, 2 * s + j, :], ps[r % NS][:, j * KEYS:(j + 1) * KEYS], ACT.Exp,
                                     bias=nm[:, o:o + 1], accum_out=sm[:, o:o + 1])
                        last.then_inc(s_free, 1)

                def turned(u):
                    n = unit_no(g, a, u)
                    act.wait_ge(t_full, n + 1)
                    if n >= 2:
                        act.wait_ge(u_full, n - 1)
                    A(ptc[n % 2][0:S2, :], ps[3][0:S2, :], ACT.Copy).then_inc(pc_done, 1)

                if a == 0:
                    for n in range(4):
                        query(n)
                        yield
                for i in range(units + 4):
                    if a == 0 and i + 4 < units:
                        query(i + 4)
                    if i < units:
                        exps(i)
                    yield
                    if 2 <= i < units + 2:
                        turned(i - 2)
                    yield
                    if a == 0 and g == 0 and 4 <= i < 4 + CH:
                        high(i - 4)
                    yield

            def main2(g):
                yield from attention(g, 0)

            def main3(g):
                n0 = g * (PAIRS + 1)
                for i in range(PAIRS + 3):
                    if i <= PAIRS:
                        n = n0 + i
                        m = 128 if i < PAIRS else EI
                        bg = v_("bg", i) if i < PAIRS else v_("bg_s")
                        act.wait_ge(mo_gu, n + 1)
                        if n >= 2:
                            act.wait_ge(mo_tu, n - 1)
                        A(si[n % 2][0:m, :], ps[n % 2][0:m, :], ACT.Silu, bias=bg[0:m, :]).then_inc(mo_si, 1)
                    yield
                    if g == 0 and 2 <= i < 2 + CH:
                        high(CH + i - 2)
                    yield

            def main4(g):
                for n in range(2 * NB):
                    act.wait_ge(re_v, g * 2 * NB + n + 1)
                    A(r_v[:, n // 2, n % 2 * 512:n % 2 * 512 + 512], ps[n % 4][:], ACT.Silu).then_inc(re_vs, 1)
                    yield

                def silus(i):
                    n = g * RH + i
                    t = r_qk[i // 2 % 2]
                    act.wait_ge(re_p, n + 1)
                    if i % 2 == 0 and n >= 4:
                        act.wait_ge(re_a, n - 2)
                    A(t[:, 2 * (i % 2) + 1, :], ps[3][:], ACT.Silu).then_inc(re_pas, 1)
                    act.wait_ge(re_t3, n + 1)
                    A(t[:, 2 * (i % 2), :], r_t1[n % 2], ACT.Silu).then_inc(re_s, 1)

                for i in range(2):
                    silus(i)
                    yield
                for p in range(RH // 2):
                    for i in range(2):
                        if p + 1 < RH // 2:
                            silus(2 * p + 2 + i)
                        yield
                    yield from idle(4)

            def main5(g):
                for p in range(4):
                    act.wait_ge(xa_full, 16 * g + p + 1)
                    A(xq_s[:, p, :], ps[p % 3][:], ACT.Copy, scale=HD ** -0.5).then_inc(xa_q, 1)
                    yield
                yield from idle(8)
                for p in range(4):
                    act.wait_ge(xa_full, 16 * g + 12 + p + 1)
                    A(xk_s[:, p, :, S2:KEYS], four(ps[(12 + p) % 3][:]), ACT.Copy).then_inc(xa_kl, 1)
                    yield
                yield from attention(g, 1)

            def main6(g):
                for j in range(4):
                    act.wait_ge(ff_up, 4 * g + j + 1)
                    if g:
                        act.wait_ge(ff_ms, 1)
                    A(f_g[:, j, :], ps[j][:], ACT.Gelu).then_inc(ff_g, 1)
                    yield
                yield from idle(7)

            run(prepare, [None, main1, main2, main3, main4, main5, main6],
                [None, chain1, chain2, chain3, chain4, chain5, chain6])

        @block_.gpsimd
        def _(pool):
            TT = nc.gpsimd.tensor_tensor

            def factor(g, k, w=1):
                yield from idle(5)
                pool.wait_ge(ln_ve[g], k + 1)
                if k < 7:
                    TT(rs_t[g][:, 0:NB * w], ve[g][:, 0:NB * w], half_n[:, 0:NB * w], ALU.pow).then_inc(ln_pow[g], 1)
                else:
                    TT(rs_t[g][:, 0:2 * NB], ve[g][:, 0:2 * NB], half_p[:, 0:2 * NB], ALU.pow).then_inc(f_root, 1)
                yield from idle(3)

            def chain1(g):
                yield
                yield
                pool.wait_ge(c_ve[g], 1)
                if g == 0:
                    pool.wait_ge(half_ok, 1)
                TT(crs[g], crs[g], half_n[0:S2, 0:NB], ALU.pow).then_inc(c_pow[g], 1)
                yield from factor(g, 0)
                yield from idle(6)

            def chain2(g):
                yield
                yield from factor(g, 1)
                yield from idle(3)

            def chain3(g):
                yield
                yield from factor(g, 2)
                yield
                yield from factor(g, 3)
                yield from idle(7)

            def chain4(g):
                yield
                yield from factor(g, 4)
                yield

            def chain5(g):
                yield
                yield from factor(g, 5, w=16)
                yield
                yield from factor(g, 6)
                yield from idle(4)

            def chain6(g):
                yield
                yield from factor(g, 7)
                yield

            def low(k):
                n, w, size = (NMOE // CH, wb, NMOE) if k < CH else (NRET // CH, wa, NRET)
                o, c = k % RING * (NMOE // CH), k % CH * n
                pool.wait_ge(w_hid, k + 1)
                TT(w[:, size + c:size + c + n], stage[:, o:o + n], w[:, c:c + n].bitcast(F32), ALU.subtract)\
                    .then_inc(w_split, 1)

            def prepare():
                yield from idle(10)

            def main1(g):
                yield from idle(14)

            def attention(g, a):
                if a == 0:
                    yield from idle(4)
                for i in range(UNITS[a] + 4):
                    if 1 <= i <= UNITS[a]:
                        n = unit_no(g, a, i - 1)
                        o = 4 * (n % 3)
                        pool.wait_ge(r_done, n + 1)
                        r = rs[:, o:o + 4].rearrange("p (h o) -> p h o", o=1).to_broadcast([128, 4, KEYS])
                        TT(P[n % 3], P[n % 3], r, ALU.mult).then_inc(n_done, 1)
                    yield
                    yield
                    if a == 0 and g == 0 and 4 <= i < 4 + CH:
                        low(i - 4)
                    yield

            def main2(g):
                yield from attention(g, 0)

            def main3(g):
                for i in range(PAIRS + 3):
                    yield
                    if g == 0 and 2 <= i < 2 + CH:
                        low(CH + i - 2)
                    yield

            def main4(g):
                yield from idle(2 * NB)

                def rotated(i):
                    n = g * RH + i
                    pool.wait_ge(re_t, 2 * n + 2)
                    TT(r_t1[n % 2], r_t1[n % 2], r_t2[n % 2], ALU.add).then_inc(re_t3, 1)

                for i in range(2):
                    rotated(i)
                    yield
                for p in range(RH // 2):
                    for i in range(2):
                        if p + 1 < RH // 2:
                            rotated(2 * p + 2 + i)
                        yield
                    yield from idle(4)

            def main5(g):
                yield from idle(4)
                for p in range(4):
                    yield
                    pool.wait_ge(xa_kx, 8 * g + 2 * p + 2)
                    TT(xk_s[:, p, :, 0:S2], xt1[:, :, 0:S2], xt2[:, :, 0:S2], ALU.add).then_inc(xa_kt, 1)
                    yield
                yield from idle(4)
                yield from attention(g, 1)

            def main6(g):
                yield
                for j in range(4):
                    pool.wait_ge(ff_g, 4 * g + j + 1)
                    if g:
                        pool.wait_ge(ff_ms, 1)
                    TT(f_sq[:, j, :], f_g[:, j, :], f_g[:, j, :], ALU.mult).then_inc(ff_sq, 1)
                    yield
                yield from idle(3)
                pool.wait_ge(f_ve, g + 1)
                TT(rs_t[g][:, 0:NB], ve[g][:, 0:NB], half_p[:, 0:NB], ALU.pow).then_inc(f_pow, 1)
                yield from idle(3)

            run(prepare, [None, main1, main2, main3, main4, main5, main6],
                [None, chain1, chain2, chain3, chain4, chain5, chain6])


def _constants():
    f = np.float32
    con = np.zeros((128, NCON), f)

    def put(name, a):
        lo, n = CON[name]
        con[:, lo:lo + n] = a
    i = np.arange(128)
    put("ident", np.eye(128))
    put("mean", np.full((128, 128), 1 / 128))
    put("block", (i[:, None] // 8 == i[None, :] // 8))
    put("head", (i[:, None] // 8 == np.arange(16)[None, :]))
    diff = i[:, None] - i[None, :]
    put("decay", np.where(diff >= 0, f(GAMMA) ** np.maximum(diff, 0).astype(f), 0))
    inv = (1.0 / 10000.0 ** (np.arange(0, ROT, 2, dtype=f) / f(ROT))).astype(f)
    ang = (np.arange(S, dtype=f)[None, :] * np.tile(np.repeat(inv, 2), 2)[:, None]).astype(f)
    put("cosA", np.cos(ang))
    put("sinA", np.sin(ang) * np.where(i % 2 == 0, -1, 1)[:, None])
    ang = (np.arange(S2, dtype=f)[None, :] * np.tile(inv, 4)[:, None]).astype(f)
    put("cosX", np.cos(ang))
    put("sinX", np.sin(ang) * np.where(i % HD < HD // 2, -1, 1)[:, None])
    sel = np.zeros((96, PAIRS * 128), f)
    for p in range(PAIRS):
        for m in range(128):
            for k in range(3):
                sel[k * E + 2 * p + m // EI, p * 128 + m] = 1
    return con, sel


def _layout(a):
    con, sel = _constants()
    f = np.float32

    def vec(name, v):
        lo = CON["vec"][0] + VEC[name][0]
        v = np.asarray(v)
        v = v.reshape(VEC[name][1], -1).T
        con[0:v.shape[0], lo:lo + v.shape[1]] = v
    for name, key in (("bq", "L0_attn_bq"), ("bo", "L0_attn_bo"), ("g_x0", "L0_xattn_g_x"), ("b_x0", "L0_xattn_b_x"),
                      ("g_l0", "L0_xattn_g_l"), ("b_l0", "L0_xattn_b_l"), ("g_o0", "L0_xattn_g_o"),
                      ("b_o0", "L0_xattn_b_o"), ("bd_s", "L0_ffn_bd_s"), ("gnw", "L1_attn_gn_weight"),
                      ("gnb", "L1_attn_gn_bias"), ("g_x1", "L1_xattn_gamma_x"), ("b_x1", "L1_xattn_beta_x"),
                      ("g_l1", "L1_xattn_gamma_l"), ("b_l1", "L1_xattn_beta_l"), ("bg", "L0_ffn_bg"),
                      ("bu", "L0_ffn_bu"), ("bg_s", "L0_ffn_bg_s"), ("bu_s", "L0_ffn_bu_s")):
        vec(name, a[key])
    lo, n = CON["bkv"]
    con[:, lo:lo + D] = a["L0_attn_bk"][None, :]
    con[:, lo + D:lo + n] = a["L0_attn_bv"][None, :]
    lo, n = CON["br"]
    con[:, lo:lo + n] = a["L0_ffn_br"][None, :]

    spl = {"lin": np.zeros((128, NLIN), f), "moe": np.zeros((128, NMOE), f), "ret": np.zeros((128, NRET), f)}

    def put(pack, table, name, w):
        lo, n = table[name]
        w = np.asarray(w).reshape(-1, n)
        pack[0:w.shape[0], lo:lo + n] = w
    put(spl["lin"], LIN, "wq", a["L0_attn_Wq"].T)
    put(spl["lin"], LIN, "wkv", np.concatenate([a["L0_attn_Wk"].T, a["L0_attn_Wv"].T], axis=1))
    put(spl["moe"], MOE, "wr", a["L0_ffn_Wr"])
    put(spl["moe"], MOE, "wg", a["L0_ffn_Wg"].transpose(1, 0, 2).reshape(D, -1))
    put(spl["moe"], MOE, "wu", a["L0_ffn_Wu"].transpose(1, 0, 2).reshape(D, -1))
    put(spl["moe"], MOE, "wg_s", a["L0_ffn_Wg_s"])
    put(spl["moe"], MOE, "wu_s", a["L0_ffn_Wu_s"])
    for k in "QK":
        w = a[f"L1_attn_W_{k}"].reshape(D, RH, D)
        rot, pas = w[:, :, 0:ROT], w[:, :, ROT:]
        put(spl["ret"], RET, f"r{k.lower()}_rot", rot.reshape(D, -1))
        put(spl["ret"], RET, f"r{k.lower()}_swp", rot[:, :, np.arange(ROT) ^ 1].reshape(D, -1))
        put(spl["ret"], RET, f"r{k.lower()}_pas", pas.reshape(D, -1))
    put(spl["ret"], RET, "rv", a["L1_attn_W_V"])

    raw, xat, ffn = np.zeros((128, NRAW), f), np.zeros((128, NXAT), f), np.zeros((128, NFFN), f)
    put(raw, RAW, "woT", a["L0_attn_Wo"].T)
    put(raw, RAW, "wd", a["L0_ffn_Wd"].reshape(PAIRS, 128, D).transpose(1, 0, 2).reshape(128, -1))
    put(raw, RAW, "wd_s", a["L0_ffn_Wd_s"])
    put(raw, RAW, "bd3", np.concatenate([a["L0_ffn_bd"]] * 3, axis=0))
    inner = LH1 * HD
    wk = a["L1_xattn_Wkv"][:, 0:inner]
    put(xat, XAT, "xq", a["L1_xattn_Wq"])
    put(xat, XAT, "xk", wk)
    put(xat, XAT, "xks", wk.reshape(D, LH1, 2, HD // 2)[:, :, ::-1, :].reshape(D, -1))
    put(ffn, FFN, "up", a["L1_ffn_w_up"].T)
    put(ffn, FFN, "down", a["L1_ffn_w_down"].T.reshape(4, 128, D).transpose(1, 0, 2).reshape(128, -1))

    def pairs(w):
        return w.reshape(-1, 128, w.shape[1]).transpose(1, 0, 2).reshape(128, -1)
    inner0 = LH0 * HD
    kv = a["L0_xattn_Wkv"]
    fold = np.concatenate([pairs(a["L0_xattn_Wq"].T), pairs(kv[:, 0:inner0].T), pairs(kv[:, inner0:].T),
                           pairs(a["L0_xattn_Wout"]), pairs(a["L1_xattn_Wkv"][:, inner:].T),
                           pairs(a["L1_xattn_Wo"])], axis=1)
    return con, sel, spl, raw, xat, ffn, fold


def kernel(**inputs):
    import ml_dtypes
    import concourse.bacc as _bacc
    from concourse.bass_utils import run_bass_kernel_spmd as _run

    a = {k: np.asarray(v) for k, v in inputs.items()}
    con, sel, spl, raw, xat, ffn, fold = _layout(a)
    arrays = {
        "x": np.ascontiguousarray(a["x"]), "ctx": np.ascontiguousarray(a["ctx_1024"]),
        "mask": np.ascontiguousarray(a["mask_BxS2_bf1"]).view(np.uint8).reshape(1, B * S2),
        "con": con, "sel": sel.astype(ml_dtypes.bfloat16), **spl, "raw": raw, "xat": xat, "ffn": ffn,
        "fold": np.ascontiguousarray(fold),
    }
    nc = _bacc.Bacc("TRN2", target_bir_lowering=False, num_devices=1)
    args = [nc.dram_tensor(f"in_{k}", v.shape, mybir.dt.from_np(v.dtype), kind="ExternalInput").ap()
            for k, v in arrays.items()]
    args.append(nc.dram_tensor("out_0", (B, S, D), F32, kind="ExternalOutput").ap())
    decoder_kernel(nc, *args)
    r = _run(nc, [{f"in_{k}": v for k, v in arrays.items()}], core_ids=[0])
    return r.results[0]["out_0"]
```

```python
from contextlib import ExitStack

import numpy as np

import concourse.bass as bass
from concourse import mybir
from concourse.alu_op_type import AluOpType as ALU

F32 = mybir.dt.float32
F32R = mybir.dt.float32r
BF16 = mybir.dt.bfloat16
U8 = mybir.dt.uint8
ACT = mybir.ActivationFunctionType
AX_X = mybir.AxisListType.X

B, S, D = 8, 128, 128
S2 = 120
NB = 4
G = B // NB
T = NB * S
KEYS = S2 + S
LH0, LH1 = 16, 8
HD = 64
E, EI, TOPK = 32, 64, 8
PAIRS = E // 2
RH = 8
ROT = 64
GAMMA = 0.96875
DFF = 512
assert TOPK == 8
EPS = 1e-5
MASKED = -3.0e38

VEC = {}
for _name, _n in (("bq", 1), ("bo", 1), ("g_x0", 1), ("b_x0", 1), ("g_l0", 1), ("b_l0", 1), ("g_o0", 1),
                  ("b_o0", 1), ("bd_s", 1), ("gnw", 1), ("gnb", 1), ("g_x1", 1), ("b_x1", 1), ("g_l1", 1),
                  ("b_l1", 1), ("bg", PAIRS), ("bu", PAIRS), ("bg_s", 1), ("bu_s", 1)):
    VEC[_name] = (sum(n for _, n in VEC.values()), _n)
NVEC = sum(n for _, n in VEC.values())

CON = {}
for _name, _n in (("ident", 128), ("mean", 128), ("block", 128), ("head", 16), ("decay", 128), ("cosA", 128),
                  ("sinA", 128), ("cosX", S2), ("sinX", S2), ("vec", NVEC), ("bkv", 2 * D), ("br", E)):
    CON[_name] = (sum(n for _, n in CON.values()), _n)
NCON = sum(n for _, n in CON.values())

def columns(*names):
    table = {}
    for name, n in names:
        table[name] = (sum(m for _, m in table.values()), n)
    return table, sum(m for _, m in table.values())


LIN, NLIN = columns(("wq", D), ("wkv", 2 * D))
MOE, NMOE = columns(("wr", E), ("wg", E * EI), ("wu", E * EI), ("wg_s", EI), ("wu_s", EI))
RET, NRET = columns(("rv", 1024), ("rq", 1024), ("rq_swp", 512), ("rk", 1024), ("rk_swp", 512))
CH = 8
RING = 5
RAW, NRAW = columns(("woT", D), ("wd", PAIRS * D), ("wd_s", D), ("bd3", D))
XAT, NXAT = columns(("xq", 512), ("xk", 512), ("xks", 512))
FFN, NFFN = columns(("up", DFF), ("down", DFF))
FOLD = {"qT": 0, "kT": 1024, "vT": 2048, "o": 3072, "vT1": 4096, "o1": 4608}
NFOLD = 5120
QF = LH0 * D
STAGE = max(RING * (NMOE // CH), 4 * T + NFFN)
ARENA = 11264


def weave(main, side, every=1, start=0):
    n = 0
    for _ in main:
        n += 1
        if n == 1 or n > start and int((n - start) / every) > int((n - 1 - start) / every):
            next(side, None)
        yield
    yield from side


def in_turn(*parts):
    for part in parts:
        yield from part


def decoder_kernel(nc, x_d, ctx_d, mask_d, con_d, sel_d, lin_d, moe_d, ret_d, raw_d, xat_d, ffn_d, fold_d, out_d):
    ctx = ExitStack()
    with ctx:
        def sb(name, shape, dt=F32):
            return ctx.enter_context(nc.sbuf_tensor(name, shape, dt))

        def sem(name):
            return ctx.enter_context(nc.semaphore(name))

        def sems(name):
            return [sem(f"{name}_{g}") for g in range(G)]

        con = sb("con", [128, NCON])
        sel = sb("sel", [96, PAIRS * 128], BF16)
        wa = sb("wa", [128, 2 * NRET], F32R)
        wb = sb("wb", [128, 2 * NMOE], F32R)
        stage = sb("stage", [128, STAGE])
        raw = sb("raw", [128, NRAW])
        fb0, fb1 = sb("fb0", [128, LH0 * D]), sb("fb1", [128, LH1 * D])
        mrow = sb("mrow", [128, B, S2], BF16)
        ones = sb("ones", [128, 128], BF16)
        small = sb("small", [128, 272])
        wpart = sb("wpart", [128, NB, E], BF16)
        m8 = sb("m8", [1, B * S2], U8)
        xT = [sb(f"xT{g}", [128, T]) for g in range(G)]
        xc = [sb(f"xc{g}", [128, T]) for g in range(G)]
        sq = [sb(f"sq{g}", [128, T]) for g in range(G)]
        hf = [sb(f"hf{g}", [128, T]) for g in range(G)]
        h_hi = [sb(f"h_hi{g}", [128, T], F32R) for g in range(G)]
        h_lo = [sb(f"h_lo{g}", [128, T], F32R) for g in range(G)]
        cT = [sb(f"cT{g}", [128, NB, S2]) for g in range(G)]
        kvT = [sb(f"kvT{g}", [128, NB, KEYS]) for g in range(G)]
        kvc = [sb(f"kvc{g}", [S2, NB, D]) for g in range(G)]
        kvl = [sb(f"kvl{g}", [128, NB, D]) for g in range(G)]
        tiny = [sb(f"tiny{g}", [128, 240]) for g in range(G)]
        arena = sb("arena", [128, ARENA])

        def shaped(v, *shape):
            names = "abcd"[:len(shape)]
            if len(shape) == 1:
                return v
            return v.rearrange(f"p ({' '.join(names)}) -> p {' '.join(names)}",
                               **{k: d for k, d in zip(names[1:], shape[1:])})

        at = [0]

        def cut(*shape):
            n = int(np.prod(shape))
            assert at[0] + n <= ARENA, (at[0], n)
            at[0] += n
            return shaped(arena[:, at[0] - n:at[0]], *shape)

        r_fold = cut(NFOLD)

        def linear_tiles(take):
            q_z, q_m, q_f = take(T), take(T), take(T)
            k_z, k_m, k_f = take(NB, D), take(NB, D), take(NB, D)
            v_1, kv_b, o_t, o_n = take(NB, D + 1), take(NB, D + 16), take(NB, D), take(T)
            return q_z, q_m, q_f, k_z, k_m, k_f, v_1, kv_b, o_t, o_n

        beside_at = [0]

        def beside(*shape):
            n, a = int(np.prod(shape)), beside_at[0]
            beside_at[0] += n
            if a + n <= STAGE:
                return shaped(stage[:, a:a + n], *shape)
            a += D - 6 * T
            assert a >= D
            return shaped(raw[:, a:a + n], *shape)

        linear = [linear_tiles(cut), linear_tiles(beside)]
        at[0] = 0
        P = [cut(4, KEYS) for _ in range(3)]
        ptc, ptl = [cut(T) for _ in range(2)], [cut(T) for _ in range(2)]
        us = cut(4, NB, S)
        g_s = [cut(4, T) for _ in range(2)]
        at[0] -= 2 * 4 * T
        xk_s = cut(4, NB, KEYS)
        xq_s = shaped(stage[:, 0:4 * T], 4, T)
        xt1, xt2 = (us[:, 0], us[:, 2]), (us[:, 1], us[:, 3])
        at[0] = 0
        si, tu, av = [cut(T) for _ in range(2)], [cut(T) for _ in range(2)], [cut(T) for _ in range(3)]
        at[0] = 0
        r_v = cut(NB, RH * D)
        r_t1, r_t2 = [cut(T) for _ in range(2)], [cut(T) for _ in range(2)]
        r_qk = [cut(4, T) for _ in range(2)]
        r_a = [cut(4, S) for _ in range(2)]
        at[0] = 0
        f_g, f_sq = cut(4, T), cut(4, T)
        x_out = [cut(NB, D) for _ in range(G)]

        lg, aff, rep, wn = ([shaped(hf[g][:, i * NB * E:(i + 1) * NB * E], NB, E) for g in range(G)] for i in range(4))
        wcat = [shaped(xc[g][:, 0:NB * 3 * E], NB, 3 * E) for g in range(G)]
        w3f = [sq[g][0:96, :] for g in range(G)]
        w3b = [xc[g][0:96, 0:T // 2].bitcast(BF16) for g in range(G)]
        nm, sm, rs = small[:, 0:12], small[:, 12:24], small[:, 24:36]
        bq1, gk0, gk1 = small[:, 36:37], small[:, 37:38], small[:, 38:39]
        wabs, thr, thr_n = small[:, 40:42], small[:, 42:44], small[:, 44:46]
        half_n, half_p, head8 = small[:, 48:112], small[:, 112:120], small[:, 120:136]
        block_mean = small[:, 136:264]
        ve, rs_t = [t[:, 0:64] for t in tiny], [t[:, 64:128] for t in tiny]
        lden = rs_t
        top, tsum = [t[:, 128:160] for t in tiny], [t[:, 160:164] for t in tiny]
        xst, xag, xrs = ([t[:, a:b] for t in tiny] for a, b in ((204, 228), (228, 236), (236, 240)))
        bnst, bnag, crs = ([t[0:S2, a:b] for t in tiny] for a, b in ((168, 192), (192, 200), (200, 204)))

        ps = [ctx.enter_context(nc.psum_tensor(f"bank{i}", [128, 512], F32)) for i in range(8)]
        OUT, CHAIN = ps[6], ps[7]

        def four(t):
            return t.rearrange("p (b s) -> p b s", b=NB)

        def c_(name):
            lo, w = CON[name]
            return con[:, lo:lo + w]

        def v_(name, i=0):
            lo = CON["vec"][0] + VEC[name][0] + i
            return con[:, lo:lo + 1]

        def split(t, base, size, table, name, i=0, n=None):
            lo, w = table[name]
            lo, n = base + lo + i, w if n is None else n
            return t[:, lo:lo + n], t[:, size + lo:size + lo + n]

        def lin(name):
            return split(wa, 2 * QF, NLIN, LIN, name)

        def moe(name, *a):
            return split(wb, 0, NMOE, MOE, name, *a)

        def ret(name, *a):
            return split(wa, 0, NRET, RET, name, *a)

        def whole(t, base, table, name, i=0, n=None):
            lo, w = table[name]
            return t[:, base + lo + i:base + lo + i + (w if n is None else n)]

        def r_(name, *a):
            return whole(raw, 0, RAW, name, *a)

        def x_(name, *a):
            return whole(fb0, 0, XAT, name, *a)

        def xw(name, *a):
            return split(wb, 0, 1024, XAT, name, *a)

        def f_(name, *a):
            return whole(stage, 4 * T, FFN, name, *a)

        fa_hi, fa_lo = wa[:, 0:QF], wa[:, QF:2 * QF]
        ident, meanm, block = c_("ident"), c_("mean"), c_("block")

        d_ident, d_con, d_raw, d_sel, d_lin, d_xat, d_ffn, d_m = (sem(n) for n in (
            "d_ident", "d_con", "d_raw", "d_sel", "d_lin", "d_xat", "d_ffn", "d_m"))
        d_fold = [sem(f"d_fold{i}") for i in range(3)]
        d_ring = [sem(f"d_ring{i}") for i in range(RING)]
        d_x, d_c, d_out = sems("d_x"), sems("d_c"), sem("d_out")
        v_link = sem("v_link")
        l_split, w_hid, w_split = sem("l_split"), sem("w_hid"), sem("w_split")
        fold_hi, fold_full, fold_out = sem("fold_hi"), sem("fold_full"), sem("fold_out")
        tern_sum, tern_all, tern_ok, half_ok = sem("tern_sum"), sem("tern_all"), sem("tern_ok"), sem("half_ok")
        ln_tr = sems("ln_tr")
        ln_x, ln_mean, ln_xc, ln_sq, ln_var, ln_ve, ln_pow, ln_bc, gn_ex, h_ok = (sems(n) for n in (
            "ln_x", "ln_mean", "ln_xc", "ln_sq", "ln_var", "ln_ve", "ln_pow", "ln_bc", "gn_ex", "h_ok"))
        xt_full, ct_full, kc_full, kl_full, cn_ok, ckv_ok, kc_ok, kl_ok, c_ve, c_pow = (sems(n) for n in (
            "xt_full", "ct_full", "kc_full", "kl_full", "cn_ok", "ckv_ok", "kc_ok", "kl_ok", "c_ve", "c_pow"))
        x_ve, x_pow, xn_ok, xn_full, x_hi = (sems(n) for n in ("x_ve", "x_pow", "xn_ok", "xn_full", "x_hi"))
        m_ok, xw_hi, xw_lo = sem("m_ok"), sem("xw_hi"), sem("xw_lo")
        mo_log, mo_lg, mo_sig, mo_w, mo_wt, mo_w3 = (sems(n) for n in (
            "mo_log", "mo_lg", "mo_sig", "mo_w", "mo_wt", "mo_w3"))
        la_full, la_read, la_min, la_exp, la_qf, la_kf = (sem(n) for n in (
            "la_full", "la_read", "la_min", "la_exp", "la_qf", "la_kf"))
        s_full, s_free, m_done, r_done, n_done = (sem(n) for n in ("s_full", "s_free", "m_done", "r_done", "n_done"))
        t_full, pc_done, pl_done, u_full, ue_done, bo_full = (sem(n) for n in (
            "t_full", "pc_done", "pl_done", "u_full", "ue_done", "bo_full"))
        mo_gu, mo_si, mo_tu, mo_wb, mo_a, mo_dn = (sem(n) for n in ("mo_gu", "mo_si", "mo_tu", "mo_wb", "mo_a",
                                                                    "mo_dn"))
        re_v, re_vs, re_p, re_t, re_t3, re_s, re_pas, re_a, re_as, re_o = (sem(n) for n in (
            "re_v", "re_vs", "re_p", "re_t", "re_t3", "re_s", "re_pas", "re_a", "re_as", "re_o"))
        xa_full, xa_q, xa_kx, xa_kt, xa_kl = (sem(n) for n in ("xa_full", "xa_q", "xa_kx", "xa_kt", "xa_kl"))
        ff_up, ff_g, ff_sq, ff_sum, ff_ms, ff_dn, fx_in, fx_t, fx_out, f_ve, f_pow, f_root = (
            sem(n) for n in ("ff_up", "ff_g", "ff_sq", "ff_sum", "ff_ms", "ff_dn", "fx_in", "fx_t", "fx_out", "f_ve",
                             "f_pow", "f_root"))

        UNITS = (4 * LH0 // 4, 4 * LH1 // 4)
        NS = 3

        def unit_no(g, a, u):
            return a * G * UNITS[0] + g * UNITS[a] + u

        def quad_no(g, a, q):
            return unit_no(g, a, 4 * q) // 4

        slots = {}
        for a in range(2):
            for g in range(G):
                for u in range(-4, UNITS[a]):
                    if a == 0 and u + 4 < UNITS[0]:
                        slots[g, a, "g", u + 4] = len(slots)
                    if u >= 0:
                        slots[g, a, u, 0] = len(slots)
                        slots[g, a, u, 1] = len(slots)
        unit_key = {unit_no(g, a, u): (g, a, u) for a in range(2) for g in range(G) for u in range(UNITS[a])}

        def exp_of(n):
            return slots[(*unit_key[n], 1)] + 1

        OUT_READ = (None, 2, 3, 5, 6, 8)

        ROUNDS = 9
        LBANK = [(ps[0], ps[1], ps[2], ps[3], ps[4], ps[1], ps[2], ps[3], OUT), (CHAIN,) * ROUNDS]

        def bc(t, n):
            return t.rearrange("p (o e) -> p o e", o=1).to_broadcast([t.shape[0], n, t.shape[1]])

        def turned_no(k):
            return k if k < 5 else k - 1

        def idle(n):
            for _ in range(n):
                yield

        def run(folds, context, main, chain):
            first = weave(in_turn(chain[1](1), context(0), context(1)), main[1](0), 1, 6)
            phases = (
                weave(in_turn(chain[1](0), first, chain[2](0)), folds(), 3, 2),
                weave(main[2](0), in_turn(main[1](1), chain[2](1)), 2, 0),
                weave(main[2](1), chain[3](0), 2, 6),
                weave(main[3](0), chain[3](1), 1, 14),
                weave(main[3](1), chain[4](0), 3.5, 1),
                weave(main[4](0), chain[4](1), 2, 3),
                weave(main[4](1), chain[5](0), 1, 3),
                weave(main[5](0), chain[5](1), 2, 18),
                weave(main[5](1), chain[6](0), 3, 19),
                weave(main[6](0), chain[6](1), 1, 2),
                main[6](1))
            for _ in in_turn(*phases):
                pass

        block_ = ctx.enter_context(nc.Block())

        @block_.sync
        def _(sp):
            def rows(t, g):
                return t[g * NB:(g + 1) * NB].rearrange("b s d -> s b d")

            first = CON["block"][0]
            sp.dma_start(hf[0][:].rearrange("p (b d) -> p b d", b=NB), rows(x_d, 0)).then_inc(d_x[0], 16)
            sp.dma_start(con[:, 0:first], con_d[:, 0:first]).then_inc(d_ident, 16)
            sp.dma_start(con[:, first:NCON], con_d[:, first:NCON]).then_inc(d_con, 16)
            sp.dma_start(kvc[0][:], rows(ctx_d, 0)).then_inc(d_c[0], 16)
            sp.dma_start(shaped(stage[:, 0:NLIN], NLIN), lin_d).then_inc(d_lin, 16)
            for i, (a, b) in enumerate(((0, FOLD["vT"]), (FOLD["vT"], FOLD["vT1"]), (FOLD["vT1"], NFOLD))):
                sp.dma_start(r_fold[:, a:b], fold_d[:, a:b]).then_inc(d_fold[i], 16)
                if i == 0:
                    sp.dma_start(hf[1][:].rearrange("p (b d) -> p b d", b=NB), rows(x_d, 1)).then_inc(d_x[1], 16)
                    sp.dma_start(kvc[1][:], rows(ctx_d, 1)).then_inc(d_c[1], 16)
                    sp.dma_start(raw[:, 0:D], raw_d[:, 0:D]).then_inc(d_raw, 16)
            sp.dma_start(m8[:], mask_d).then_inc(d_m, 16)
            for k in range(2 * CH):
                if k == 0:
                    sp.wait_ge(la_full, G * ROUNDS)
                    sp.dma_start(raw[:, D:NRAW], raw_d[:, D:NRAW]).then_inc(d_raw, 16)
                if k == CH:
                    sp.wait_ge(bo_full, quad_no(1, 0, 3) + 1)
                    sp.dma_start(fb0[:, 0:NXAT], xat_d).then_inc(d_xat, 16)
                if k >= RING:
                    sp.wait_ge(w_split, k - RING + 1)
                src, n = (moe_d, NMOE // CH) if k < CH else (ret_d, NRET // CH)
                sp.dma_start(stage[:, k % RING * (NMOE // CH):k % RING * (NMOE // CH) + n],
                             src[:, k % CH * n:k % CH * n + n]).then_inc(d_ring[k % RING], 16)
            sp.wait_ge(w_split, 2 * CH)
            sp.dma_start(stage[:, 4 * T:4 * T + NFFN], ffn_d).then_inc(d_ffn, 16)
            for g in range(G):
                sp.wait_ge(fx_out, g + 1)
                sp.dma_start(rows(out_d, g), x_out[g]).then_inc(d_out, 16)
            sp.wait_ge(d_out, 16 * G)

        @block_.tensor
        def _(pe):
            mm, tr = nc.tensor.matmul, nc.tensor.transpose

            def mm3(out, w, m, start=True, stop=True):
                mm(out, w[0], m[0], start=start, stop=False)
                mm(out, w[1], m[0], start=False, stop=False)
                return mm(out, w[0], m[1], start=False, stop=stop)

            def norm(g, k, src):
                pe.wait_ge(ln_x[g], k + 1)
                for b in range(NB):
                    last = tr(CHAIN[:, b * D:(b + 1) * D], four(src)[:, b, :], ident)
                last.then_inc(ln_tr[g], 1)
                yield from idle(4)
                pe.wait_ge(ln_xc[g], k)
                for b in range(NB):
                    last = tr(CHAIN[:, b * S:(b + 1) * S], xc[g][:, b * D:(b + 1) * D], ident)
                last.then_inc(ln_bc[g], 1)
                yield

            def group_norm(g, k, src):
                pe.wait_ge(ln_x[g], k + 1)
                mm(CHAIN[:], block_mean, src, start=True, stop=True).then_inc(ln_mean[g], 1)
                yield from idle(3)
                pe.wait_ge(ln_sq[g], 1)
                w = D // 8
                for b in range(NB):
                    last = mm(CHAIN[:, b * w:(b + 1) * w], four(sq[g][:])[:, b, :], head8, start=True, stop=True)
                last.then_inc(ln_var[g], 1)
                yield from idle(10)
                pe.wait_ge(gn_ex[g], 1)
                for b in range(NB):
                    last = tr(CHAIN[:, b * S:(b + 1) * S], four(sq[g][:])[:, b, :], ident)
                last.then_inc(ln_bc[g], 1)
                yield

            def output_free(g, stage):
                if g == 1 and stage < 6:
                    pe.wait_ge(ln_x[0], OUT_READ[stage])
                if g == 0 and stage > 2:
                    pe.wait_ge(ln_x[1], OUT_READ[stage - 1])

            def keys_out(g, n):
                for b in range(NB):
                    src = kvT[g][:, b, 0:S2] if n == S2 else kvT[g][:, b, S2:KEYS]
                    last = tr(CHAIN[0:n, b * D:(b + 1) * D], src, ident)
                last.then_inc(kc_full[g] if n == S2 else kl_full[g], 1)

            def chain1(g):
                pe.wait_ge(d_x[g], 16)
                if g == 0:
                    pe.wait_ge(d_ident, 16)
                else:
                    pe.wait_ge(h_ok[0], 1)
                for b in range(NB):
                    last = tr(CHAIN[:, b * S:(b + 1) * S], hf[g][:, b * D:(b + 1) * D], ident)
                last.then_inc(xt_full[g], 1)
                yield from idle(3)
                pe.wait_ge(ln_x[g], 1)
                pe.wait_ge(xn_ok[g], 1)
                for b in range(NB):
                    last = tr(CHAIN[:, b * S:(b + 1) * S], xc[g][:, b * D:(b + 1) * D], ident)
                last.then_inc(xn_full[g], 1)
                yield from idle(3)

            def context(g):
                if g:
                    pe.wait_ge(kc_ok[0], 1)
                yield
                pe.wait_ge(cn_ok[g], 1)
                for b in range(NB):
                    last = tr(CHAIN[:, b * 128:b * 128 + S2], kvc[g][:, b, :], ident[0:S2, 0:S2])
                last.then_inc(ct_full[g], 1)
                yield
                yield
                pe.wait_ge(ckv_ok[g], 1)
                keys_out(g, S2)
                yield
                yield

            def chain2(g):
                yield
                if g == 0:
                    pe.wait_ge(kc_ok[1], 1)
                yield from norm(g, 1, xT[g][:])
                yield
                pe.wait_ge(h_ok[g], 2)
                keys_out(g, S)
                yield
                yield

            def chain3(g):
                yield
                if g == 0:
                    pe.wait_ge(kl_ok[1], 1)
                yield from norm(g, 2, hf[g][:])
                yield
                yield from norm(g, 3, xT[g][:])
                yield from idle(2)
                pe.wait_ge(h_ok[g], 3)
                pe.wait_ge(w_split, 1)
                hb = four(h_hi[g][:]), four(h_lo[g][:])
                for b in range(NB):
                    last = mm3(CHAIN[:, b * E:(b + 1) * E], (hb[0][:, b], hb[1][:, b]), moe("wr"))
                last.then_inc(mo_log[g], 1)
                yield
                yield
                yield
                yield from idle(3)
                pe.wait_ge(mo_w[g], 1)
                for b in range(NB):
                    last = tr(CHAIN[0:3 * E, b * S:(b + 1) * S], wcat[g][:, b, :], ident)
                last.then_inc(mo_wt[g], 1)
                yield
                yield

            def chain4(g):
                yield
                yield from norm(g, 4, xT[g][:])
                yield from idle(2)

            def chain5(g):
                yield
                if g == 1:
                    pe.wait_ge(kl_ok[0], 2)
                yield from group_norm(g, 5, hf[g][:])
                yield
                yield from norm(g, 6, xT[g][:])
                yield
                pe.wait_ge(h_ok[g], 5)
                keys_out(g, S2)
                yield
                yield
                pe.wait_ge(kc_ok[g], 2)
                keys_out(g, S)
                yield
                yield

            def chain6(g):
                yield
                if g == 0:
                    pe.wait_ge(kl_ok[1], 2)
                yield from norm(g, 7, xT[g][:])
                yield

            def folds():
                yield
                for n in range((2 * LH0 + LH1) // 4):
                    kind = 0 if n < 4 else 1 if n < 8 else 2
                    if n % 4 == 0:
                        pe.wait_ge(d_fold[kind], 16)
                    if n:
                        pe.wait_ge(fold_out, n)
                    a, b, h0 = (("qT", "kT", 0), ("vT", "o", LH0), ("vT1", "o1", 2 * LH0))[kind]
                    for j in range(4):
                        h = 8 * (n // 2) + n % 2 + 2 * j - h0
                        rows = slice(HD * (h % 2), HD * (h % 2) + HD)
                        ca, cb = FOLD[a] + h // 2 * D, FOLD[b] + h // 2 * D
                        last = mm(ps[5][:, j * D:(j + 1) * D], r_fold[rows, ca:ca + D], r_fold[rows, cb:cb + D],
                                  start=True, stop=True)
                    last.then_inc(fold_full, 1)
                    yield
                yield

            def main1(g):
                q_z, q_m, q_f, k_z, k_m, k_f, v_1, kv_b, o_t, o_n = linear[g]
                pe.wait_ge(h_ok[g], 1)
                if g == 0:
                    pe.wait_ge(l_split, 1)
                else:
                    pe.wait_ge(kl_ok[0], 1)
                hh = h_hi[g][:], h_lo[g][:]
                hb = four(hh[0]), four(hh[1])

                def bank(i):
                    if g and i:
                        pe.wait_ge(la_read, (ROUNDS - 1) * g + i)
                    elif 5 <= i < ROUNDS - 1:
                        pe.wait_ge(la_read, i - 3)
                    return LBANK[g][i]

                mm3(bank(0)[:], lin("wq"), hh).then_inc(la_full, 1)
                yield
                for i in range(2):
                    t = bank(1 + i)
                    for b in range(2 * i, 2 * i + 2):
                        last = mm3(t[:, 256 * (b % 2):256 * (b % 2) + 256], (hb[0][:, b], hb[1][:, b]), lin("wkv"))
                    last.then_inc(la_full, 1)
                    yield
                yield from idle(3)
                pe.wait_ge(la_kf, g + 1)
                for i in range(2):
                    t = bank(3 + i)
                    for b in range(2 * i, 2 * i + 2):
                        last = mm(t[:, (D + 1) * (b % 2):(D + 1) * (b % 2) + D + 1], k_f[:, b, :], v_1[:, b, :],
                                  start=True, stop=True)
                    last.then_inc(la_full, 1)
                    yield
                yield
                pe.wait_ge(la_qf, g + 1)
                w = D + 16
                for i in range(2):
                    pe.wait_ge(la_read, (ROUNDS - 1) * g + 4 + i)
                    t = bank(5 + i)
                    for b in range(2 * i, 2 * i + 2):
                        last = mm(t[:, w * (b % 2):w * (b % 2) + w], four(q_f)[:, b, :], kv_b[:, b, :], start=True,
                                  stop=True)
                    last.then_inc(la_full, 1)
                    yield
                yield
                pe.wait_ge(la_read, (ROUNDS - 1) * g + 7)
                t = bank(7)
                for b in range(NB):
                    last = tr(t[:, b * S:(b + 1) * S], o_t[:, b, :], ident)
                last.then_inc(la_full, 1)
                yield
                yield
                pe.wait_ge(la_read, (ROUNDS - 1) * g + 8)
                if g == 0:
                    pe.wait_ge(d_raw, 16)
                mm(bank(8)[:], r_("woT"), o_n, start=True, stop=True).then_inc(la_full, 1)
                yield

            def attention(g, a):
                units, fb = UNITS[a], (fb0, fb1)[a]

                def slot(key):
                    r = slots[key]
                    if r >= NS:
                        pe.wait_ge(s_free, r - NS + 1)
                    return ps[r % NS]

                def q_fold(g, n):
                    if n == 0:
                        pe.wait_ge(h_ok[g], 2)
                    w = fa_hi[:, n * D:(n + 1) * D], fa_lo[:, n * D:(n + 1) * D]
                    mm3(slot((g, 0, "g", n))[:], w, (h_hi[g][:], h_lo[g][:])).then_inc(s_full, 1)

                def scores(u):
                    q, b = u // 4, u % 4
                    if b == 0 and a == 0:
                        pe.wait_ge(s_free, slots[g, 0, "g", 4 * q + 3] + 1)
                    for s in range(2):
                        bank = slot((g, a, u, s))
                        if a == 0:
                            mm(bank[:, 0:2 * KEYS].rearrange("p (h k) -> p h k", h=2)[:, :, 0:S2], ones[:],
                               bc(mrow[:, g * NB + b, :], 2), start=True, stop=False, skip_group_check=True)
                        for j in range(2):
                            out = bank[:, j * KEYS:(j + 1) * KEYS]
                            if a == 0:
                                last = mm(out, four(g_s[q % 2][:, 2 * s + j, :])[:, b, :], kvT[g][:, b, :], start=False,
                                          stop=True, skip_group_check=True)
                            else:
                                rows, p = slice(HD * s, HD * s + HD), (4 * q + s + 2 * j) // 2
                                last = mm(out, four(xq_s[:, p, :])[rows, b, :], xk_s[rows, p, b, :], start=True,
                                          stop=True)
                        last.then_inc(s_full, 1)

                def turn(u):
                    n = unit_no(g, a, u)
                    pe.wait_ge(n_done, n + 1)
                    if n:
                        pe.wait_ge(pc_done, n)
                        pe.wait_ge(pl_done, n)
                    for h in range(4):
                        tr(ps[3][0:S2, h * S:(h + 1) * S], P[n % 3][:, h, 0:S2], ident)
                        last = tr(ps[4][:, h * S:(h + 1) * S], P[n % 3][:, h, S2:KEYS], ident)
                    last.then_inc(t_full, 1)

                def weigh(u):
                    n, b = unit_no(g, a, u), u % 4
                    pe.wait_ge(pc_done, n + 1)
                    pe.wait_ge(pl_done, n + 1)
                    if n:
                        pe.wait_ge(ue_done, n)
                    mm(ps[5][:], kvc[g][:, b, :], ptc[n % 2][0:S2, :], start=True, stop=False)
                    mm(ps[5][:], kvl[g][:, b, :], ptl[n % 2], start=False, stop=True).then_inc(u_full, 1)

                def project(q):
                    pe.wait_ge(ue_done, unit_no(g, a, 4 * q + 3) + 1)
                    if q == 0:
                        output_free(g, (2, 5)[a])
                    for j in range(4):
                        h = 4 * q + (j if a == 0 else (0, 2, 1, 3)[j])
                        last = mm(OUT[:], fb[:, h * D:(h + 1) * D], us[:, j].rearrange("p b s -> p (b s)"),
                                  start=(q == 0 and j == 0), stop=(q == units // 4 - 1 and j == 3))
                    last.then_inc(bo_full, 1)

                if a == 0 and g == 0:
                    for n in range(4):
                        q_fold(0, n)
                        yield
                for i in range(units + 4):
                    if a == 0 and i + 4 < units:
                        q_fold(g, i + 4)
                    if a == 0 and g == 0 and i >= units:
                        q_fold(1, i - units)
                    if i < units:
                        scores(i)
                    yield
                    if 2 <= i < units + 2:
                        turn(i - 2)
                    yield
                    if 3 <= i < units + 3:
                        if i == 3:
                            pe.wait_ge(kc_ok[g], a + 1)
                            pe.wait_ge(kl_ok[g], a + 1)
                        weigh(i - 3)
                    if i >= 4 and (i - 4) % 4 == 3:
                        project((i - 4) // 4)
                    yield

            def main2(g):
                if g == 0:
                    pe.wait_ge(m_ok, 1)
                    pe.wait_ge(fold_out, (2 * LH0 + LH1) // 4)
                yield from attention(g, 0)

            def main3(g):
                hh = h_hi[g][:], h_lo[g][:]
                n0 = g * (PAIRS + 1)

                def hidden(i):
                    n = n0 + i
                    if n >= 2:
                        pe.wait_ge(mo_si, n - 1)
                        pe.wait_ge(mo_tu, n - 1)
                    m = 128 if i < PAIRS else EI
                    wg = moe("wg", i * 128, 128) if i < PAIRS else moe("wg_s")
                    wu = moe("wu", i * 128, 128) if i < PAIRS else moe("wu_s")
                    mm3(ps[n % 2][0:m, :], wg, hh)
                    mm3(ps[2 + n % 2][0:m, :], wu, hh).then_inc(mo_gu, 1)

                def spread(i):
                    n = g * PAIRS + i
                    if i == 0:
                        pe.wait_ge(mo_w3[g], 1)
                        if g == 0:
                            pe.wait_ge(d_sel, 16)
                    if n >= 2:
                        pe.wait_ge(mo_a, n - 1)
                    mm(ps[4 + i % 2][:], sel[:, i * 128:(i + 1) * 128], w3b[g], start=True, stop=True)\
                        .then_inc(mo_wb, 1)

                def down(i):
                    if i < PAIRS:
                        pe.wait_ge(mo_a, g * PAIRS + i + 1)
                    else:
                        pe.wait_ge(mo_tu, n0 + i + 1)
                    if i == 0:
                        output_free(g, 3)
                        pe.wait_ge(d_raw, 32)
                        mm(OUT[:], r_("bd3")[0:96, :], w3f[g], start=True, stop=False)
                    m = 128 if i < PAIRS else EI
                    w = r_("wd", i * D, D) if i < PAIRS else r_("wd_s")[0:EI, :]
                    mm(OUT[:], w, av[(n0 + i) % 3][0:m, :], start=False, stop=(i == PAIRS)).then_inc(mo_dn, 1)

                pe.wait_ge(h_ok[g], 3)
                if g == 0:
                    pe.wait_ge(w_split, CH)
                    pe.wait_ge(u_full, unit_no(1, 0, UNITS[0] - 1) + 1)
                hidden(0)
                hidden(1)
                for i in range(PAIRS + 3):
                    if 2 <= i <= PAIRS:
                        hidden(i)
                    yield
                    if i < PAIRS:
                        spread(i)
                    if i >= 2:
                        down(i - 2)
                    yield

            def main4(g):
                pe.wait_ge(h_ok[g], 4)
                pe.wait_ge(w_split, 2 * CH)
                if g == 0:
                    pe.wait_ge(tern_sum, 1)
                    mm(ps[5][:, 0:2], meanm, wabs, start=True, stop=True).then_inc(tern_all, 1)
                hh = h_hi[g][:], h_lo[g][:]
                hb = four(hh[0]), four(hh[1])
                for n in range(2 * NB):
                    b, half = n // 2, n % 2
                    if n >= 4:
                        pe.wait_ge(re_vs, g * 2 * NB + n - 3)
                    mm3(ps[n % 4][:], (hb[0][:, b], hb[1][:, b]), ret("rv", half * 512, 512)).then_inc(re_v, 1)
                    yield

                def project(i):
                    n = g * RH + i
                    p, k = i // 2, "qk"[i % 2]
                    if i == 0:
                        pe.wait_ge(re_vs, (g + 1) * 2 * NB)
                    elif i >= 2:
                        pe.wait_ge(re_t, 3 * (n - 2) + 3)
                    mm3(ps[3 * i % 4][:], ret(f"r{k}", 2 * p * 128, 128), hh).then_inc(re_p, 1)
                    if i:
                        pe.wait_ge(re_t, 3 * (n - 1) + 1)
                        pe.wait_ge(re_pas, 2 * (n - 1) + 1)
                    mm3(ps[(3 * i + 1) % 4][:], ret(f"r{k}", (2 * p + 1) * 128, 128), hh).then_inc(re_p, 1)
                    if i:
                        pe.wait_ge(re_t, 3 * (n - 1) + 2)
                        pe.wait_ge(re_pas, 2 * (n - 1) + 2)
                    mm3(ps[(3 * i + 2) % 4][:], ret(f"r{k}_swp", p * 128, 128), hh).then_inc(re_p, 1)

                def decay(p, h):
                    n = g * RH + 2 * p + h
                    if h == 0:
                        pe.wait_ge(re_s, g * RH + 2 * p + 2)
                        pe.wait_ge(re_pas, 2 * (g * RH + 2 * p + 2))
                    if n >= 2:
                        pe.wait_ge(re_as, n - 1)
                    if n < 2:
                        pe.wait_ge(tern_ok, 1)
                    t = r_qk[p % 2]
                    for b in range(NB):
                        last = mm(ps[4 + h][:, b * S:(b + 1) * S], four(t[:, h])[:, b], four(t[:, 2 + h])[:, b],
                                  start=True, stop=True)
                    last.then_inc(re_a, 1)

                def mix(p, h):
                    n = g * RH + 2 * p + h
                    pe.wait_ge(re_as, n + 1)
                    if p == 0 and h == 0:
                        output_free(g, 4)
                    for b in range(NB):
                        c = (2 * p + h) * D
                        last = mm(OUT[:, b * S:(b + 1) * S], r_v[:, b, c:c + D], r_a[n % 2][:, b, :],
                                  start=(p == 0 and h == 0 and b == 0), stop=(p == RH // 2 - 1 and h == 1),
                                  skip_group_check=True)
                    last.then_inc(re_o, 1)

                for i in range(2):
                    project(i)
                    yield
                for p in range(RH // 2):
                    for h in range(2):
                        if p + 1 < RH // 2:
                            project(2 * p + 2 + h)
                        yield
                        n = 2 * p + h
                        if n == RH - 1:
                            decay(p, h)
                        elif n:
                            mix(*divmod(n - 1, 2))
                        yield
                        if n == RH - 1:
                            mix(*divmod(n - 1, 2))
                        else:
                            decay(p, h)
                        yield
                mix(RH // 2 - 1, 1)
                yield

            def main5(g):
                pe.wait_ge(h_ok[g], 5)
                if g == 0:
                    pe.wait_ge(xw_lo, 2)
                else:
                    pe.wait_ge(s_free, exp_of(unit_no(1, 1, 0) - 1))
                hh = h_hi[g][:], h_lo[g][:]
                for r in range(16):
                    p, kind = r // 4, r % 4
                    if r >= 3:
                        before, p0 = (r - 3) % 4, (r - 3) // 4
                        if before == 0:
                            pe.wait_ge(xa_q, 4 * g + p0 + 1)
                        elif before == 3:
                            pe.wait_ge(xa_kl, 4 * g + p0 + 1)
                        else:
                            pe.wait_ge(xa_kx, 8 * g + 2 * p0 + before)
                    bank = ps[r % 3]
                    if kind in (0, 3):
                        last = mm3(bank[:], xw(("xq", "xk")[kind // 3], p * 128, 128), hh)
                    else:
                        last = mm(bank[:, 0:NB * S2], x_(("xk", "xks")[kind - 1], p * 128, 128),
                                  kvT[g][:, :, 0:S2], start=True, stop=True)
                    last.then_inc(xa_full, 1)
                    yield
                pe.wait_ge(xa_kl, 4 * (g + 1))
                pe.wait_ge(xa_kt, 4 * (g + 1))
                yield from attention(g, 1)

            def main6(g):
                pe.wait_ge(h_ok[g], 6)
                if g:
                    pe.wait_ge(fx_in, 1)
                for b in range(NB):
                    last = tr(ps[5][:, b * D:(b + 1) * D], four(xT[g][:])[:, b, :], ident)
                last.then_inc(fx_t, 1)
                for j in range(4):
                    if g:
                        pe.wait_ge(ff_g, j + 1)
                    mm(ps[j][:], f_("up", j * 128, 128), hf[g][:], start=True, stop=True).then_inc(ff_up, 1)
                    yield
                for j in range(4):
                    pe.wait_ge(ff_g, 4 * g + j + 1)
                    if j == 0:
                        output_free(g, 6)
                        if g:
                            pe.wait_ge(fx_out, 1)
                    for b in range(NB):
                        last = mm(OUT[:, b * D:(b + 1) * D], four(f_g[:, j, :])[:, b, :], f_("down", j * 128, 128),
                                  start=(j == 0 and b == 0), stop=(j == 3), skip_group_check=True)
                    if j == 3:
                        last.then_inc(ff_dn, 1)
                    if j == 2:
                        pe.wait_ge(ff_sum, g + 1)
                        if g:
                            pe.wait_ge(f_ve, 1)
                        for b in range(NB):
                            last = mm(ps[4][:, b:b + 1], four(f_sq[:, 0, :])[:, b, :], meanm[:, 0:1], start=True,
                                      stop=True)
                        last.then_inc(ff_ms, 1)
                    yield
                yield
                yield

            run(folds, context, [None, main1, main2, main3, main4, main5, main6],
                [None, chain1, chain2, chain3, chain4, chain5, chain6])

        @block_.vector
        def _(dve):
            V = nc.vector
            count = [0]

            def link(ins):
                count[0] += 1
                ins.then_inc(v_link, 1)
                dve.wait_ge(v_link, count[0])

            def stats(src, st, ag):
                for b in range(NB):
                    last = V.bn_stats(st[:, 6 * b:6 * b + 6], src[:, b, :])
                link(last)
                for b in range(NB):
                    last = V.bn_aggr(ag[:, 2 * b:2 * b + 2], st[:, 6 * b:6 * b + 6])
                link(last)
                return ag.rearrange("p (b k) -> p k b", k=2)[:, 1, :]

            def normalise(dst, src, ag, rs_b):
                for b in range(NB):
                    last = V.tensor_scalar(dst[:, b, :], src[:, b, :], ag[:, 2 * b:2 * b + 1], rs_b[:, b:b + 1],
                                           ALU.subtract, ALU.mult)
                return last

            def norm(g, k, eps=EPS):
                yield
                dve.wait_ge(ln_tr[g], turned_no(k))
                V.tensor_scalar(ve[g][:, 0:NB], stats(four(CHAIN[:]), xst[g], xag[g]), eps, None, ALU.add)\
                    .then_inc(ln_ve[g], 1)
                yield
                yield
                dve.wait_ge(ln_pow[g], k)
                normalise(four(xc[g][:]), four(CHAIN[:]), xag[g], rs_t[g]).then_inc(ln_xc[g], 1)
                yield
                yield
                dve.wait_ge(ln_bc[g], k)

            def group_norm(g, k, src):
                w = D // 8
                yield
                dve.wait_ge(ln_mean[g], 1)
                V.tensor_tensor(xc[g][:], src, CHAIN[:], ALU.subtract).then_inc(ln_xc[g], 1)
                yield from idle(3)
                dve.wait_ge(ln_var[g], 1)
                V.tensor_scalar(ve[g][:, 0:NB * w], CHAIN[:, 0:NB * w], EPS, None, ALU.add).then_inc(ln_ve[g], 1)
                yield from idle(8)
                dve.wait_ge(ln_pow[g], k)
                V.tensor_copy(sq[g][:].rearrange("p (k e) -> p k e", e=D // w),
                              rs_t[g][:, 0:NB * w].rearrange("p (k o) -> p k o", o=1).to_broadcast(
                                  [128, NB * w, D // w])).then_inc(gn_ex[g], 1)
                yield from idle(2)
                dve.wait_ge(ln_bc[g], k)

            def plain_norm(g, k, n):
                yield from norm(g, k)
                yield
                dve.wait_ge(x_hi[g], n)
                V.tensor_tensor(h_lo[g][:], CHAIN[:], h_hi[g][:].bitcast(F32), ALU.subtract).then_inc(h_ok[g], 1)
                yield

            def twice_norm(g, k, gk, shift):
                yield from norm(g, k, eps=EPS * EPS / (1 + EPS))
                link(V.tensor_scalar(hf[g][:], CHAIN[:], gk, shift, ALU.mult, ALU.add))
                V.tensor_copy(kvT[g][:, :, S2:KEYS], four(hf[g][:]))
                link(V.tensor_copy(h_hi[g][:], hf[g][:]))
                V.tensor_tensor(h_lo[g][:], hf[g][:], h_hi[g][:].bitcast(F32), ALU.subtract).then_inc(h_ok[g], 1)
                yield

            def context_keys(g, a):
                V.tensor_scalar(kvT[g][:, :, 0:S2], cT[g][:], v_(f"g_x{a}"), v_(f"b_x{a}"), ALU.mult, ALU.add)\
                    .then_inc(ckv_ok[g], 1)

            def chain1(g):
                dve.wait_ge(d_x[g], 16)
                V.tensor_scalar(xrs[g], stats(four(hf[g][:]), xst[g], xag[g]), EPS, None, ALU.add)\
                    .then_inc(x_ve[g], 1)
                yield
                dve.wait_ge(xt_full[g], 1)
                V.tensor_copy(xT[g][:], CHAIN[:]).then_inc(ln_x[g], 1)
                yield
                dve.wait_ge(x_pow[g], 1)
                normalise(four(xc[g][:]), four(hf[g][:]), xag[g], xrs[g]).then_inc(xn_ok[g], 1)
                yield
                dve.wait_ge(d_c[g], 16)
                V.tensor_scalar(crs[g], stats(kvc[g][:], bnst[g], bnag[g]), EPS, None, ALU.add).then_inc(c_ve[g], 1)
                yield
                yield
                dve.wait_ge(x_hi[g], 1)
                V.tensor_tensor(h_lo[g][:], CHAIN[:], h_hi[g][:].bitcast(F32), ALU.subtract).then_inc(h_ok[g], 1)
                yield

            def context(g):
                dve.wait_ge(c_pow[g], 1)
                normalise(kvc[g], kvc[g], bnag[g], crs[g]).then_inc(cn_ok[g], 1)
                yield
                yield
                dve.wait_ge(ct_full[g], 1)
                link(V.tensor_copy(cT[g][:], CHAIN[:].rearrange("p (b k) -> p b k", b=NB)[:, :, 0:S2]))
                context_keys(g, 0)
                yield
                yield
                yield

            def chain2(g):
                dve.wait_ge(la_full, ROUNDS * (g + 1))
                V.scalar_tensor_tensor(out=xT[g][:], in0=LBANK[g][8][:], scalar=v_("bo"), in1=xT[g][:], op0=ALU.add,
                                       op1=ALU.add).then_inc(ln_x[g], 1)
                yield
                yield from twice_norm(g, 1, gk0, v_("b_l0"))
                yield
                yield

            def chain3(g):
                dve.wait_ge(bo_full, quad_no(g, 0, LH0 // 4 - 1) + 1)
                V.tensor_copy(hf[g][:], OUT[:]).then_inc(ln_x[g], 1)
                yield
                yield from norm(g, 2)
                link(V.tensor_scalar(hf[g][:], CHAIN[:], v_("g_o0"), v_("b_o0"), ALU.mult, ALU.add))
                V.tensor_tensor(xT[g][:], hf[g][:], xT[g][:], ALU.add).then_inc(ln_x[g], 1)
                yield
                yield from plain_norm(g, 3, 2)
                yield
                dve.wait_ge(mo_log[g], 1)
                V.tensor_tensor(lg[g], CHAIN[:, 0:NB * E].rearrange("p (b e) -> p b e", b=NB), bc(c_("br"), NB),
                                ALU.add).then_inc(mo_lg[g], 1)
                yield
                yield
                dve.wait_ge(mo_sig[g], 1)
                for b in range(NB):
                    last = V.max(top[g][:, 8 * b:8 * b + 8], aff[g][:, b, :])
                link(last)
                for b in range(NB):
                    V.match_replace(rep[g][:, b, :], top[g][:, 8 * b:8 * b + 8], aff[g][:, b, :], 0.0)
                link(V.tensor_reduce(tsum[g], top[g].rearrange("p (b k) -> p b k", b=NB), AX_X, ALU.add))
                link(V.tensor_scalar(tsum[g], tsum[g], 1e-9, None, ALU.add))
                V.tensor_tensor(wn[g], aff[g], rep[g], ALU.subtract)
                link(V.reciprocal(tsum[g], tsum[g]))
                share = tsum[g].rearrange("p (b o) -> p b o", o=1).to_broadcast([128, NB, E])
                link(V.tensor_tensor(wn[g], wn[g], share, ALU.mult))
                for k in range(3):
                    link(V.tensor_copy(wpart[:], wn[g]))
                    last = V.tensor_copy(wcat[g][:, :, k * E:(k + 1) * E], wpart[:])
                    if k < 2:
                        link(V.tensor_tensor(wn[g], wn[g], wpart[:], ALU.subtract))
                last.then_inc(mo_w[g], 1)
                yield from idle(4)
                dve.wait_ge(mo_wt[g], 1)
                link(V.tensor_copy(w3f[g], CHAIN[0:96, :]))
                V.tensor_copy(w3b[g], w3f[g]).then_inc(mo_w3[g], 1)
                yield

            def chain4(g):
                dve.wait_ge(mo_dn, (g + 1) * (PAIRS + 1))
                V.scalar_tensor_tensor(out=xT[g][:], in0=OUT[:], scalar=v_("bd_s"), in1=xT[g][:], op0=ALU.add,
                                       op1=ALU.add).then_inc(ln_x[g], 1)
                yield
                yield from plain_norm(g, 4, 3)

            def chain5(g):
                dve.wait_ge(re_o, (g + 1) * RH)
                V.tensor_copy(hf[g][:], OUT[:]).then_inc(ln_x[g], 1)
                context_keys(g, 1)
                yield
                yield from group_norm(g, 5, hf[g][:])
                link(V.scalar_tensor_tensor(out=hf[g][:], in0=xc[g][:], scalar=v_("gnw"), in1=CHAIN[:], op0=ALU.mult,
                                            op1=ALU.mult))
                V.scalar_tensor_tensor(out=xT[g][:], in0=hf[g][:], scalar=v_("gnb"), in1=xT[g][:], op0=ALU.add,
                                       op1=ALU.add).then_inc(ln_x[g], 1)
                yield
                yield from twice_norm(g, 6, gk1, v_("b_l1"))
                yield
                yield
                yield

            def chain6(g):
                dve.wait_ge(bo_full, quad_no(g, 1, LH1 // 4 - 1) + 1)
                V.tensor_tensor(xT[g][:], OUT[:], xT[g][:], ALU.add).then_inc(ln_x[g], 1)
                yield
                yield
                dve.wait_ge(ln_tr[g], turned_no(7))
                var = stats(four(CHAIN[:]), xst[g], xag[g])
                V.tensor_copy(ve[g][:, 0:NB], var)
                V.tensor_scalar(ve[g][:, NB:2 * NB], var, EPS, None, ALU.add).then_inc(ln_ve[g], 1)
                yield
                yield
                dve.wait_ge(f_root, g + 1)
                link(V.scalar_tensor_tensor(out=rs_t[g][:, 0:NB], in0=rs_t[g][:, NB:2 * NB], scalar=1e-8,
                                            in1=rs_t[g][:, 0:NB], op0=ALU.mult, op1=ALU.add))
                link(V.reciprocal(rs_t[g][:, 0:NB], rs_t[g][:, 0:NB]))
                normalise(four(xc[g][:]), four(CHAIN[:]), xag[g], rs_t[g]).then_inc(ln_xc[g], 1)
                yield
                yield
                dve.wait_ge(ln_bc[g], 7)
                V.tensor_copy(hf[g][:], CHAIN[:]).then_inc(h_ok[g], 1)
                yield

            def heads(t, n):
                c = n // 2 % 2 * 1024
                return t[:, c:c + 1024].rearrange("p (j two d) -> p two j d", two=2, d=D)[:, n % 2]

            def folds():
                V.memset(half_n, -0.5)
                V.memset(half_p, 0.5).then_inc(half_ok, 1)
                V.memset(ones[:], 1.0)
                link(V.memset(mrow[:], 0.0))
                V.memset(linear[0][6][:, :, D:D + 1], 1.0)
                V.memset(linear[1][6][:, :, D:D + 1], 1.0)
                yield
                dve.wait_ge(d_con, 16)
                V.tensor_scalar(bq1, v_("bq"), 1.0, None, ALU.add)
                V.tensor_scalar(gk0, v_("g_l0"), (1 + EPS) ** -0.5, None, ALU.mult)
                V.tensor_scalar(gk1, v_("g_l1"), (1 + EPS) ** -0.5, None, ALU.mult)
                V.tensor_scalar(block_mean, block, 0.125, None, ALU.mult)
                link(V.tensor_scalar(head8, c_("head"), 0.125, None, ALU.mult))
                dve.wait_ge(d_lin, 16)
                hi, lo = wa[:, 2 * QF:2 * QF + NLIN], wa[:, 2 * QF + NLIN:2 * QF + 2 * NLIN]
                link(V.tensor_copy(hi, stage[:, 0:NLIN]))
                V.tensor_tensor(lo, stage[:, 0:NLIN], hi.bitcast(F32), ALU.subtract).then_inc(l_split, 1)
                yield
                for n in range((2 * LH0 + LH1) // 4):
                    if n < 4:
                        dve.wait_ge(fold_hi, n + 1)
                        V.scalar_tensor_tensor(out=heads(fa_lo, n), in0=ps[5][:].rearrange("p (j d) -> p j d", d=D),
                                               scalar=HD ** -0.5, in1=heads(fa_hi, n).bitcast(F32), op0=ALU.mult,
                                               op1=ALU.subtract).then_inc(fold_out, 1)
                    yield
                dve.wait_ge(d_m, 16)
                V.tensor_scalar(mrow[0:1], shaped(m8[:], B, S2), -MASKED, MASKED, ALU.mult, ALU.add).then_inc(m_ok, 1)

            def main1(g):
                q_z, q_m, q_f, k_z, k_m, k_f, v_1, kv_b, o_t, o_n = linear[g]
                bkv = c_("bkv")

                def bank(i):
                    dve.wait_ge(la_full, ROUNDS * g + i + 1)
                    return LBANK[g][i]

                yield
                t = bank(0)
                V.tensor_scalar(q_m, t[:], v_("bq"), 0.0, ALU.add, ALU.min).then_inc(la_min, 1)
                V.tensor_scalar(q_z, t[:], bq1, None, ALU.add).then_inc(la_read, 1)
                yield
                for i in range(2):
                    pv = bank(1 + i)[:].rearrange("p (b k e) -> p k b e", b=2, k=2)
                    V.tensor_tensor(k_z[:, 2 * i:2 * i + 2, :], pv[:, 0], bc(bkv[:, 0:D], 2), ALU.add)
                    V.tensor_tensor(v_1[:, 2 * i:2 * i + 2, 0:D], pv[:, 1], bc(bkv[:, D:2 * D], 2), ALU.add)\
                        .then_inc(la_read, 1)
                    if i == 0:
                        yield
                dve.wait_ge(la_read, (ROUNDS - 1) * g + 3)
                V.tensor_scalar(k_m, k_z, 0.0, None, ALU.min).then_inc(la_min, 1)
                yield
                dve.wait_ge(la_exp, 2 * g + 1)
                link(V.tensor_scalar(q_m, q_m, -1.0, 1.0, ALU.add, ALU.add))
                V.tensor_tensor(q_f, q_z, q_m, ALU.max).then_inc(la_qf, 1)
                yield
                dve.wait_ge(la_exp, 2 * g + 2)
                link(V.tensor_scalar(k_m, k_m, -1.0, 1.0, ALU.add, ALU.add))
                V.scalar_tensor_tensor(out=k_f, in0=k_z, scalar=1.0, in1=k_m, op0=ALU.add, op1=ALU.max)\
                    .then_inc(la_kf, 1)
                yield
                yield
                for i in range(2):
                    pv = bank(3 + i)[:, 0:2 * (D + 1)].rearrange("p (b e) -> p b e", b=2)
                    V.tensor_tensor(kv_b[:, 2 * i:2 * i + 2, 0:D], pv[:, :, 0:D], bc(block, 2), ALU.mult)
                    for j in range(2):
                        last = V.tensor_scalar(kv_b[:, 2 * i + j, D:D + 16], c_("head"), pv[:, j, D:D + 1], None,
                                               ALU.mult)
                    last.then_inc(la_read, 1)
                    yield
                yield
                ld = lden[g].rearrange("p (b h) -> p b h", b=NB)
                for i in range(2):
                    nd = bank(5 + i)[:, 0:2 * (D + 16)].rearrange("p (b e) -> p b e", b=2)
                    half = lden[g][:, 32 * i:32 * i + 32]
                    link(V.tensor_scalar(ld[:, 2 * i:2 * i + 2, :], nd[:, :, D:D + 16], 1e-6, None, ALU.add))
                    link(V.reciprocal(half, half))
                    for b in range(2 * i, 2 * i + 2):
                        last = V.tensor_tensor(
                            o_t[:, b, :].rearrange("p (h e) -> p h e", h=16),
                            nd[:, b % 2, 0:D].rearrange("p (h e) -> p h e", h=16),
                            ld[:, b, :].rearrange("p (h o) -> p h o", o=1).to_broadcast([128, 16, 8]), ALU.mult)
                    last.then_inc(la_read, 1)
                    yield
                yield
                V.tensor_copy(o_n, bank(7)[:]).then_inc(la_read, 1)
                yield
                yield

            def attention(g, a):
                units = UNITS[a]

                def top_(u):
                    n = unit_no(g, a, u)
                    for s in range(2):
                        r = slots[g, a, u, s]
                        dve.wait_ge(s_full, r + 1)
                        if n >= 3 and s == 0:
                            dve.wait_ge(s_free, exp_of(n - 3))
                        o = 4 * (n % 3) + 2 * s
                        V.tensor_reduce(nm[:, o:o + 2], ps[r % NS][:, 0:2 * KEYS].rearrange("p (h k) -> p h k", h=2),
                                        AX_X, ALU.max, negate=True).then_inc(m_done, 1)

                def recip(u):
                    n = unit_no(g, a, u)
                    o = 4 * (n % 3)
                    dve.wait_ge(s_free, exp_of(n))
                    if n >= 3:
                        dve.wait_ge(n_done, n - 2)
                    V.reciprocal(rs[:, o:o + 4], sm[:, o:o + 4]).then_inc(r_done, 1)

                def turned(u):
                    n = unit_no(g, a, u)
                    dve.wait_ge(t_full, n + 1)
                    if n >= 2:
                        dve.wait_ge(u_full, n - 1)
                    V.tensor_copy(ptl[n % 2], ps[4][:]).then_inc(pl_done, 1)

                def weighed(u):
                    n = unit_no(g, a, u)
                    q, b = u // 4, u % 4
                    dve.wait_ge(u_full, n + 1)
                    if b == 0 and quad_no(g, a, q) >= 1:
                        dve.wait_ge(bo_full, quad_no(g, a, q))
                    V.tensor_copy(us[:, :, b, :], four(ps[5][:])).then_inc(ue_done, 1)

                if a == 0 and g == 0:
                    yield from idle(4)
                for i in range(units + 4):
                    if i < units:
                        top_(i)
                    if 1 <= i <= units:
                        recip(i - 1)
                    yield
                    if 2 <= i < units + 2:
                        turned(i - 2)
                    yield
                    if 3 <= i < units + 3:
                        weighed(i - 3)
                    yield

            def main2(g):
                yield from attention(g, 0)

            def main3(g):
                n0 = g * (PAIRS + 1)
                for i in range(PAIRS + 3):
                    if i > PAIRS:
                        yield
                        yield
                        continue
                    n = n0 + i
                    m = 128 if i < PAIRS else EI
                    bu = v_("bu", i) if i < PAIRS else v_("bu_s")
                    dve.wait_ge(mo_si, n + 1)
                    dst = tu[n % 2] if i < PAIRS else av[n % 3]
                    if i == PAIRS:
                        dve.wait_ge(mo_dn, n - 2)
                    ins = V.scalar_tensor_tensor(out=dst[0:m, :], in0=ps[2 + n % 2][0:m, :], scalar=bu[0:m, :],
                                                 in1=si[n % 2][0:m, :], op0=ALU.add, op1=ALU.mult)
                    ins.then_inc(mo_tu, 1)
                    yield
                    if i < PAIRS:
                        dve.wait_ge(mo_tu, n + 1)
                        dve.wait_ge(mo_wb, g * PAIRS + i + 1)
                        if n >= 3:
                            dve.wait_ge(mo_dn, n - 2)
                        V.tensor_tensor(av[n % 3], tu[n % 2], ps[4 + i % 2][:], ALU.mult).then_inc(mo_a, 1)
                    if g and i in (8, 9):
                        dve.wait_ge(d_ffn, 16)
                        ins = V.tensor_reduce(wabs[:, i - 8:i - 7], f_(("up", "down")[i - 8]), AX_X, ALU.add,
                                              apply_absolute_value=True)
                        if i == 9:
                            ins.then_inc(tern_sum, 1)
                    yield

            def ternary():
                yield
                dve.wait_ge(tern_all, 1)
                V.tensor_scalar(thr, ps[5][:, 0:2], 0.5 / DFF, None, ALU.mult)
                link(V.tensor_scalar(thr_n, ps[5][:, 0:2], -0.5 / DFF, None, ALU.mult))
                yield
                t1, t2 = stage[:, 0:DFF], stage[:, DFF:2 * DFF]
                for k, name in enumerate(("up", "down")):
                    w = f_(name)
                    V.tensor_scalar(t1, w, thr[:, k:k + 1], None, ALU.is_gt)
                    link(V.tensor_scalar(t2, w, thr_n[:, k:k + 1], None, ALU.is_lt))
                    link(V.tensor_tensor(t1, t1, t2, ALU.subtract))
                    yield
                    link(V.tensor_tensor(t1, t1, w, ALU.subtract))
                    last = V.tensor_tensor(w, t1, w, ALU.add)
                    if k == 0:
                        link(last)
                    else:
                        last.then_inc(tern_ok, 1)
                    yield

            def main4(g):
                cos, sin = c_("cosA"), c_("sinA")

                def rotate(i):
                    n = g * RH + i
                    if n >= 2:
                        dve.wait_ge(re_s, n - 1)
                    for h in range(2):
                        rows = slice(ROT * h, ROT * h + ROT)
                        dve.wait_ge(re_p, 3 * n + h + 1)
                        V.tensor_tensor(four(r_t1[n % 2])[rows], four(ps[(3 * i + h) % 4][:])[rows], bc(cos, NB)[rows],
                                        ALU.mult).then_inc(re_t, 1)
                    dve.wait_ge(re_p, 3 * n + 3)
                    V.tensor_tensor(four(r_t2[n % 2]), four(ps[(3 * i + 2) % 4][:]), bc(sin, NB), ALU.mult)\
                        .then_inc(re_t, 1)
                    dve.wait_ge(re_t, 3 * n + 3)
                    V.tensor_tensor(r_t1[n % 2], r_t1[n % 2], r_t2[n % 2], ALU.add).then_inc(re_t3, 1)

                def decayed(p, h):
                    n = g * RH + 2 * p + h
                    dve.wait_ge(re_a, n + 1)
                    if n >= 2:
                        dve.wait_ge(re_o, n - 1)
                    V.tensor_tensor(r_a[n % 2], four(ps[4 + h][:]), bc(c_("decay"), 4), ALU.mult).then_inc(re_as, 1)

                if g:
                    yield from idle(2 * NB)
                else:
                    yield from ternary()
                    yield from idle(2)
                for i in range(2):
                    rotate(i)
                    yield
                for p in range(RH // 2):
                    for h in range(2):
                        if p + 1 < RH // 2:
                            rotate(2 * p + 2 + h)
                        yield
                        yield
                        decayed(p, h)
                        yield
                yield

            def main5(g):
                cos, sin = c_("cosX"), c_("sinX")
                for p in range(4):
                    yield
                    for k, (o, f) in enumerate(((xt1[p % 2], cos), (xt2[p % 2], sin))):
                        r = 4 * p + 1 + k
                        dve.wait_ge(xa_full, 16 * g + r + 1)
                        if p >= 2:
                            dve.wait_ge(xa_kt, 4 * g + p - 1)
                        V.tensor_tensor(o[:, :, 0:S2], ps[r % 3][:, 0:NB * S2].rearrange("p (b k) -> p b k", b=NB),
                                        bc(f, NB), ALU.mult).then_inc(xa_kx, 1)
                        yield
                    yield
                yield from attention(g, 1)

            def main6(g):
                yield
                dve.wait_ge(fx_t, g + 1)
                V.tensor_copy(x_out[g], four(ps[5][:])).then_inc(fx_in, 1)
                yield from idle(3)
                if g:
                    dve.wait_ge(ff_ms, 1)
                for j in range(1, 4):
                    if j > 1:
                        dve.wait_ge(ff_g, 4 * g + j + 1)
                        link(V.tensor_tensor(f_sq[:, j, :], f_g[:, j, :], f_g[:, j, :], ALU.mult))
                    else:
                        dve.wait_ge(ff_sq, 2 * g + 2)
                    ins = V.tensor_tensor(f_sq[:, 0, :], f_sq[:, 0, :], f_sq[:, j, :], ALU.add)
                    if j < 3:
                        link(ins)
                    else:
                        ins.then_inc(ff_sum, 1)
                    if j > 1:
                        yield
                yield
                dve.wait_ge(ff_ms, g + 1)
                V.tensor_scalar(ve[g][:, 0:NB], ps[4][:, 0:NB], 128.0 / DFF, None, ALU.mult).then_inc(f_ve, 1)
                yield
                yield
                dve.wait_ge(f_pow, g + 1)
                link(V.tensor_scalar(rs_t[g][:, 0:NB], rs_t[g][:, 0:NB], 1e-8, None, ALU.add))
                link(V.reciprocal(rs_t[g][:, 0:NB], rs_t[g][:, 0:NB]))
                dve.wait_ge(ff_dn, g + 1)
                for b in range(NB):
                    last = V.scalar_tensor_tensor(out=x_out[g][:, b, :], in0=OUT[:, b * D:(b + 1) * D],
                                                  scalar=rs_t[g][:, b:b + 1], in1=x_out[g][:, b, :], op0=ALU.mult,
                                                  op1=ALU.add)
                last.then_inc(fx_out, 1)

            run(folds, context, [None, main1, main2, main3, main4, main5, main6],
                [None, chain1, chain2, chain3, chain4, chain5, chain6])

        @block_.scalar
        def _(act):
            A = nc.scalar.activation

            def high_part(g, k):
                yield from idle(5)
                act.wait_ge(ln_bc[g], k)
                A(h_hi[g][:], CHAIN[:], ACT.Copy).then_inc(x_hi[g], 1)
                yield
                yield

            def group_norm(g, k):
                yield
                yield
                act.wait_ge(ln_xc[g], k)
                A(sq[g][:], xc[g][:], ACT.Square).then_inc(ln_sq[g], 1)
                yield from idle(12)

            def keys(g, k, n):
                if n == S2:
                    act.wait_ge(kc_full[g], k)
                    A(kvc[g][:], CHAIN[0:S2, :].rearrange("p (b d) -> p b d", b=NB), ACT.Copy).then_inc(kc_ok[g], 1)
                else:
                    act.wait_ge(kl_full[g], k)
                    A(kvl[g][:], four(CHAIN[:]), ACT.Copy).then_inc(kl_ok[g], 1)

            def chain1(g):
                yield from idle(4)
                act.wait_ge(xn_full[g], 1)
                A(h_hi[g][:], CHAIN[:], ACT.Copy).then_inc(x_hi[g], 1)
                yield from idle(2)

            def context(g):
                yield from idle(4)
                keys(g, 1, S2)
                yield

            def chain2(g):
                yield
                yield from idle(5)
                yield
                yield
                keys(g, 1, S)
                yield

            def chain3(g):
                yield
                yield from idle(5)
                yield
                yield from high_part(g, 3)
                yield from idle(2)
                act.wait_ge(mo_lg[g], 1)
                A(aff[g], lg[g], ACT.Sigmoid).then_inc(mo_sig[g], 1)
                yield from idle(6)

            def chain4(g):
                yield
                yield from high_part(g, 4)

            def chain5(g):
                yield
                yield from group_norm(g, 5)
                yield
                yield from idle(5)
                yield
                yield
                keys(g, 2, S2)
                yield
                yield
                keys(g, 2, S)
                yield

            def chain6(g):
                yield
                yield from idle(5)
                yield

            def high(k):
                n, w = (NMOE // CH, wb) if k < CH else (NRET // CH, wa)
                act.wait_ge(d_ring[k % RING], 16 * (k // RING + 1))
                o = k % RING * (NMOE // CH)
                A(w[:, k % CH * n:k % CH * n + n], stage[:, o:o + n], ACT.Copy).then_inc(w_hid, 1)

            def folds():
                act.dma_start(sel[:], sel_d).then_inc(d_sel, 16)
                yield
                yield
                for n in range((2 * LH0 + LH1) // 4):
                    c = n // 2 % 2 * 1024
                    out = (fa_hi if n < 4 else fb0 if n < 8 else fb1)[:, c:c + 1024]
                    out = out.rearrange("p (j two d) -> p two j d", two=2, d=D)[:, n % 2]
                    bank = ps[5][:].rearrange("p (j d) -> p j d", d=D)
                    act.wait_ge(fold_full, n + 1)
                    if n < 4:
                        A(out, bank, ACT.Copy, scale=HD ** -0.5).then_inc(fold_hi, 1)
                    else:
                        A(out, bank, ACT.Copy).then_inc(fold_out, 1)
                    yield

            def main1(g):
                q_z, q_m, q_f, k_z, k_m = linear[g][0:5]
                yield
                yield
                act.wait_ge(la_min, 2 * g + 1)
                A(q_m, q_m, ACT.Exp).then_inc(la_exp, 1)
                yield
                yield
                act.wait_ge(la_min, 2 * g + 2)
                A(k_m, k_m, ACT.Exp).then_inc(la_exp, 1)
                yield from idle(11)

            def attention(g, a):
                units = UNITS[a]

                def query(g, n):
                    r = slots[g, 0, "g", n]
                    act.wait_ge(s_full, r + 1)
                    A(g_s[n // 4 % 2][:, n % 4, :], ps[r % NS][:], ACT.Copy).then_inc(s_free, 1)

                def exps(u):
                    n = unit_no(g, a, u)
                    for s in range(2):
                        r = slots[g, a, u, s]
                        act.wait_ge(m_done, 2 * n + s + 1)
                        if s == 0 and n >= 3:
                            act.wait_ge(t_full, n - 2)
                            act.wait_ge(r_done, n - 2)
                        for j in range(2):
                            o = 4 * (n % 3) + 2 * s + j
                            last = A(P[n % 3][:, 2 * s + j, :], ps[r % NS][:, j * KEYS:(j + 1) * KEYS], ACT.Exp,
                                     bias=nm[:, o:o + 1], accum_out=sm[:, o:o + 1])
                        last.then_inc(s_free, 1)

                def turned(u):
                    n = unit_no(g, a, u)
                    act.wait_ge(t_full, n + 1)
                    if n >= 2:
                        act.wait_ge(u_full, n - 1)
                    A(ptc[n % 2][0:S2, :], ps[3][0:S2, :], ACT.Copy).then_inc(pc_done, 1)

                if a == 0 and g == 0:
                    for n in range(4):
                        query(0, n)
                        yield
                for i in range(units + 4):
                    if a == 0 and i + 4 < units:
                        query(g, i + 4)
                    if a == 0 and g == 0 and i >= units:
                        query(1, i - units)
                    if i < units:
                        exps(i)
                    yield
                    if 2 <= i < units + 2:
                        turned(i - 2)
                    yield
                    if a == 0 and g == 1 and 4 <= i < 4 + CH:
                        high(i - 4)
                    yield

            def main2(g):
                yield from attention(g, 0)

            def main3(g):
                n0 = g * (PAIRS + 1)
                for i in range(PAIRS + 3):
                    if i <= PAIRS:
                        n = n0 + i
                        m = 128 if i < PAIRS else EI
                        bg = v_("bg", i) if i < PAIRS else v_("bg_s")
                        act.wait_ge(mo_gu, n + 1)
                        if n >= 2:
                            act.wait_ge(mo_tu, n - 1)
                        A(si[n % 2][0:m, :], ps[n % 2][0:m, :], ACT.Silu, bias=bg[0:m, :]).then_inc(mo_si, 1)
                    yield
                    if g == 0 and 2 <= i < 2 + CH:
                        high(CH + i - 2)
                    yield

            def main4(g):
                for n in range(2 * NB):
                    act.wait_ge(re_v, g * 2 * NB + n + 1)
                    A(r_v[:, n // 2, n % 2 * 512:n % 2 * 512 + 512], ps[n % 4][:], ACT.Silu).then_inc(re_vs, 1)
                    yield

                def silus(i):
                    n = g * RH + i
                    t = r_qk[i // 2 % 2]
                    if i % 2 == 0 and n >= 4:
                        act.wait_ge(re_a, n - 2)
                    for h in range(2):
                        rows = slice(ROT * (1 - h), ROT * (1 - h) + ROT)
                        act.wait_ge(re_p, 3 * n + h + 1)
                        A(t[rows, 2 * (i % 2) + h, :], ps[(3 * i + h) % 4][rows, :], ACT.Silu).then_inc(re_pas, 1)
                    act.wait_ge(re_t3, n + 1)
                    for h in range(2):
                        rows = slice(ROT * h, ROT * h + ROT)
                        last = A(t[rows, 2 * (i % 2) + h, :], r_t1[n % 2][rows, :], ACT.Silu)
                    last.then_inc(re_s, 1)

                for i in range(2):
                    silus(i)
                    if g == 0:
                        if i == 0:
                            act.wait_ge(d_xat, 16)
                            act.wait_ge(mo_gu, G * (PAIRS + 1))
                        A(wb[:, i * 512:i * 512 + 512], x_(("xq", "xk")[i]), ACT.Copy).then_inc(xw_hi, 1)
                    yield
                for p in range(RH // 2):
                    for i in range(2):
                        if p + 1 < RH // 2:
                            silus(2 * p + 2 + i)
                        yield from idle(3)
                yield

            def main5(g):
                for p in range(4):
                    act.wait_ge(xa_full, 16 * g + 4 * p + 1)
                    A(xq_s[:, p, :], ps[4 * p % 3][:], ACT.Copy, scale=HD ** -0.5).then_inc(xa_q, 1)
                    yield from idle(3)
                    act.wait_ge(xa_full, 16 * g + 4 * p + 4)
                    A(xk_s[:, p, :, S2:KEYS], four(ps[(4 * p + 3) % 3][:]), ACT.Copy).then_inc(xa_kl, 1)
                    yield
                yield from attention(g, 1)

            def main6(g):
                for j in range(4):
                    act.wait_ge(ff_up, 4 * g + j + 1)
                    if g:
                        act.wait_ge(ff_dn, 1)
                    A(f_g[:, j, :], ps[j][:], ACT.Gelu).then_inc(ff_g, 1)
                    yield
                yield from idle(6)

            run(folds, context, [None, main1, main2, main3, main4, main5, main6],
                [None, chain1, chain2, chain3, chain4, chain5, chain6])

        @block_.gpsimd
        def _(pool):
            TT = nc.gpsimd.tensor_tensor

            def factor(g, k, w=1):
                yield from idle(2 if w == 1 else 5)
                pool.wait_ge(ln_ve[g], k)
                if w > 1:
                    for c in range(0, NB * w, w):
                        ins = TT(rs_t[g][:, c:c + w], ve[g][:, c:c + w], half_n[:, c:c + w], ALU.pow)
                        if c + w < NB * w:
                            yield
                            yield
                        else:
                            ins.then_inc(ln_pow[g], 1)
                    yield from idle(3)
                    return
                if k < 7:
                    TT(rs_t[g][:, 0:NB * w], ve[g][:, 0:NB * w], half_n[:, 0:NB * w], ALU.pow).then_inc(ln_pow[g], 1)
                else:
                    TT(rs_t[g][:, 0:2 * NB], ve[g][:, 0:2 * NB], half_p[:, 0:2 * NB], ALU.pow).then_inc(f_root, 1)
                yield from idle(3)

            def chain1(g):
                yield
                pool.wait_ge(x_ve[g], 1)
                if g == 0:
                    pool.wait_ge(half_ok, 1)
                TT(xrs[g], xrs[g], half_n[:, 0:NB], ALU.pow).then_inc(x_pow[g], 1)
                yield from idle(4)
                pool.wait_ge(c_ve[g], 1)
                TT(crs[g], crs[g], half_n[0:S2, 0:NB], ALU.pow).then_inc(c_pow[g], 1)
                yield

            def context(g):
                yield from idle(5)

            def chain2(g):
                yield
                yield from factor(g, 1)
                yield from idle(3)

            def chain3(g):
                yield
                yield from factor(g, 2)
                yield
                yield from factor(g, 3)
                yield from idle(10)

            def chain4(g):
                yield
                yield from factor(g, 4)
                yield from idle(2)

            def chain5(g):
                yield
                yield from factor(g, 5, w=16)
                yield
                yield from factor(g, 6)
                yield from idle(4)

            def chain6(g):
                yield
                yield from factor(g, 7)
                yield

            def low(k):
                n, w, size = (NMOE // CH, wb, NMOE) if k < CH else (NRET // CH, wa, NRET)
                o, c = k % RING * (NMOE // CH), k % CH * n
                pool.wait_ge(w_hid, k + 1)
                TT(w[:, size + c:size + c + n], stage[:, o:o + n], w[:, c:c + n].bitcast(F32), ALU.subtract)\
                    .then_inc(w_split, 1)

            def folds():
                yield from idle(12)

            def main1(g):
                yield from idle(15)

            def attention(g, a):
                if a == 0 and g == 0:
                    yield from idle(4)
                for i in range(UNITS[a] + 4):
                    if 1 <= i <= UNITS[a]:
                        n = unit_no(g, a, i - 1)
                        o = 4 * (n % 3)
                        pool.wait_ge(r_done, n + 1)
                        r = rs[:, o:o + 4].rearrange("p (h o) -> p h o", o=1).to_broadcast([128, 4, KEYS])
                        TT(P[n % 3], P[n % 3], r, ALU.mult).then_inc(n_done, 1)
                    yield
                    yield
                    if a == 0 and g == 1 and 4 <= i < 4 + CH:
                        low(i - 4)
                    yield

            def main2(g):
                yield from attention(g, 0)

            def main3(g):
                for i in range(PAIRS + 3):
                    yield
                    if g == 0 and 2 <= i < 2 + CH:
                        low(CH + i - 2)
                    yield

            def main4(g):
                yield from idle(2 * NB)
                for i in range(2):
                    if g == 0:
                        pool.wait_ge(xw_hi, i + 1)
                        TT(wb[:, 1024 + i * 512:1536 + i * 512], x_(("xq", "xk")[i]),
                           wb[:, i * 512:i * 512 + 512].bitcast(F32), ALU.subtract).then_inc(xw_lo, 1)
                    yield
                yield from idle(3 * RH + 1)

            def main5(g):
                for p in range(4):
                    yield from idle(2)
                    pool.wait_ge(xa_kx, 8 * g + 2 * p + 2)
                    TT(xk_s[:, p, :, 0:S2], xt1[p % 2][:, :, 0:S2], xt2[p % 2][:, :, 0:S2], ALU.add)\
                        .then_inc(xa_kt, 1)
                    yield from idle(2)
                yield from attention(g, 1)

            def main6(g):
                yield
                for j in range(2):
                    pool.wait_ge(ff_g, 4 * g + j + 1)
                    if g:
                        pool.wait_ge(ff_ms, 1)
                    TT(f_sq[:, j, :], f_g[:, j, :], f_g[:, j, :], ALU.mult).then_inc(ff_sq, 1)
                    yield
                yield from idle(5)
                pool.wait_ge(f_ve, g + 1)
                TT(rs_t[g][:, 0:NB], ve[g][:, 0:NB], half_p[:, 0:NB], ALU.pow).then_inc(f_pow, 1)
                yield from idle(2)

            run(folds, context, [None, main1, main2, main3, main4, main5, main6],
                [None, chain1, chain2, chain3, chain4, chain5, chain6])


def _constants():
    f = np.float32
    con = np.zeros((128, NCON), f)

    def put(name, a):
        lo, n = CON[name]
        con[:, lo:lo + n] = a
    i = np.arange(128)
    put("ident", np.eye(128))
    put("mean", np.full((128, 128), 1 / 128))
    put("block", (i[:, None] // 8 == i[None, :] // 8))
    put("head", (i[:, None] // 8 == np.arange(16)[None, :]))
    diff = i[:, None] - i[None, :]
    put("decay", np.where(diff >= 0, f(GAMMA) ** np.maximum(diff, 0).astype(f), 0))
    inv = (1.0 / 10000.0 ** (np.arange(0, ROT, 2, dtype=f) / f(ROT))).astype(f)
    ang = (np.arange(S, dtype=f)[None, :] * np.tile(np.repeat(inv, 2), 2)[:, None]).astype(f)
    put("cosA", np.cos(ang))
    put("sinA", np.sin(ang) * np.where(i % 2 == 0, -1, 1)[:, None])
    ang = (np.arange(S2, dtype=f)[None, :] * np.tile(inv, 4)[:, None]).astype(f)
    put("cosX", np.cos(ang))
    put("sinX", np.sin(ang) * np.where(i % HD < HD // 2, -1, 1)[:, None])
    sel = np.zeros((96, PAIRS * 128), f)
    for p in range(PAIRS):
        for m in range(128):
            for k in range(3):
                sel[k * E + 2 * p + m // EI, p * 128 + m] = 1
    return con, sel


def _layout(a):
    con, sel = _constants()
    f = np.float32

    def vec(name, v):
        lo = CON["vec"][0] + VEC[name][0]
        v = np.asarray(v)
        v = v.reshape(VEC[name][1], -1).T
        con[0:v.shape[0], lo:lo + v.shape[1]] = v
    for name, key in (("bq", "L0_attn_bq"), ("bo", "L0_attn_bo"), ("g_x0", "L0_xattn_g_x"), ("b_x0", "L0_xattn_b_x"),
                      ("g_l0", "L0_xattn_g_l"), ("b_l0", "L0_xattn_b_l"), ("g_o0", "L0_xattn_g_o"),
                      ("b_o0", "L0_xattn_b_o"), ("bd_s", "L0_ffn_bd_s"), ("gnw", "L1_attn_gn_weight"),
                      ("gnb", "L1_attn_gn_bias"), ("g_x1", "L1_xattn_gamma_x"), ("b_x1", "L1_xattn_beta_x"),
                      ("g_l1", "L1_xattn_gamma_l"), ("b_l1", "L1_xattn_beta_l"), ("bg", "L0_ffn_bg"),
                      ("bu", "L0_ffn_bu"), ("bg_s", "L0_ffn_bg_s"), ("bu_s", "L0_ffn_bu_s")):
        vec(name, a[key])
    lo, n = CON["bkv"]
    con[:, lo:lo + D] = a["L0_attn_bk"][None, :]
    con[:, lo + D:lo + n] = a["L0_attn_bv"][None, :]
    lo, n = CON["br"]
    con[:, lo:lo + n] = a["L0_ffn_br"][None, :]

    spl = {"lin": np.zeros((128, NLIN), f), "moe": np.zeros((128, NMOE), f), "ret": np.zeros((128, NRET), f)}

    def put(pack, table, name, w):
        lo, n = table[name]
        w = np.asarray(w).reshape(-1, n)
        pack[0:w.shape[0], lo:lo + n] = w
    put(spl["lin"], LIN, "wq", a["L0_attn_Wq"].T)
    put(spl["lin"], LIN, "wkv", np.concatenate([a["L0_attn_Wk"].T, a["L0_attn_Wv"].T], axis=1))
    put(spl["moe"], MOE, "wr", a["L0_ffn_Wr"])
    put(spl["moe"], MOE, "wg", a["L0_ffn_Wg"].transpose(1, 0, 2).reshape(D, -1))
    put(spl["moe"], MOE, "wu", a["L0_ffn_Wu"].transpose(1, 0, 2).reshape(D, -1))
    put(spl["moe"], MOE, "wg_s", a["L0_ffn_Wg_s"])
    put(spl["moe"], MOE, "wu_s", a["L0_ffn_Wu_s"])
    for k in "QK":
        w = a[f"L1_attn_W_{k}"].reshape(D, RH, D)
        rot, pas = w[:, :, 0:ROT], w[:, :, ROT:]
        both = np.stack([np.concatenate([rot, pas] if h % 2 == 0 else [pas, rot], axis=2)[:, h] for h in range(RH)],
                        axis=1)
        put(spl["ret"], RET, f"r{k.lower()}", both.reshape(D, -1))
        put(spl["ret"], RET, f"r{k.lower()}_swp", rot[:, :, np.arange(ROT) ^ 1].reshape(D, -1))
    put(spl["ret"], RET, "rv", a["L1_attn_W_V"])

    raw, xat, ffn = np.zeros((128, NRAW), f), np.zeros((128, NXAT), f), np.zeros((128, NFFN), f)
    put(raw, RAW, "woT", a["L0_attn_Wo"].T)
    put(raw, RAW, "wd", a["L0_ffn_Wd"].reshape(PAIRS, 128, D).transpose(1, 0, 2).reshape(128, -1))
    put(raw, RAW, "wd_s", a["L0_ffn_Wd_s"])
    put(raw, RAW, "bd3", np.concatenate([a["L0_ffn_bd"]] * 3, axis=0))
    inner = LH1 * HD
    wk = a["L1_xattn_Wkv"][:, 0:inner]
    put(xat, XAT, "xq", a["L1_xattn_Wq"])
    put(xat, XAT, "xk", wk)
    put(xat, XAT, "xks", wk.reshape(D, LH1, 2, HD // 2)[:, :, ::-1, :].reshape(D, -1))
    put(ffn, FFN, "up", a["L1_ffn_w_up"].T)
    put(ffn, FFN, "down", a["L1_ffn_w_down"].T.reshape(4, 128, D).transpose(1, 0, 2).reshape(128, -1))

    def pairs(w):
        return w.reshape(-1, 128, w.shape[1]).transpose(1, 0, 2).reshape(128, -1)
    inner0 = LH0 * HD
    kv = a["L0_xattn_Wkv"]
    fold = np.concatenate([pairs(a["L0_xattn_Wq"].T), pairs(kv[:, 0:inner0].T), pairs(kv[:, inner0:].T),
                           pairs(a["L0_xattn_Wout"]), pairs(a["L1_xattn_Wkv"][:, inner:].T),
                           pairs(a["L1_xattn_Wo"])], axis=1)
    return con, sel, spl, raw, xat, ffn, fold


def kernel(**inputs):
    import ml_dtypes
    import concourse.bacc as _bacc
    from concourse.bass_utils import run_bass_kernel_spmd as _run

    a = {k: np.asarray(v) for k, v in inputs.items()}
    con, sel, spl, raw, xat, ffn, fold = _layout(a)
    arrays = {
        "x": np.ascontiguousarray(a["x"]), "ctx": np.ascontiguousarray(a["ctx_1024"]),
        "mask": np.ascontiguousarray(a["mask_BxS2_bf1"]).view(np.uint8).reshape(1, B * S2),
        "con": con, "sel": sel.astype(ml_dtypes.bfloat16), **spl, "raw": raw, "xat": xat, "ffn": ffn,
        "fold": np.ascontiguousarray(fold),
    }
    nc = _bacc.Bacc("TRN2", target_bir_lowering=False, num_devices=1)
    args = [nc.dram_tensor(f"in_{k}", v.shape, mybir.dt.from_np(v.dtype), kind="ExternalInput").ap()
            for k, v in arrays.items()]
    args.append(nc.dram_tensor("out_0", (B, S, D), F32, kind="ExternalOutput").ap())
    decoder_kernel(nc, *args)
    r = _run(nc, [{f"in_{k}": v for k, v in arrays.items()}], core_ids=[0])
    return r.results[0]["out_0"]
```
